# Optimizing a Trainium2 kernel written in Bass

```python
import numpy as np
import jax
import jax.numpy as jnp

def _softmax(x, axis=-1):
    return jax.nn.softmax(x, axis=axis)

def _gelu(x):
    return jax.nn.gelu(x, approximate=True)

def _silu(x):
    return jax.nn.silu(x)

def _sigmoid(x):
    return jax.nn.sigmoid(x)

def _layernorm(x, axis=-1, eps=1e-05):
    m = jnp.mean(x, axis=axis, keepdims=True)
    v = jnp.var(x, axis=axis, keepdims=True)
    return (x - m) / jnp.sqrt(v + eps)

def _scatter_add(tgt, idx, src, axis=0):
    return tgt.at[idx].add(src)

def _segment_sum(src, seg, n):
    return jax.ops.segment_sum(src, seg, n)
kernel_name = 'mk_gnn_ffn_d4_gnn_r32_82485f'

def setup_inputs(seed: int=0):
    np.random.seed(seed)
    _w = jnp.asarray

    def _rec_inputs():
        import jax
        import jax.numpy as jnp
        _gk = jax.random.key(seed)
        x = -0.0002928 + 1 * jax.random.normal(jax.random.fold_in(_gk, 1), (256, 512), jnp.float32)
        src = jax.random.randint(jax.random.fold_in(_gk, 2), (4096,), 0, 256, jnp.int32)
        dst = jnp.minimum((256 * jax.random.uniform(jax.random.fold_in(_gk, 3), (4096,)) ** 2.0).astype(jnp.int32), 8191)
        _o = jnp.argsort(dst, stable=True)
        src = src[_o]
        dst = dst[_o]
        edge_weight = jax.random.uniform(jax.random.fold_in(_gk, 13), (4096,), jnp.float32, 0.0, 0.999999)
        return (x, src, dst, edge_weight)
    x, src, dst, edge_weight = _rec_inputs()

    def _L0_gnn_setup():
        import jax, jax.numpy as jnp
        import numpy as np
        N = 256
        D = 512
        E = 8192
        STEPS = 3
        key = jax.random.key(seed)
        k1, k2, k3 = jax.random.split(key, 3)
        x = jax.random.normal(k1, (N, D), dtype=jnp.float32)
        edge_index = jax.random.randint(k2, (2, E), 0, N, dtype=jnp.int32)
        W = jax.random.normal(k3, (D, D), dtype=jnp.float32) / np.sqrt(D)
        b = jnp.zeros((D,), dtype=jnp.float32)
        diffusion_weights = jnp.ones((STEPS + 1,), dtype=jnp.float32) / (STEPS + 1)
        return {'x': x, 'edge_index': edge_index, 'W': W, 'b': b, 'diffusion_weights': diffusion_weights}
    _L0_gnn_all = _L0_gnn_setup()
    _L0_gnn_in = {k: v for k, v in _L0_gnn_all.items() if k in ('W', 'b', 'diffusion_weights')}
    del _L0_gnn_all

    def _L0_ffn_setup():
        import jax, jax.numpy as jnp
        import numpy as np
        E = 8
        TOP_K = 2
        D = 512
        H = 1024
        B, S = (16, 128)
        key = jax.random.key(seed)
        ks = jax.random.split(key, 10)
        sd = lambda fan_in: 1.0 / np.sqrt(fan_in)
        x = jax.random.normal(ks[0], (B, S, D), dtype=jnp.float32)
        gw1 = jax.random.uniform(ks[1], (D, D // 2), jnp.float32, -sd(D), sd(D))
        gb1 = jnp.zeros((D // 2,), jnp.float32)
        gw2 = jax.random.uniform(ks[2], (D // 2, E), jnp.float32, -sd(D // 2), sd(D // 2))
        gb2 = jnp.zeros((E,), jnp.float32)
        we1 = jax.random.uniform(ks[3], (E, D, H), jnp.float32, -sd(D), sd(D))
        be1 = jnp.zeros((E, H), jnp.float32)
        we2 = jax.random.uniform(ks[4], (E, H, D), jnp.float32, -sd(H), sd(H))
        be2 = jnp.zeros((E, D), jnp.float32)
        return {'x': x, 'gw1': gw1, 'gb1': gb1, 'gw2': gw2, 'gb2': gb2, 'we1': we1, 'be1': be1, 'we2': we2, 'be2': be2}
    _L0_ffn_all = _L0_ffn_setup()
    _L0_ffn_in = {k: v for k, v in _L0_ffn_all.items() if k in ('gw1', 'gb1', 'gw2', 'gb2', 'we1', 'be1', 'we2', 'be2')}
    del _L0_ffn_all

    def _L1_gnn_setup():
        import jax, jax.numpy as jnp
        import numpy as np
        N_NODES = 3125
        N_EDGES = 25000
        D_IN = 512
        D_OUT = 512
        key = jax.random.key(seed)
        k1, k2, k3, k4, k5, k6 = jax.random.split(key, 6)
        x = jax.random.normal(k1, (N_NODES, D_IN), dtype=jnp.float32)
        src = jax.random.randint(k2, (N_EDGES,), 0, N_NODES)
        dst = jax.random.randint(k3, (N_EDGES,), 0, N_NODES)
        adj_vals = jax.random.uniform(k4, (N_EDGES,), dtype=jnp.float32)
        stdv = 1.0 / float(np.sqrt(D_OUT))
        weight = jax.random.uniform(k5, (D_IN, D_OUT), dtype=jnp.float32, minval=-stdv, maxval=stdv)
        bias = jax.random.uniform(k6, (D_OUT,), dtype=jnp.float32, minval=-stdv, maxval=stdv)
        return {'x': x, 'adj_vals': adj_vals, 'weight': weight, 'bias': bias, 'src': src, 'dst': dst}
    _L1_gnn_all = _L1_gnn_setup()
    _L1_gnn_in = {k: v for k, v in _L1_gnn_all.items() if k in ('weight', 'bias')}
    del _L1_gnn_all

    def _L1_ffn_setup():
        import jax, jax.numpy as jnp
        import numpy as np
        D_MODEL = 512
        D_FF = 64
        NUM_EXPERTS = 8
        TOP_K = 2
        key = jax.random.key(seed)
        k_x, k_r, k_w1, k_w2 = jax.random.split(key, 4)
        x = jax.random.normal(k_x, (4, 64, D_MODEL), dtype=jnp.float32)
        Wr = jax.random.normal(k_r, (NUM_EXPERTS, D_MODEL), dtype=jnp.float32) * (1.0 / np.sqrt(D_MODEL))
        W1 = jax.random.normal(k_w1, (NUM_EXPERTS, D_FF, D_MODEL), dtype=jnp.float32) * (1.0 / np.sqrt(D_MODEL))
        W2 = jax.random.normal(k_w2, (NUM_EXPERTS, D_MODEL, D_FF), dtype=jnp.float32) * (1.0 / np.sqrt(D_FF))
        return {'x': x, 'Wr': Wr, 'W1': W1, 'W2': W2}
    _L1_ffn_all = _L1_ffn_setup()
    _L1_ffn_in = {k: v for k, v in _L1_ffn_all.items() if k in ('Wr', 'W1', 'W2')}
    del _L1_ffn_all

    def _L2_gnn_setup():
        import jax, jax.numpy as jnp
        import numpy as np
        N = 512
        D = 512
        NNZ = 5120
        NUM_ITERS = 10
        key = jax.random.key(seed)
        k1, k2, k3, k4 = jax.random.split(key, 4)
        x = jax.random.normal(k1, (N, D), dtype=jnp.float32)
        edge_val = jax.random.uniform(k2, (NNZ,), dtype=jnp.float32)
        edge_row = jnp.sort(jax.random.randint(k3, (NNZ,), 0, N, dtype=jnp.int32))
        edge_col = jax.random.randint(k4, (NNZ,), 0, N, dtype=jnp.int32)
        alpha = jnp.zeros((1,), dtype=jnp.float32)
        beta = jnp.zeros((1,), dtype=jnp.float32)
        sigma = jnp.ones((1,), dtype=jnp.float32)
        return {'x': x, 'alpha': alpha, 'beta': beta, 'sigma': sigma, 'edge_val': edge_val, 'edge_row': edge_row, 'edge_col': edge_col, 'num_iters': NUM_ITERS}
    _L2_gnn_all = _L2_gnn_setup()
    _L2_gnn_in = {k: v for k, v in _L2_gnn_all.items() if k in ('alpha', 'beta', 'sigma')}
    del _L2_gnn_all

    def _L2_ffn_setup():
        import jax, jax.numpy as jnp
        import numpy as np
        B, S, D, E, O = (1024, 256, 512, 16, 512)
        key = jax.random.key(seed)
        k_x, k_wg, k_bg, k_we, k_be = jax.random.split(key, 5)
        scale_g = 1.0 / np.sqrt(D)
        scale_e = 1.0 / np.sqrt(D)
        return {'x': jax.random.normal(k_x, (B, S, D), dtype=jnp.float32), 'Wg': jax.random.uniform(k_wg, (D, E), jnp.float32, -scale_g, scale_g), 'bg': jax.random.uniform(k_bg, (E,), jnp.float32, -scale_g, scale_g), 'We': jax.random.uniform(k_we, (E, D, O), jnp.float32, -scale_e, scale_e), 'be': jax.random.uniform(k_be, (E, O), jnp.float32, -scale_e, scale_e)}
    _L2_ffn_all = _L2_ffn_setup()
    _L2_ffn_in = {k: v for k, v in _L2_ffn_all.items() if k in ('Wg', 'bg', 'We', 'be')}
    del _L2_ffn_all

    def _L3_gnn_setup():
        import jax, jax.numpy as jnp
        import numpy as np
        N_NODES = 50000
        IN_CH = 512
        OUT_CH = 512
        N_EDGES = 25000
        key = jax.random.key(seed)
        k_x, k_e, k_w, k_b = jax.random.split(key, 4)
        x = jax.random.normal(k_x, (N_NODES, IN_CH), dtype=jnp.float32)
        edge_index = jax.random.randint(k_e, (2, N_EDGES), 0, N_NODES, dtype=jnp.int32)
        bound = 1.0 / np.sqrt(2 * IN_CH)
        W = jax.random.uniform(k_w, (OUT_CH, 2 * IN_CH), minval=-bound, maxval=bound, dtype=jnp.float32)
        b = jax.random.uniform(k_b, (OUT_CH,), minval=-bound, maxval=bound, dtype=jnp.float32)
        return {'x': x, 'edge_index': edge_index, 'W': W, 'b': b}
    _L3_gnn_all = _L3_gnn_setup()
    _L3_gnn_in = {k: v for k, v in _L3_gnn_all.items() if k in ('W', 'b')}
    del _L3_gnn_all

    def _L3_ffn_setup():
        import jax, jax.numpy as jnp
        import numpy as np
        B, T, D, F, E, K = (8, 1024, 512, 64, 8, 2)

        def _moe_forward(x, Wr, br, W1, b1, W2, b2):
            Bx, Tx, Dx = x.shape
            xf = x.reshape(-1, Dx)
            logits = xf @ Wr + br
            probs = jax.nn.softmax(logits, axis=-1)
            vals, idx = jax.lax.top_k(probs, K)
            cw = (jax.nn.one_hot(idx, E, dtype=x.dtype) * vals[..., None]).sum(axis=1)

            def body(acc, params):
                W1e, b1e, W2e, b2e, cwe = params
                h = jax.nn.relu(xf @ W1e + b1e)
                y = h @ W2e + b2e
                return (acc + cwe[:, None] * y, None)
            out, _ = jax.lax.scan(body, jnp.zeros_like(xf), (W1, b1, W2, b2, cw.T))
            return out.reshape(Bx, Tx, Dx)
        key = jax.random.key(seed)
        k0, k1, k2, k3 = jax.random.split(key, 4)
        s_d = 1.0 / np.sqrt(D)
        s_f = 1.0 / np.sqrt(F)
        return {'x': jax.random.normal(k0, (B, T, D), jnp.float32), 'Wr': jax.random.uniform(k1, (D, E), jnp.float32, -s_d, s_d), 'br': jnp.zeros((E,), jnp.float32), 'W1': jax.random.uniform(k2, (E, D, F), jnp.float32, -s_d, s_d), 'b1': jnp.zeros((E, F), jnp.float32), 'W2': jax.random.uniform(k3, (E, F, D), jnp.float32, -s_f, s_f), 'b2': jnp.zeros((E, D), jnp.float32)}
    _L3_ffn_all = _L3_ffn_setup()
    _L3_ffn_in = {k: v for k, v in _L3_ffn_all.items() if k in ('Wr', 'br', 'W1', 'b1', 'W2', 'b2')}
    del _L3_ffn_all
    return {'x': x, 'src': src, 'dst': dst, 'edge_weight': edge_weight, 'L0_gnn_W': _L0_gnn_in['W'], 'L0_gnn_b': _L0_gnn_in['b'], 'L0_gnn_diffusion_weights': _L0_gnn_in['diffusion_weights'], 'L0_ffn_gw1': _L0_ffn_in['gw1'], 'L0_ffn_gb1': _L0_ffn_in['gb1'], 'L0_ffn_gw2': _L0_ffn_in['gw2'], 'L0_ffn_gb2': _L0_ffn_in['gb2'], 'L0_ffn_we1': _L0_ffn_in['we1'], 'L0_ffn_be1': _L0_ffn_in['be1'], 'L0_ffn_we2': _L0_ffn_in['we2'], 'L0_ffn_be2': _L0_ffn_in['be2'], 'L1_gnn_weight': _L1_gnn_in['weight'], 'L1_gnn_bias': _L1_gnn_in['bias'], 'L1_ffn_Wr': _L1_ffn_in['Wr'], 'L1_ffn_W1': _L1_ffn_in['W1'], 'L1_ffn_W2': _L1_ffn_in['W2'], 'L2_gnn_alpha': _L2_gnn_in['alpha'], 'L2_gnn_beta': _L2_gnn_in['beta'], 'L2_gnn_sigma': _L2_gnn_in['sigma'], 'L2_ffn_Wg': _L2_ffn_in['Wg'], 'L2_ffn_bg': _L2_ffn_in['bg'], 'L2_ffn_We': _L2_ffn_in['We'], 'L2_ffn_be': _L2_ffn_in['be'], 'L3_gnn_W': _L3_gnn_in['W'], 'L3_gnn_b': _L3_gnn_in['b'], 'L3_ffn_Wr': _L3_ffn_in['Wr'], 'L3_ffn_br': _L3_ffn_in['br'], 'L3_ffn_W1': _L3_ffn_in['W1'], 'L3_ffn_b1': _L3_ffn_in['b1'], 'L3_ffn_W2': _L3_ffn_in['W2'], 'L3_ffn_b2': _L3_ffn_in['b2']}

def reference(x, src, dst, edge_weight, L0_gnn_W, L0_gnn_b, L0_gnn_diffusion_weights, L0_ffn_gw1, L0_ffn_gb1, L0_ffn_gw2, L0_ffn_gb2, L0_ffn_we1, L0_ffn_be1, L0_ffn_we2, L0_ffn_be2, L1_gnn_weight, L1_gnn_bias, L1_ffn_Wr, L1_ffn_W1, L1_ffn_W2, L2_gnn_alpha, L2_gnn_beta, L2_gnn_sigma, L2_ffn_Wg, L2_ffn_bg, L2_ffn_We, L2_ffn_be, L3_gnn_W, L3_gnn_b, L3_ffn_Wr, L3_ffn_br, L3_ffn_W1, L3_ffn_b1, L3_ffn_W2, L3_ffn_b2):
    import jax
    import jax.numpy as jnp

    def _L0_gnn_ref(x, edge_index, W, b, diffusion_weights):
        import jax, jax.numpy as jnp
        import numpy as np
        N = 256
        D = 512
        E = 8192
        STEPS = 3
        h = x @ W + b
        row, col = (edge_index[0], edge_index[1])
        adj = jnp.zeros((N, N), dtype=h.dtype)
        adj = adj.at[row, col].set(1.0)
        adj = adj.at[col, row].set(1.0)
        adj = adj + jnp.eye(N, dtype=h.dtype)
        row_sum = adj.sum(axis=1, keepdims=True)
        adj = adj / jnp.maximum(row_sum, 1.0)
        out = diffusion_weights[0] * h
        cur = h
        for i in range(STEPS):
            cur = adj @ cur
            out = out + diffusion_weights[i + 1] * cur
        return jax.nn.relu(out)

    def _L0_ffn_ref(x, gw1, gb1, gw2, gb2, we1, be1, we2, be2):
        import jax, jax.numpy as jnp
        import numpy as np
        E = 8
        TOP_K = 2
        D = 512
        H = 1024
        B, S = (16, 128)
        b, s, d = x.shape
        xf = x.reshape(-1, d)
        T = xf.shape[0]
        gate_logits = jax.nn.relu(xf @ gw1 + gb1) @ gw2 + gb2
        gate_weights = jax.nn.softmax(gate_logits, axis=-1)
        top_w, top_idx = jax.lax.top_k(gate_weights, TOP_K)
        top_w = jax.nn.softmax(top_w, axis=-1)
        combine = jnp.zeros((T, E), dtype=xf.dtype)
        combine = combine.at[jnp.arange(T)[:, None], top_idx].add(top_w)
        out = jnp.zeros_like(xf)
        for e in range(E):
            h = jax.nn.gelu(xf @ we1[e] + be1[e], approximate=False)
            y = h @ we2[e] + be2[e]
            out = out + combine[:, e:e + 1] * y
        return out.reshape(b, s, d)

    def _L1_gnn_ref(x, adj_vals, weight, bias, src, dst):
        import jax, jax.numpy as jnp
        import numpy as np
        N_NODES = 3125
        N_EDGES = 25000
        D_IN = 512
        D_OUT = 512
        support = jax.ops.segment_sum(adj_vals[:, None] * x[src], dst, num_segments=x.shape[0])
        return support @ weight + bias

    def _L1_ffn_ref(x, Wr, W1, W2):
        import jax, jax.numpy as jnp
        import numpy as np
        D_MODEL = 512
        D_FF = 64
        NUM_EXPERTS = 8
        TOP_K = 2
        B, L, D = x.shape
        T = B * L
        x_flat = x.reshape(T, D)
        logits = x_flat @ Wr.T
        sm = jax.nn.softmax(logits, axis=-1)
        top_v, top_i = jax.lax.top_k(sm, TOP_K)
        probs = jnp.zeros_like(sm).at[jnp.arange(T)[:, None], top_i].set(top_v)
        h = jnp.einsum('td,efd->tef', x_flat, W1)
        h = jax.nn.gelu(h, approximate=False)
        expert_out = jnp.einsum('tef,edf->ted', h, W2)
        out = jnp.einsum('te,ted->td', probs, expert_out)
        return out.reshape(B, L, D)

    def _L2_gnn_ref(x, alpha, beta, sigma, edge_val, edge_row, edge_col, num_iters):
        import jax, jax.numpy as jnp
        import numpy as np
        N = 512
        D = 512
        NNZ = 5120
        NUM_ITERS = 10
        n = x.shape[0]
        xn = x * jax.lax.rsqrt(jnp.maximum(jnp.sum(x * x, axis=1, keepdims=True), 1e-12))
        sim_e = jnp.sum(xn[edge_row] * xn[edge_col], axis=-1)
        sim_e = jnp.where(edge_row == edge_col, 0.0, sim_e)
        s = jnp.exp(sigma[0])
        sigma_sq = 2.0 * s * s
        sim_e = jnp.exp(sim_e / (2.0 * sigma_sq))
        sup = edge_val * sim_e
        normalize = jax.ops.segment_sum(sup, edge_row, num_segments=n)
        a = jnp.exp(alpha[0])
        b = jnp.exp(beta[0])
        denom = b + normalize[:, None] * a + a

        def step(out, _):
            Ax = jax.ops.segment_sum(sup[:, None] * out[edge_col], edge_row, num_segments=n)
            out = (x * b + (Ax + out) * a) / denom
            return (out, None)
        out, _ = jax.lax.scan(step, x, None, length=num_iters)
        return out

    def _L2_ffn_ref(x, Wg, bg, We, be):
        import jax, jax.numpy as jnp
        import numpy as np
        B, S, D, E, O = (1024, 256, 512, 16, 512)
        scores = jax.nn.softmax(jnp.mean(x, axis=1) @ Wg + bg, axis=-1)
        idx = jnp.argmax(scores, axis=-1)
        gate = jnp.take_along_axis(scores, idx[:, None], axis=-1)
        W_sel = We[idx]
        b_sel = be[idx]
        y = jnp.einsum('bsd,bdo->bso', x, W_sel) + b_sel[:, None, :]
        return gate[:, :, None] * y

    def _L3_gnn_ref(x, edge_index, W, b):
        import jax, jax.numpy as jnp
        import numpy as np
        N_NODES = 50000
        IN_CH = 512
        OUT_CH = 512
        N_EDGES = 25000
        src, dst = (edge_index[0], edge_index[1])
        src_feats = x[src]
        neighbor_sum = jax.ops.segment_sum(src_feats, dst, num_segments=x.shape[0])
        neighbor_count = jax.ops.segment_sum(jnp.ones((src.shape[0],), dtype=x.dtype), dst, num_segments=x.shape[0])
        neighbor_count = jnp.maximum(neighbor_count, 1.0)
        neighbor_mean = neighbor_sum / neighbor_count[:, None]
        h = jnp.concatenate([x, neighbor_mean], axis=-1)
        return h @ W.T + b

    def _L3_ffn_ref(x, Wr, br, W1, b1, W2, b2):
        import jax, jax.numpy as jnp
        import numpy as np
        B, T, D, F, E, K = (8, 1024, 512, 64, 8, 2)

        def _moe_forward(x, Wr, br, W1, b1, W2, b2):
            Bx, Tx, Dx = x.shape
            xf = x.reshape(-1, Dx)
            logits = xf @ Wr + br
            probs = jax.nn.softmax(logits, axis=-1)
            vals, idx = jax.lax.top_k(probs, K)
            cw = (jax.nn.one_hot(idx, E, dtype=x.dtype) * vals[..., None]).sum(axis=1)

            def body(acc, params):
                W1e, b1e, W2e, b2e, cwe = params
                h = jax.nn.relu(xf @ W1e + b1e)
                y = h @ W2e + b2e
                return (acc + cwe[:, None] * y, None)
            out, _ = jax.lax.scan(body, jnp.zeros_like(xf), (W1, b1, W2, b2, cw.T))
            return out.reshape(Bx, Tx, Dx)
        return _moe_forward(x, Wr, br, W1, b1, W2, b2)
    edge_index = jnp.stack([src, dst])
    x = x + _L0_gnn_ref(_layernorm(x, axis=-1), edge_index, L0_gnn_W, L0_gnn_b, L0_gnn_diffusion_weights)
    x = x + _L0_ffn_ref(_layernorm(x, axis=-1)[None], L0_ffn_gw1, L0_ffn_gb1, L0_ffn_gw2, L0_ffn_gb2, L0_ffn_we1, L0_ffn_be1, L0_ffn_we2, L0_ffn_be2)[0]
    x = x + _L1_gnn_ref(_layernorm(x, axis=-1), edge_weight, L1_gnn_weight, L1_gnn_bias, src, dst)
    x = x + _L1_ffn_ref(_layernorm(x, axis=-1)[None], L1_ffn_Wr, L1_ffn_W1, L1_ffn_W2)[0]
    x = x + _L2_gnn_ref(_layernorm(x, axis=-1), L2_gnn_alpha, L2_gnn_beta, L2_gnn_sigma, edge_weight, src, dst, 10)
    x = x + _L2_ffn_ref(_layernorm(x, axis=-1)[None], L2_ffn_Wg, L2_ffn_bg, L2_ffn_We, L2_ffn_be)[0]
    x = x + _L3_gnn_ref(_layernorm(x, axis=-1), edge_index, L3_gnn_W, L3_gnn_b)
    x = x + _L3_ffn_ref(_layernorm(x, axis=-1)[None], L3_ffn_Wr, L3_ffn_br, L3_ffn_W1, L3_ffn_b1, L3_ffn_W2, L3_ffn_b2)[0]
    return x

_drawn_inputs = setup_inputs


def setup_inputs(seed=0):
    import zlib

    import numpy as np

    out = dict(_drawn_inputs(seed))
    spreads = {'L0_gnn_b': (0.0, 0.1),
     'L0_gnn_diffusion_weights': (0.25, 0.6),
     'L0_ffn_gb1': (0.0, 0.1),
     'L0_ffn_gb2': (0.0, 0.1),
     'L0_ffn_be1': (0.0, 0.1),
     'L0_ffn_be2': (0.0, 0.1),
     'L3_ffn_br': (0.0, 0.628),
     'L3_ffn_b1': (0.0, 0.8),
     'L3_ffn_b2': (0.0, 0.543)}
    factors = {'L2_ffn_bg': 8.0, 'L2_ffn_be': 41.642, 'L3_gnn_b': 6.789}
    for name, (base, spread) in spreads.items():
        noise = np.random.default_rng([zlib.crc32(name.encode()), seed]).standard_normal(out[name].shape)
        drawn = base * np.exp(spread * noise) if base else spread * noise
        out[name] = jnp.asarray(drawn.astype(out[name].dtype))
    for name, factor in factors.items():
        out[name] = (out[name] * factor).astype(out[name].dtype)
    return out
```

```python
from contextlib import ExitStack

import concourse.bass as bass
from concourse import mybir

ALU = mybir.AluOpType
ACT = mybir.ActivationFunctionType
F32 = mybir.dt.float32
F32R = mybir.dt.float32r
BF16 = mybir.dt.bfloat16
I32 = mybir.dt.int32
U32 = mybir.dt.uint32
AX_X = mybir.AxisListType.X

P = 128
N = 256
NT = N // P
D = 512
DC = D // P
EDGES = 4096
EC = EDGES // P
EU = 4
EXPERTS = 8
H0 = 1024
HC = H0 // P
LN_EPS = 1e-5
NORM_FLOOR = 1e-12
DIFFUSION_STEPS = 3
SMOOTH_STEPS = 10
GATES2 = 16


def build(nc, x, src, dst, edge_weight, L0_gnn_W, L0_gnn_b, L0_gnn_diffusion_weights, L0_ffn_gw1, L0_ffn_gb1,
          L0_ffn_gw2, L0_ffn_gb2, L0_ffn_we1, L0_ffn_be1, L0_ffn_we2, L0_ffn_be2, L1_gnn_weight, L1_gnn_bias,
          L1_ffn_Wr, L1_ffn_W1, L1_ffn_W2, L2_gnn_alpha, L2_gnn_beta, L2_gnn_sigma, L2_ffn_Wg, L2_ffn_bg,
          L2_ffn_We, L2_ffn_be, L3_gnn_W, L3_gnn_b, L3_ffn_Wr, L3_ffn_br, L3_ffn_W1, L3_ffn_b1, L3_ffn_W2,
          L3_ffn_b2, out):
    with ExitStack() as ctx:
        def sb(name, shape, dt=F32):
            return ctx.enter_context(nc.sbuf_tensor(name, shape, dt))

        sems = {}

        def sig(name):
            if name not in sems:
                sems[name] = ctx.enter_context(nc.semaphore(name))
            return sems[name]

        every = ("G0", "F0", "G1", "F1", "G2", "F2", "G3", "F3")
        turned = tuple(s for s in every if s != "G1")
        GIVEN = {
            "var": dict.fromkeys(every, NT), "rstd": dict.fromkeys(every, 1), "xn": dict.fromkeys(every, NT),
            "xT": dict.fromkeys(turned, 2), "xnT0": dict.fromkeys(turned, 1), "xnT1": dict.fromkeys(turned, 1),
            "logits": dict.fromkeys(("F0", "F1", "F2", "F3"), 1), "neg_m": dict.fromkeys(("F0", "F1", "F2", "F3"), 1),
            "exp": {"F0": NT, "F1": NT, "F2": 1, "F3": NT}, "cw": dict.fromkeys(("F0", "F1", "F3"), 1),
            "cwT_ps": dict.fromkeys(("F0", "F1", "F3"), 1), "cwT": dict.fromkeys(("F0", "F1", "F3"), 1),
            "out": dict.fromkeys(("F0", "G1", "F1", "F2", "G3", "F3"), NT),
            "hidden": {"F1": 2, "F3": 2}, "act": {"F1": DC, "F3": DC}, "hid": {"F1": DC, "F3": DC},
            "spread": {"F1": 2, "F3": 2}, "supT_ps": {"G1": 2, "G3": 2}, "supT0": {"G1": 1, "G3": 1},
            "supT1": {"G1": 1, "G3": 1},
        }

        def at(stage, name, n):
            given = GIVEN[name]
            return sig(name), n + sum(k for s, k in given.items() if every.index(s) < every.index(stage))

        X = sb("X", [P, NT, D])
        xn = sb("xn", [P, NT, D])
        xnT = sb("xnT", [P, DC, N])
        wide = sb("wide", [P, HC, N])
        cur = sb("cur", [P, NT, D])
        acc = sb("acc", [P, NT, D])
        supT = sb("supT", [P, DC, N])
        bn = sb("bn", [P, NT, 6])
        mv = sb("mv", [P, NT, 2])
        rstd = sb("rstd", [P, NT])
        neg_half = sb("neg_half", [P, NT])

        ident = sb("ident", [P, P])
        ones = sb("ones", [P, P])
        iota = sb("iota", [P, N], BF16)
        iota8 = sb("iota8", [P, EXPERTS])
        spread = sb("spread", [EXPERTS, D])

        edge_i = sb("edge_i", [P, 2, EC], I32)
        edge_f = sb("edge_f", [P, 2, EC])
        ew = sb("ew", [P, EC])
        ew_hi = sb("ew_hi", [P, EC], F32R)
        ew_lo = sb("ew_lo", [P, EC])
        hot_s = sb("hot_s", [P, EU, N], BF16)
        hot_d = sb("hot_d", [P, EU, N], BF16)
        hot_sr = sb("hot_sr", [P, EU, N], F32R)
        hot_dw = sb("hot_dw", [P, EU, 2 * N], F32R)
        cnt = sb("cnt", [P, NT, N])
        adj = sb("adj", [P, NT, N])
        adj_sum = sb("adj_sum", [P, NT])
        adj_inv = sb("adj_inv", [P, NT])
        wgt = sb("wgt", [P, NT, N])
        wgtT = sb("wgtT", [P, NT, N])
        mean_w = sb("mean_w", [P, NT, N])
        deg_inv = sb("deg_inv", [P, N])

        diff_w = sb("diff_w", [P, DIFFUSION_STEPS + 1])
        bias_rows = sb("bias_rows", [70, P])
        bias_cols = sb("bias_cols", [P, 70])
        gb2_b = sb("gb2_b", [P, EXPERTS])
        br_b = sb("br_b", [P, EXPERTS])
        bg_b = sb("bg_b", [P, GATES2])
        be2_sb = sb("be2_sb", [EXPERTS, D])
        b2_sb = sb("b2_sb", [EXPERTS, D])
        b0_b = sb("b0_b", [P, D])
        b1_b = sb("b1_b", [P, D])
        b3_b = sb("b3_b", [P, D])
        be_sel = sb("be_sel", [P, D])
        wr_rows = sb("wr_rows", [EXPERTS, D])
        wr1T = sb("wr1T", [P, DC, EXPERTS])
        wr3 = sb("wr3", [P, DC, EXPERTS])
        gw2 = sb("gw2", [P, NT, EXPERTS])
        wg2 = sb("wg2", [P, DC, GATES2])
        abs_b = sb("abs_b", [P, 3])

        lg = sb("lg", [P, NT, GATES2])
        mx = sb("mx", [P, NT, 8])
        neg_m = sb("neg_m", [P, NT])
        ex = sb("ex", [P, NT, GATES2])
        sm = sb("sm", [P, NT])
        rs = sb("rs", [P, NT])
        sw = sb("sw", [P, NT, EXPERTS])
        m2 = sb("m2", [P, NT, 8])
        ix = sb("ix", [P, NT, 8], U32)
        ixf = sb("ixf", [P, NT, 2])
        pw = sb("pw", [P, NT, 2])
        gap = sb("gap", [P, NT])
        cwa = sb("cwa", [P, NT, EXPERTS])
        cwb = sb("cwb", [P, NT, EXPERTS])
        cw = sb("cw", [P, NT, EXPERTS])
        cwT = sb("cwT", [EXPERTS, N])

        off_diag = sb("off_diag", [P, P])
        sim = sb("sim", [P, NT, N])
        sup = sb("sup", [P, NT, N])
        loopT = sb("loopT", [P, NT, N])
        loop = sb("loop", [P, NT, N])
        loopTs = sb("loopTs", [P, NT, N])
        twoT = sb("twoT", [P, NT, N])
        sc = sb("sc", [P, 16])
        norm = sb("norm", [P, NT])
        r2 = sb("r2", [P, NT])
        rb = sb("rb", [P, NT])
        meanT = sb("meanT", [P, DC])
        pick = sb("pick", [P, 8], U32)

        w0 = sb("w0", [P, DC, D])
        gw1 = sb("gw1", [P, DC, N])
        w1g = sb("w1g", [P, DC, D])
        w1T = sb("w1T", [P, DC, D])
        w2T = sb("w2T", [P, DC, D])
        ring = sb("ring", [P, 2, 2, 4096])

        we1_ring = [ring[:, u, 0, :].rearrange("p (c n) -> p c n", c=DC) for u in range(2)]
        we2_ring = [ring[:, u, 1, :].rearrange("p (k n) -> p k n", k=HC) for u in range(2)]

        w1_raw = sb("w1_raw", [P, DC, D])
        w2_raw = w0
        w3_raw = ring[:, 0, 0, :].rearrange("p (c n) -> p c n", c=DC)
        w3T = ring[:, 0, 1, :].rearrange("p (k n) -> p k n", k=8)
        we_sel = ring[:, 1, 0, 0:2048].rearrange("p (c n) -> p c n", c=DC)
        w31 = ring[:, 1, 0, 2048:4096].rearrange("p (c n) -> p c n", c=DC)
        w32 = ring[:, 1, 1, 0:2048].rearrange("p (c n) -> p c n", c=DC)

        PS = ctx.enter_context(nc.psum_tensor("PS", [P, 8, 512], F32))
        TR, OUT, SMALL, HID = 0, 2, 4, 4

        block = ctx.enter_context(nc.Block())

        @block.sync
        def _(sp):
            def load(to, of, name):
                sp.dma_start(to, of).then_inc(sig(name), 16)

            load(X[:], x.rearrange("(t p) d -> p t d", p=P), "ld_x")
            load(edge_i[:, 0, :], src.rearrange("(p j) -> p j", p=P), "ld_edges")
            load(edge_i[:, 1, :], dst.rearrange("(p j) -> p j", p=P), "ld_edges")
            load(w0[:], L0_gnn_W.rearrange("(c p) n -> p c n", p=P), "ld_w0")
            load(b0_b[:], L0_gnn_b.partition_broadcast(P), "ld_b0")
            load(diff_w[:], L0_gnn_diffusion_weights.partition_broadcast(P), "ld_b0")
            load(gw1[:], L0_ffn_gw1.rearrange("(c p) n -> p c n", p=P), "ld_gate0")
            load(gw2[:], L0_ffn_gw2.rearrange("(c p) n -> p c n", p=P), "ld_gate0")
            load(gb2_b[:], L0_ffn_gb2.partition_broadcast(P), "ld_gate0")
            load(bias_rows[0:64, :], L0_ffn_be1.rearrange("e (k p) -> (e k) p", p=P), "ld_bias_rows")
            load(bias_rows[64:66, :], L0_ffn_gb1.rearrange("(k p) -> k p", p=P), "ld_bias_rows")
            load(bias_rows[66:70, :], L3_ffn_b1.rearrange("(a e) f -> a (e f)", a=4), "ld_bias_rows")
            load(be2_sb[:], L0_ffn_be2, "ld_be2")
            load(ew[:], edge_weight.rearrange("(p j) -> p j", p=P), "ld_ew")

            def load_expert(e, u):
                load(we1_ring[u], L0_ffn_we1[bass.ds(e, 1)].rearrange("a (c p) n -> p (a c) n", p=P), f"ld_we1_slot{u}")
                load(we2_ring[u], L0_ffn_we2[bass.ds(e, 1)].rearrange("a (k p) n -> p (a k) n", p=P), f"ld_we2_slot{u}")

            for u in range(2):
                load_expert(u, u)
            load(w1g[:], L1_gnn_weight.rearrange("(c p) n -> p c n", p=P), "ld_w1g")
            load(b1_b[:], L1_gnn_bias.partition_broadcast(P), "ld_w1g")
            load(wr_rows[:], L1_ffn_Wr, "ld_wr1")
            load(w1_raw[:], L1_ffn_W1.rearrange("e f d -> (e f) d").rearrange("(c p) d -> p c d", p=P), "ld_w1_raw")
            sp.wait_ge(sig("G0_h"), NT)
            for c in range(DC):
                load(w2_raw[:, c, :].rearrange("p (e f) -> p e f", e=EXPERTS),
                     L1_ffn_W2[:, c * P:(c + 1) * P, :].rearrange("e p f -> p e f"), "ld_w2_raw")
            load(wg2[:], L2_ffn_Wg.rearrange("(c p) n -> p c n", p=P), "ld_l2")
            load(bg_b[:], L2_ffn_bg.partition_broadcast(P), "ld_l2")
            load(abs_b[:, 0:1], L2_gnn_alpha.partition_broadcast(P), "ld_abs")
            load(abs_b[:, 1:2], L2_gnn_beta.partition_broadcast(P), "ld_abs")
            load(abs_b[:, 2:3], L2_gnn_sigma.partition_broadcast(P), "ld_abs")
            load(b3_b[:], L3_gnn_b.partition_broadcast(P), "ld_b3")
            load(wr3[:], L3_ffn_Wr.rearrange("(c p) n -> p c n", p=P), "ld_gate3")
            load(br_b[:], L3_ffn_br.partition_broadcast(P), "ld_gate3")
            load(b2_sb[:], L3_ffn_b2, "ld_gate3")
            with sp.Fori(1, EXPERTS // 2) as g:
                for u in range(2):
                    sp.wait_ge(sig("F0_hidden"), g * 2 * DC + (u - 1) * DC)
                    load(we1_ring[u], L0_ffn_we1.rearrange("(g u) (c p) n -> g u p c n", u=2, p=P)
                         [bass.ds(g, 1), u].rearrange("g p c n -> p (g c) n"), f"ld_we1_slot{u}")
                    sp.wait_ge(sig("F0_y"), g * 2 + (u - 1))
                    load(we2_ring[u], L0_ffn_we2.rearrange("(g u) (k p) n -> g u p k n", u=2, p=P)
                         [bass.ds(g, 1), u].rearrange("g p k n -> p (g k) n"), f"ld_we2_slot{u}")
            sp.wait_ge(sig("F0_y"), EXPERTS - 1)
            load(w3_raw, L3_gnn_W.rearrange("(c p) n -> p c n", p=P), "ld_w3_raw")
            sp.wait_ge(sig("F0_y"), EXPERTS)
            for c in range(DC):
                load(w31[:, c, :].rearrange("p (e f) -> p e f", e=EXPERTS),
                     L3_ffn_W1[:, c * P:(c + 1) * P, :].rearrange("e p f -> p e f"), "ld_w31")
            load(w32, L3_ffn_W2.rearrange("e f d -> (e f) d").rearrange("(c p) d -> p c d", p=P), "ld_w32")
            sp.wait_ge(sig("F2_pick"), 1)
            e = sp.value_load(pick[0:1, 0:1], min_val=0, max_val=GATES2 - 1)
            load(we_sel, L2_ffn_We[bass.ds(e, 1)].rearrange("a (c p) n -> p (a c) n", p=P), "ld_we_sel")
            load(be_sel[:], L2_ffn_be[bass.ds(e, 1)].rearrange("a n -> (a n)").partition_broadcast(P), "ld_we_sel")
            for t in range(NT):
                sp.wait_ge(sig("X_final"), t + 1)
                sp.dma_start(out[t * P:(t + 1) * P, :], X[:, t, :]).then_inc(sig("stored"), 16)
            sp.wait_ge(sig("stored"), 16 * NT)

        @block.gpsimd
        def _(pool):
            g = nc.gpsimd
            g.memset(ident[:], 0.0).then_inc(sig("pool_fill"), 1)
            g.memset(ones[:], 1.0).then_inc(sig("pool_fill"), 1)
            g.memset(neg_half[:], -0.5).then_inc(sig("pool_fill"), 1)
            g.iota(iota[:], [[1, N]], base=0, channel_multiplier=0,
                   allow_small_or_imprecise_dtypes=True).then_inc(sig("const_iota"), 1)
            g.iota(iota8[:], [[1, EXPERTS]], base=0, channel_multiplier=0,
                   allow_small_or_imprecise_dtypes=True).then_inc(sig("const_iota"), 1)
            pool.wait_ge(sig("pool_fill"), 3)
            g.affine_select(out=ident[:], in_=ident[:], compare_op=ALU.not_equal, fill=1.0, base=0,
                            pattern=[[-1, P]], channel_multiplier=1).then_inc(sig("const_ident"), 1)
            g.affine_select(out=off_diag[:], in_=ones[:], compare_op=ALU.not_equal, fill=0.0, base=0,
                            pattern=[[-1, P]], channel_multiplier=1).then_inc(sig("const_mask"), 1)
            g.memset(spread[:], 1.0).then_inc(sig("const_spread"), 1)
            pool.wait_ge(sig("const_spread"), 1)
            g.affine_select(out=spread[:], in_=spread[:], compare_op=ALU.is_ge, fill=0.0, base=0,
                            pattern=[[1, D]], channel_multiplier=-64).then_inc(sig("const_spread"), 1)
            pool.wait_ge(sig("const_spread"), 2)
            g.affine_select(out=spread[:], in_=spread[:], compare_op=ALU.is_ge, fill=0.0, base=63,
                            pattern=[[-1, D]], channel_multiplier=64).then_inc(sig("const_spread"), 1)

            def inverse_std(s):
                pool.wait_ge(*at(s, "var", NT))
                g.tensor_scalar(rstd[:], mv[:, :, 1], LN_EPS, None, ALU.add).then_inc(sig("pool_own"), 1)
                pool.wait_ge(sig("pool_own"), every.index(s) + 1)
                g.tensor_tensor(rstd[:], rstd[:], neg_half[:], ALU.pow).then_inc(sig("rstd"), 1)

            for s in ("G0", "F0", "G1", "F1", "G2"):
                inverse_std(s)
            pool.wait_ge(sig("G2_sumsq"), 1)
            g.tensor_scalar(rs[:], sm[:], NORM_FLOOR, None, ALU.max).then_inc(sig("G2_floored"), 1)
            pool.wait_ge(sig("G2_floored"), 1)
            g.tensor_tensor(rs[:], rs[:], neg_half[:], ALU.pow).then_inc(sig("G2_rnorm"), 1)
            for s in ("F2", "G3", "F3"):
                inverse_std(s)

        @block.vector
        def _(dve):
            v = nc.vector
            own = [0]

            def done(ins):
                own[0] += 1
                ins.then_inc(sig("dve_own"), 1)
                dve.wait_ge(sig("dve_own"), own[0])

            def layer_norm(s):
                for t in range(NT):
                    done(v.bn_stats(bn[:, t, :], X[:, t, :]))
                for t in range(NT):
                    v.bn_aggr(mv[:, t, :], bn[:, t, :]).then_inc(sig("var"), 1)
                dve.wait_ge(*at(s, "rstd", 1))
                for t in range(NT):
                    v.tensor_scalar(xn[:, t, :], X[:, t, :], mv[:, t, 0:1], rstd[:, t:t + 1],
                                    ALU.subtract, ALU.mult).then_inc(sig("xn"), 1)

            def take_transposed(s):
                dve.wait_ge(*at(s, "xT", 1))
                v.tensor_copy(xnT[:, 0:2, :], PS[:, TR, :]).then_inc(sig("xnT0"), 1)

            def top2(s, bias, softmax_of_two):
                dve.wait_ge(*at(s, "logits", 1))
                for t in range(NT):
                    of = PS[:, SMALL, t * EXPERTS:(t + 1) * EXPERTS]
                    if bias is None:
                        ins = v.tensor_copy(lg[:, t, 0:EXPERTS], of)
                    else:
                        ins = v.tensor_tensor(lg[:, t, 0:EXPERTS], of, bias[:], ALU.add)
                done(ins)
                for t in range(NT):
                    ins = v.max(mx[:, t, :], lg[:, t, 0:EXPERTS])
                done(ins)
                v.tensor_scalar(neg_m[:], mx[:, :, 0], -1.0, None, ALU.mult).then_inc(sig("neg_m"), 1)
                dve.wait_ge(*at(s, "exp", NT))
                done(v.reciprocal(rs[:], sm[:]))
                for t in range(NT):
                    ins = v.tensor_scalar(sw[:, t, :], ex[:, t, 0:EXPERTS], rs[:, t:t + 1], None, ALU.mult)
                done(ins)
                for t in range(NT):
                    ins = v.max(m2[:, t, :], sw[:, t, :])
                done(ins)
                for t in range(NT):
                    ins = v.max_index(ix[:, t, :], m2[:, t, :], sw[:, t, :])
                done(ins)
                if softmax_of_two:
                    v.tensor_tensor(gap[:], m2[:, :, 1], m2[:, :, 0], ALU.subtract).then_inc(sig(s + "_gap"), 1)
                done(v.tensor_copy(ixf[:], ix[:, :, 0:2]))
                if softmax_of_two:
                    dve.wait_ge(sig(s + "_gap_exp"), 1)
                    done(v.tensor_scalar(pw[:, :, 0], gap[:], 1.0, None, ALU.add))
                    done(v.reciprocal(pw[:, :, 0], pw[:, :, 0]))
                    done(v.tensor_tensor(pw[:, :, 1], pw[:, :, 0], gap[:], ALU.mult))
                    weight = pw
                else:
                    weight = m2
                for t in range(NT):
                    v.tensor_scalar(cwa[:, t, :], iota8[:], ixf[:, t, 0:1], weight[:, t, 0:1],
                                    ALU.is_equal, ALU.mult)
                    ins = v.tensor_scalar(cwb[:, t, :], iota8[:], ixf[:, t, 1:2], weight[:, t, 1:2],
                                          ALU.is_equal, ALU.mult)
                done(ins)
                v.tensor_tensor(cw[:], cwa[:], cwb[:], ALU.add).then_inc(sig("cw"), 1)
                dve.wait_ge(*at(s, "cwT_ps", 1))
                v.tensor_copy(cwT[:], PS[0:EXPERTS, SMALL, 0:N]).then_inc(sig("cwT"), 1)

            def add_to_state(s, gate=None):
                for t in range(NT):
                    dve.wait_ge(*at(s, "out", t + 1))
                    done(v.tensor_tensor(X[:, t, :], PS[:, OUT + t, :], X[:, t, :], ALU.add))

            dve.wait_ge(sig("ld_x"), 16)
            layer_norm("G0")
            dve.wait_ge(sig("ld_edges"), 32)
            dve.wait_ge(sig("const_iota"), 2)
            done(v.tensor_copy(edge_f[:], edge_i[:]))
            ends = edge_f[:].rearrange("p s (g u) -> p s g u", u=EU)

            def one_hots(g, u):
                v.tensor_scalar(hot_s[:, u, :], iota[:], ends[:, 0, bass.ds(g, 1), u], None, ALU.is_equal)
                v.tensor_scalar(hot_d[:, u, :], iota[:], ends[:, 1, bass.ds(g, 1), u], None,
                                ALU.is_equal).then_inc(sig("hot"), 1)

            for u in range(EU):
                one_hots(0, u)
            with dve.Fori(1, EC // EU) as i:
                for u in range(EU):
                    dve.wait_ge(sig("hot_used"), i * EU + (u - EU + 1))
                    one_hots(i, u)
            take_transposed("G0")
            dve.wait_ge(sig("ld_b0"), 32)
            for t in range(NT):
                dve.wait_ge(sig("G0_h"), t + 1)
                ins = v.tensor_tensor(cur[:, t, :], PS[:, OUT + t, :], b0_b[:], ALU.add)
                ins.then_inc(sig("G0_cur"), 1)
            dve.wait_ge(sig("hot_used"), EC)
            for t in range(NT):
                v.tensor_copy(cnt[:, t, :], PS[:, 5 + t, 0:N]).then_inc(sig("cnt"), 1)
            dve.wait_ge(sig("cntT"), 1)
            for t in range(NT):
                ins = v.tensor_tensor(adj[:, t, :], cnt[:, t, :], PS[:, 5 + t, 0:N], ALU.add)
            done(ins)
            for t in range(NT):
                ins = v.tensor_scalar(adj[:, t, :], adj[:, t, :], 1.0, 0.0, ALU.min, ALU.add,
                                      accum_out=adj_sum[:, t:t + 1])
            done(ins)
            for t in range(NT):
                v.tensor_tensor(adj[:, t, t * P:(t + 1) * P], adj[:, t, t * P:(t + 1) * P], ident[:],
                                ALU.add).then_inc(sig("adj"), 1)
            done(v.tensor_scalar(adj_inv[:], adj_sum[:], 1.0, 1.0, ALU.add, ALU.max))
            done(v.reciprocal(adj_inv[:], adj_inv[:]))
            for t in range(NT):
                ins = v.tensor_scalar(acc[:, t, :], cur[:, t, :], diff_w[:, 0:1], None, ALU.mult)
            done(ins)
            for k in range(1, DIFFUSION_STEPS + 1):
                for t in range(NT):
                    dve.wait_ge(sig("G0_step"), NT * (k - 1) + t + 1)
                    if t == 0:
                        dve.wait_ge(sig("G0_step"), NT * k)
                    v.tensor_scalar(cur[:, t, :], PS[:, OUT + t, :], adj_inv[:, t:t + 1], None,
                                    ALU.mult).then_inc(sig("G0_cur"), 1)
                dve.wait_ge(sig("G0_cur"), NT * (k + 1))
                for t in range(NT):
                    ins = v.scalar_tensor_tensor(acc[:, t, :], in0=cur[:, t, :], scalar=diff_w[:, k:k + 1],
                                                 in1=acc[:, t, :], op0=ALU.mult, op1=ALU.add)
                done(ins)
            for t in range(NT):
                ins = v.scalar_tensor_tensor(X[:, t, :], in0=acc[:, t, :], scalar=0.0, in1=X[:, t, :],
                                             op0=ALU.max, op1=ALU.add)
            done(ins)

            layer_norm("F0")
            take_transposed("F0")
            dve.wait_ge(sig("bias_ps"), 1)
            v.tensor_copy(bias_cols[:], PS[:, SMALL, 256:326]).then_inc(sig("bias_cols"), 1)
            dve.wait_ge(sig("ld_gate0"), 48)
            top2("F0", gb2_b, True)
            for t in range(NT):
                dve.wait_ge(*at("F0", "out", t + 1))
                v.tensor_tensor(X[:, t, :], PS[:, OUT + t, :], X[:, t, :], ALU.add).then_inc(sig("F0_biased"), 1)
            dve.wait_ge(sig("F0_biased"), NT)
            with dve.Fori(0, EXPERTS) as i:
                dve.wait_ge(sig("F0_y"), i + 1)
                for t in range(NT):
                    ins = v.scalar_tensor_tensor(X[:, t, :], in0=PS[:, OUT + t, :], scalar=cw[:, t, bass.ds(i, 1)],
                                                 in1=X[:, t, :], op0=ALU.mult, op1=ALU.add)
                ins.then_inc(sig("F0_added"), 1)
                dve.wait_ge(sig("F0_added"), i + 1)

            layer_norm("G1")
            dve.wait_ge(sig("ld_ew"), 16)
            done(v.tensor_copy(ew_hi[:], ew[:]))
            done(v.tensor_tensor(ew_lo[:], ew[:], ew_hi[:].bitcast(F32), ALU.subtract))
            hi = ew_hi[:].bitcast(F32).rearrange("p (g u) -> p g u", u=EU)
            lo = ew_lo[:].rearrange("p (g u) -> p g u", u=EU)

            def weighted(g, u):
                v.tensor_scalar(hot_sr[:, u, :], iota[:], ends[:, 0, bass.ds(g, 1), u], None, ALU.is_equal)
                v.tensor_scalar(hot_dw[:, u, 0:N], iota[:], ends[:, 1, bass.ds(g, 1), u],
                                hi[:, bass.ds(g, 1), u], ALU.is_equal, ALU.mult)
                v.tensor_scalar(hot_dw[:, u, N:2 * N], iota[:], ends[:, 1, bass.ds(g, 1), u],
                                lo[:, bass.ds(g, 1), u], ALU.is_equal, ALU.mult).then_inc(sig("hotw"), 1)

            for u in range(EU):
                weighted(0, u)
            with dve.Fori(1, EC // EU) as i:
                for u in range(EU):
                    dve.wait_ge(sig("hotw_used"), i * EU + (u - EU + 1))
                    weighted(i, u)
            dve.wait_ge(sig("hotw_used"), EC)
            for t in range(NT):
                ins = v.tensor_copy(wgt[:, t, :], PS[:, 6 + t, 0:N])
            done(ins)
            for t in range(NT):
                v.tensor_tensor(wgt[:, t, :], PS[:, 6 + t, N:2 * N], wgt[:, t, :], ALU.add).then_inc(sig("wgt"), 1)
            dve.wait_ge(sig("deg"), 1)
            done(v.tensor_scalar(deg_inv[:], PS[:, SMALL, 0:N], 1.0, None, ALU.max))
            done(v.reciprocal(deg_inv[:], deg_inv[:]))
            for t in range(NT):
                v.tensor_tensor(mean_w[:, t, :], cnt[:, t, :], deg_inv[:], ALU.mult).then_inc(sig("mean_w"), 1)
            dve.wait_ge(sig("wgtT_ps"), 1)
            for t in range(NT):
                v.tensor_copy(wgtT[:, t, :], PS[:, 5, t * N:(t + 1) * N]).then_inc(sig("wgtT"), 1)

            def take_support(s):
                dve.wait_ge(*at(s, "supT_ps", 1))
                v.tensor_copy(supT[:, 0:2, :], PS[:, TR, :]).then_inc(sig("supT0"), 1)

            take_support("G1")
            dve.wait_ge(sig("ld_w1g"), 32)
            for t in range(NT):
                done(v.tensor_tensor(X[:, t, :], X[:, t, :], b1_b[:], ALU.add))
            add_to_state("G1")

            layer_norm("F1")
            take_transposed("F1")
            dve.wait_ge(sig("wr1_ps"), 1)
            v.tensor_copy(wr1T[:], PS[:, 5, 0:DC * EXPERTS]).then_inc(sig("wr1T"), 1)
            top2("F1", None, False)

            def weigh_hidden(s):
                for k in range(DC):
                    dve.wait_ge(*at(s, "spread", k // 2 + 1))
                    dve.wait_ge(*at(s, "act", k + 1))
                    v.tensor_tensor(wide[:, k, :], wide[:, k, :], PS[:, TR + k // 2, (k % 2) * N:(k % 2 + 1) * N],
                                    ALU.mult).then_inc(sig("hid"), 1)

            weigh_hidden("F1")
            add_to_state("F1")

            layer_norm("G2")
            dve.wait_ge(*at("G2", "xn", NT))
            for t in range(NT):
                ins = v.tensor_tensor_reduce(out=cur[:, t, :], in0=xn[:, t, :], in1=xn[:, t, :], scale=1.0, scalar=0.0,
                                             op0=ALU.mult, op1=ALU.add, accum_out=sm[:, t:t + 1])
            ins.then_inc(sig("G2_sumsq"), 1)
            dve.wait_ge(sig("G2_exps"), 2)
            done(v.tensor_scalar(sc[:, 3:4], sc[:, 2:3], 0.25, None, ALU.mult))
            dve.wait_ge(sig("G2_rnorm"), 1)
            for t in range(NT):
                v.tensor_scalar(acc[:, t, :], xn[:, t, :], rs[:, t:t + 1], None, ALU.mult).then_inc(sig("G2_unit"), 1)
            take_transposed("G2")
            for t in range(NT):
                dve.wait_ge(sig("G2_sim"), t + 1)
                done(v.tensor_copy(sim[:, t, :], PS[:, OUT + t, 0:N]))
                v.tensor_tensor(sim[:, t, t * P:(t + 1) * P], sim[:, t, t * P:(t + 1) * P], off_diag[:],
                                ALU.mult).then_inc(sig("G2_masked"), 1)
            dve.wait_ge(sig("G2_simexp"), NT)
            for t in range(NT):
                ins = v.tensor_tensor_reduce(out=loop[:, t, :], in0=wgt[:, t, :], in1=sup[:, t, :], scale=1.0,
                                             scalar=0.0, op0=ALU.mult, op1=ALU.add, accum_out=norm[:, t:t + 1])
                ins = v.tensor_tensor(loopT[:, t, :], wgtT[:, t, :], sup[:, t, :], ALU.mult)
            done(ins)
            for t in range(NT):
                v.tensor_tensor(loop[:, t, t * P:(t + 1) * P], loop[:, t, t * P:(t + 1) * P], ident[:],
                                ALU.add).then_inc(sig("G2_loop"), 1)
                ins = v.tensor_tensor(loopT[:, t, t * P:(t + 1) * P], loopT[:, t, t * P:(t + 1) * P], ident[:], ALU.add)
                ins.then_inc(sig("G2_loopT"), 1)
            done(v.tensor_scalar(norm[:], norm[:], sc[:, 0:1], sc[:, 0:1], ALU.mult, ALU.add))
            done(v.tensor_scalar(norm[:], norm[:], sc[:, 1:2], None, ALU.add))
            done(v.reciprocal(norm[:], norm[:]))
            v.tensor_scalar(r2[:], norm[:], sc[:, 0:1], None, ALU.mult)
            done(v.tensor_scalar(rb[:], norm[:], sc[:, 1:2], None, ALU.mult))
            dve.wait_ge(sig("G2_loopT"), NT)
            for t in range(NT):
                v.tensor_scalar(loopTs[:, t, :], loopT[:, t, :], r2[:, t:t + 1], None, ALU.mult).then_inc(sig("G2_loopTs"), 1)
            for t in range(NT):
                ins = v.tensor_scalar(acc[:, t, :], xn[:, t, :], rb[:, t:t + 1], None, ALU.mult)
                ins.then_inc(sig("G2_const"), 1)
            dve.wait_ge(sig("G2_const"), NT)
            for t in range(NT):
                dve.wait_ge(sig("G2_twoT_ps"), t + 1)
                v.tensor_copy(twoT[:, t, :], PS[:, 5 + t, 0:N]).then_inc(sig("G2_twoT"), 1)
            dve.wait_ge(sig("G2_const_ps"), NT)
            for t in range(NT):
                ins = v.scalar_tensor_tensor(acc[:, t, :], in0=PS[:, OUT + t, :], scalar=r2[:, t:t + 1],
                                             in1=acc[:, t, :], op0=ALU.mult, op1=ALU.add)
                ins.then_inc(sig("G2_const2"), 1)
            dve.wait_ge(sig("G2_const2"), NT)
            for k in range(SMOOTH_STEPS // 2):
                last = k == SMOOTH_STEPS // 2 - 1
                dve.wait_ge(sig("G2_two"), NT * (k + 1))
                for t in range(NT):
                    ins = v.scalar_tensor_tensor(cur[:, t, :], in0=PS[:, (OUT, TR)[k % 2] + t, :], scalar=r2[:, t:t + 1],
                                                 in1=acc[:, t, :], op0=ALU.mult, op1=ALU.add)
                    ins.then_inc(sig("G2_cur"), 1)
            dve.wait_ge(sig("G2_cur"), NT * SMOOTH_STEPS // 2)
            for t in range(NT):
                ins = v.tensor_tensor(X[:, t, :], cur[:, t, :], X[:, t, :], ALU.add)
            done(ins)

            layer_norm("F2")
            dve.wait_ge(sig("F2_mean_ps"), 1)
            v.tensor_scalar(meanT[:], PS[:, SMALL, 0:DC], 1.0 / N, None, ALU.mult).then_inc(sig("F2_mean"), 1)
            take_transposed("F2")
            dve.wait_ge(sig("ld_l2"), 32)
            dve.wait_ge(*at("F2", "logits", 1))
            done(v.tensor_tensor(lg[:, 0, :], PS[:, SMALL, 16:16 + GATES2], bg_b[:], ALU.add))
            done(v.max(mx[:, 0, :], lg[:, 0, :]))
            v.tensor_scalar(neg_m[:, 0:1], mx[:, 0, 0:1], -1.0, None, ALU.mult).then_inc(sig("neg_m"), 1)
            dve.wait_ge(*at("F2", "exp", 1))
            done(v.reciprocal(rs[:, 0:1], sm[:, 0:1]))
            done(v.tensor_scalar(lg[:, 1, :], ex[:, 0, :], rs[:, 0:1], None, ALU.mult))
            done(v.max(m2[:, 0, :], lg[:, 1, :]))
            v.max_index(pick[:], m2[:, 0, :], lg[:, 1, :]).then_inc(sig("F2_pick"), 1)
            dve.wait_ge(sig("ld_we_sel"), 32)
            for t in range(NT):
                dve.wait_ge(*at("F2", "out", t + 1))
                done(v.tensor_tensor(cur[:, t, :], PS[:, OUT + t, :], be_sel[:], ALU.add))
                ins = v.scalar_tensor_tensor(X[:, t, :], in0=cur[:, t, :], scalar=m2[:, 0, 0:1], in1=X[:, t, :],
                                             op0=ALU.mult, op1=ALU.add)
            done(ins)

            layer_norm("G3")
            take_transposed("G3")
            take_support("G3")
            dve.wait_ge(sig("ld_b3"), 16)
            for t in range(NT):
                done(v.tensor_tensor(X[:, t, :], X[:, t, :], b3_b[:], ALU.add))
            add_to_state("G3")

            layer_norm("F3")
            take_transposed("F3")
            dve.wait_ge(sig("ld_gate3"), 48)
            top2("F3", br_b, False)
            weigh_hidden("F3")
            for t in range(NT):
                dve.wait_ge(*at("F3", "out", t + 1))
                v.tensor_tensor(X[:, t, :], PS[:, OUT + t, :], X[:, t, :], ALU.add).then_inc(sig("X_final"), 1)

        @block.scalar
        def _(act):
            a = nc.scalar

            def take_transposed(s):
                act.wait_ge(*at(s, "xT", 2))
                a.activation(xnT[:, 2:4, :], PS[:, TR + 1, :], ACT.Copy).then_inc(sig("xnT1"), 1)

            def router_exps(s, softmax_of_two):
                act.wait_ge(*at(s, "neg_m", 1))
                for t in range(NT):
                    a.activation(ex[:, t, 0:EXPERTS], lg[:, t, 0:EXPERTS], ACT.Exp, bias=neg_m[:, t:t + 1],
                                 accum_out=sm[:, t:t + 1]).then_inc(sig("exp"), 1)
                if softmax_of_two:
                    act.wait_ge(sig(s + "_gap"), 1)
                    a.activation(gap[:], gap[:], ACT.Exp).then_inc(sig(s + "_gap_exp"), 1)

            def take_support(s):
                act.wait_ge(*at(s, "supT_ps", 2))
                a.activation(supT[:, 2:4, :], PS[:, TR + 1, :], ACT.Copy).then_inc(sig("supT1"), 1)

            take_transposed("G0")
            take_transposed("F0")
            act.wait_ge(sig("bias_cols"), 1)
            for j in range(NT):
                act.wait_ge(sig("F0_gate"), j + 1)
                a.activation(wide[:, j, :], PS[:, 6 + j, 0:N], ACT.Relu,
                             bias=bias_cols[:, 64 + j:65 + j]).then_inc(sig("F0_gate_act"), 1)
            router_exps("F0", True)
            for m, (wT, name) in enumerate(((w1T, "w1T"), (w2T, "w2T"))):
                for c in range(DC):
                    act.wait_ge(sig("wT_ps"), m * DC + c + 1)
                    a.activation(wT[:, c, :], PS[:, TR + c % 2, :], ACT.Copy).then_inc(sig(name), 1)
            be1_cols = bias_cols[:, 0:EXPERTS * HC].rearrange("p (e k) -> p e k", k=HC)
            with act.Fori(0, EXPERTS) as i:
                for k in range(HC):
                    if k % 2 == 0:
                        act.wait_ge(sig("F0_hidden"), i * DC + (k // 2 + 1))
                    a.activation(wide[:, k, :], PS[:, HID + k // 2, (k % 2) * N:(k % 2 + 1) * N], ACT.Gelu,
                                 bias=be1_cols[:, bass.ds(i, 1), k]).then_inc(sig("F0_act"), 1)

            take_support("G1")
            take_transposed("F1")
            router_exps("F1", False)
            for k in range(DC):
                act.wait_ge(*at("F1", "hidden", k // 2 + 1))
                a.activation(wide[:, k, :], PS[:, 6 + k // 2, (k % 2) * N:(k % 2 + 1) * N],
                             ACT.Gelu).then_inc(sig("act"), 1)

            act.wait_ge(sig("ld_abs"), 48)
            a.activation(sc[:, 0:2], abs_b[:, 0:2], ACT.Exp).then_inc(sig("G2_exps"), 1)
            a.activation(sc[:, 2:3], abs_b[:, 2:3], ACT.Exp, scale=-2.0).then_inc(sig("G2_exps"), 1)
            take_transposed("G2")
            for t in range(NT):
                act.wait_ge(sig("G2_masked"), t + 1)
                a.activation(sup[:, t, :], sim[:, t, :], ACT.Exp, scale=sc[:, 3:4]).then_inc(sig("G2_simexp"), 1)
            for k in range(8):
                act.wait_ge(sig("w3T_ps"), k + 1)
                a.activation(w3T[:, k, :], PS[:, 4 + k % 4, :], ACT.Copy).then_inc(sig("w3T"), 1)

            take_transposed("F2")
            act.wait_ge(*at("F2", "neg_m", 1))
            a.activation(ex[:, 0, :], lg[:, 0, :], ACT.Exp, bias=neg_m[:, 0:1],
                         accum_out=sm[:, 0:1]).then_inc(sig("exp"), 1)

            take_transposed("G3")
            take_support("G3")

            take_transposed("F3")
            router_exps("F3", False)
            for k in range(DC):
                act.wait_ge(*at("F3", "hidden", k // 2 + 1))
                a.activation(wide[:, k, :], PS[:, 6 + k // 2, (k % 2) * N:(k % 2 + 1) * N], ACT.Relu,
                             bias=bias_cols[:, 66 + k:67 + k]).then_inc(sig("act"), 1)

        @block.tensor
        def _(pe):
            mm = nc.tensor.matmul

            def transposes(s, of=xn):
                for t in range(NT):
                    if of is xn:
                        pe.wait_ge(*at(s, "xn", t + 1))
                    else:
                        pe.wait_ge(sig("G2_unit"), t + 1)
                    for c in range(DC):
                        ins = nc.tensor.transpose(PS[:, TR + c // 2, (c % 2) * N + t * P:(c % 2) * N + (t + 1) * P],
                                                  of[:, t, c * P:(c + 1) * P], ident[:])
                        if t == NT - 1 and c % 2 == 1:
                            ins.then_inc(sig("xT"), 1)

            def xnT_ready(s):
                pe.wait_ge(*at(s, "xnT0", 1))
                pe.wait_ge(*at(s, "xnT1", 1))

            def project(lhsT, w, name="out", more=False, first=True):
                for t in range(NT):
                    for c in range(DC):
                        ins = mm(PS[:, OUT + t, :], lhsT[:, c, t * P:(t + 1) * P], w[:, c, :],
                                 start=first and c == 0, stop=not more and c == DC - 1)
                    if not more:
                        ins.then_inc(sig(name), 1)

            def logits(s, lhsT, w, chunks):
                for t in range(NT):
                    for c in range(chunks):
                        ins = mm(PS[:, SMALL, t * EXPERTS:(t + 1) * EXPERTS], lhsT[:, c, t * P:(t + 1) * P], w[:, c, :],
                                 start=c == 0, stop=c == chunks - 1)
                ins.then_inc(sig("logits"), 1)

            def transpose_cw(s):
                pe.wait_ge(*at(s, "cw", 1))
                for t in range(NT):
                    ins = nc.tensor.transpose(PS[0:EXPERTS, SMALL, t * P:(t + 1) * P], cw[:, t, :], ident[:])
                ins.then_inc(sig("cwT_ps"), 1)
                pe.wait_ge(*at(s, "cwT", 1))

            def aggregate(s, m):
                for c in range(DC):
                    for t in range(NT):
                        ins = mm(PS[:, TR + c // 2, (c % 2) * N:(c % 2 + 1) * N], xn[:, t, c * P:(c + 1) * P], m[:, t, :],
                                 start=t == 0, stop=t == NT - 1)
                    if c % 2 == 1:
                        ins.then_inc(sig("supT_ps"), 1)

            def graph_step(lhsT, z, bank, name):
                for t in range(NT):
                    for k in range(NT):
                        ins = mm(PS[:, bank + t, :], lhsT[:, k, t * P:(t + 1) * P], z[:, k, :],
                                 start=k == 0, stop=k == NT - 1)
                    ins.then_inc(sig(name), 1)

            pe.wait_ge(sig("const_ident"), 1)
            transposes("G0")

            def count_edges(n, u, first, last):
                pe.wait_ge(sig("hot"), n)
                for t in range(NT):
                    ins = mm(PS[:, 5 + t, 0:N], hot_s[:, u, t * P:(t + 1) * P], hot_d[:, u, :], start=first, stop=last)
                ins.then_inc(sig("hot_used"), 1)

            for u in range(EU):
                count_edges(u + 1, u, u == 0, False)
            with pe.Fori(1, EC // EU - 1) as i:
                for u in range(EU):
                    count_edges(i * EU + (u + 1), u, False, False)
            for u in range(EU):
                count_edges(EC - EU + u + 1, u, False, u == EU - 1)

            xnT_ready("G0")
            pe.wait_ge(sig("ld_w0"), 16)
            project(xnT, w0, "G0_h")
            pe.wait_ge(sig("cnt"), NT)
            for t in range(NT):
                for k in range(NT):
                    ins = nc.tensor.transpose(PS[:, 5 + t, k * P:(k + 1) * P], cnt[:, k, t * P:(t + 1) * P], ident[:])
            ins.then_inc(sig("cntT"), 1)
            pe.wait_ge(sig("adj"), NT)
            for k in range(DIFFUSION_STEPS):
                pe.wait_ge(sig("G0_cur"), NT * (k + 1))
                graph_step(adj, cur, OUT, "G0_step")

            transposes("F0")
            pe.wait_ge(sig("ld_bias_rows"), 48)
            nc.tensor.transpose(PS[:, SMALL, 256:326], bias_rows[:], ident[0:70, 0:70]).then_inc(sig("bias_ps"), 1)
            xnT_ready("F0")
            pe.wait_ge(sig("ld_gate0"), 48)
            for j in range(NT):
                for c in range(DC):
                    ins = mm(PS[:, 6 + j, 0:N], gw1[:, c, j * P:(j + 1) * P], xnT[:, c, :], start=c == 0, stop=c == DC - 1)
                ins.then_inc(sig("F0_gate"), 1)
            pe.wait_ge(sig("F0_gate_act"), NT)
            pe.wait_ge(sig("bias_cols"), 1)
            logits("F0", wide, gw2, NT)
            for m, (raw, name) in enumerate(((w1_raw, "ld_w1_raw"), (w2_raw, "ld_w2_raw"))):
                pe.wait_ge(sig(name), 16 if m == 0 else 16 * DC)
                for c in range(DC):
                    if m + c >= 2 or m == 1:
                        pe.wait_ge(sig("w1T" if m * DC + c - 1 <= DC else "w2T"),
                                   m * DC + c - 1 if m * DC + c - 1 <= DC else m * DC + c - 1 - DC)
                    for k in range(DC):
                        ins = nc.tensor.transpose(PS[:, TR + c % 2, k * P:(k + 1) * P], raw[:, k, c * P:(c + 1) * P],
                                                  ident[:])
                    ins.then_inc(sig("wT_ps"), 1)
            transpose_cw("F0")
            pe.wait_ge(sig("ld_be2"), 16)
            for t in range(NT):
                mm(PS[:, OUT + t, :], cwT[:, t * P:(t + 1) * P], be2_sb[:], start=True, stop=True).then_inc(sig("out"), 1)

            def expert(first_load, e_hidden, u, before):
                pe.wait_ge(sig(f"ld_we1_slot{u}"), first_load)
                for k in range(HC):
                    for c in range(DC):
                        ins = mm(PS[:, HID + k // 2, (k % 2) * N:(k % 2 + 1) * N],
                                 we1_ring[u][:, c, k * P:(k + 1) * P], xnT[:, c, :], start=c == 0, stop=c == DC - 1)
                    if k % 2 == 1:
                        ins.then_inc(sig("F0_hidden"), 1)
                pe.wait_ge(sig(f"ld_we2_slot{u}"), first_load)
                if before is not None:
                    pe.wait_ge(sig("F0_added"), before)
                else:
                    pe.wait_ge(sig("F0_biased"), NT)
                for k in range(HC):
                    pe.wait_ge(sig("F0_act"), e_hidden + (k + 1))
                    for t in range(NT):
                        ins = mm(PS[:, OUT + t, :], wide[:, k, t * P:(t + 1) * P], we2_ring[u][:, k, :],
                                 start=k == 0, stop=k == HC - 1)
                ins.then_inc(sig("F0_y"), 1)

            pe.wait_ge(sig("w2T"), DC)
            expert(16, 0, 0, None)
            expert(16, HC, 1, 1)
            with pe.Fori(1, EXPERTS // 2) as i:
                for u in range(2):
                    expert(i * 16 + 16, i * (2 * HC) + u * HC, u, i * 2 + u)

            def weigh_edges(n, u, first, last):
                pe.wait_ge(sig("hotw"), n)
                for t in range(NT):
                    ins = mm(PS[:, 6 + t, :], hot_sr[:, u, t * P:(t + 1) * P], hot_dw[:, u, :], start=first, stop=last)
                ins.then_inc(sig("hotw_used"), 1)

            for u in range(EU):
                weigh_edges(u + 1, u, u == 0, False)
            with pe.Fori(1, EC // EU - 1) as i:
                for u in range(EU):
                    weigh_edges(i * EU + (u + 1), u, False, False)
            for u in range(EU):
                weigh_edges(EC - EU + u + 1, u, False, u == EU - 1)
            for t in range(NT):
                ins = mm(PS[:, SMALL, 0:N], ones[:], cnt[:, t, :], start=t == 0, stop=t == NT - 1)
            ins.then_inc(sig("deg"), 1)
            pe.wait_ge(sig("wgt"), NT)
            for t in range(NT):
                for k in range(NT):
                    ins = nc.tensor.transpose(PS[:, 5, t * N + k * P:t * N + (k + 1) * P], wgt[:, k, t * P:(t + 1) * P],
                                              ident[:])
            ins.then_inc(sig("wgtT_ps"), 1)
            pe.wait_ge(*at("G1", "xn", NT))
            aggregate("G1", wgt)
            pe.wait_ge(*at("G1", "supT0", 1))
            pe.wait_ge(*at("G1", "supT1", 1))
            pe.wait_ge(sig("ld_w1g"), 32)
            project(supT, w1g)

            pe.wait_ge(sig("ld_wr1"), 16)
            pe.wait_ge(sig("wgtT"), NT)
            for c in range(DC):
                ins = nc.tensor.transpose(PS[:, 5, c * EXPERTS:(c + 1) * EXPERTS], wr_rows[:, c * P:(c + 1) * P],
                                          ident[0:EXPERTS, 0:EXPERTS])
            ins.then_inc(sig("wr1_ps"), 1)
            transposes("F1")
            xnT_ready("F1")
            pe.wait_ge(sig("wr1T"), 1)
            logits("F1", xnT, wr1T, DC)

            def small_experts(s, w1, w2, b2):
                for k in range(DC):
                    for c in range(DC):
                        ins = mm(PS[:, 6 + k // 2, (k % 2) * N:(k % 2 + 1) * N], w1[:, c, k * P:(k + 1) * P],
                                 xnT[:, c, :], start=c == 0, stop=c == DC - 1)
                    if k % 2 == 1:
                        ins.then_inc(sig("hidden"), 1)
                transpose_cw(s)
                for k in range(DC):
                    ins = mm(PS[:, TR + k // 2, (k % 2) * N:(k % 2 + 1) * N], spread[:, k * P:(k + 1) * P], cwT[:],
                             start=True, stop=True)
                    if k % 2 == 1:
                        ins.then_inc(sig("spread"), 1)
                if b2 is not None:
                    for t in range(NT):
                        mm(PS[:, OUT + t, :], cwT[:, t * P:(t + 1) * P], b2[:], start=True, stop=False)
                pe.wait_ge(*at(s, "hid", DC))
                project(wide, w2, first=b2 is None)

            pe.wait_ge(sig("const_spread"), 3)
            small_experts("F1", w1T, w2T, None)

            transposes("G2", acc)
            xnT_ready("G2")
            for t in range(NT):
                for c in range(DC):
                    ins = mm(PS[:, OUT + t, 0:N], xnT[:, c, t * P:(t + 1) * P], xnT[:, c, :], start=c == 0, stop=c == DC - 1)
                ins.then_inc(sig("G2_sim"), 1)
            pe.wait_ge(sig("G2_loop"), NT)
            pe.wait_ge(sig("G2_loopTs"), NT)
            for t in range(NT):
                for k in range(NT):
                    ins = mm(PS[:, 5 + t, 0:N], loop[:, k, t * P:(t + 1) * P], loopTs[:, k, :], start=k == 0, stop=k == NT - 1)
                ins.then_inc(sig("G2_twoT_ps"), 1)
            pe.wait_ge(sig("G2_const"), NT)
            graph_step(loopT, acc, OUT, "G2_const_ps")
            pe.wait_ge(sig("G2_twoT"), NT)
            pe.wait_ge(sig("G2_const2"), NT)
            for k in range(SMOOTH_STEPS // 2):
                if k:
                    pe.wait_ge(sig("G2_cur"), NT * k)
                graph_step(twoT, cur if k else xn, (OUT, TR)[k % 2], "G2_two")
            pe.wait_ge(sig("ld_w3_raw"), 16)
            for k in range(8):
                if k >= 4:
                    pe.wait_ge(sig("w3T"), k - 3)
                for c in range(DC):
                    ins = nc.tensor.transpose(PS[:, 4 + k % 4, c * P:(c + 1) * P], w3_raw[:, c, k * P:(k + 1) * P], ident[:])
                ins.then_inc(sig("w3T_ps"), 1)

            pe.wait_ge(*at("F2", "xn", NT))
            pe.wait_ge(sig("w3T"), 8)
            for c in range(DC):
                for t in range(NT):
                    ins = mm(PS[:, SMALL, c:c + 1], xn[:, t, c * P:(c + 1) * P], ones[:, 0:1], start=t == 0, stop=t == NT - 1)
            ins.then_inc(sig("F2_mean_ps"), 1)
            pe.wait_ge(sig("F2_mean"), 1)
            pe.wait_ge(sig("ld_l2"), 32)
            for c in range(DC):
                ins = mm(PS[:, SMALL, 16:16 + GATES2], meanT[:, c:c + 1].broadcast_to([P, P]), wg2[:, c, :],
                         start=c == 0, stop=c == DC - 1)
            ins.then_inc(sig("logits"), 1)
            transposes("F2")
            xnT_ready("F2")
            pe.wait_ge(sig("ld_we_sel"), 32)
            project(xnT, we_sel)

            transposes("G3")
            xnT_ready("G3")
            pe.wait_ge(sig("mean_w"), NT)
            aggregate("G3", mean_w)
            project(xnT, w3T[:, 0:4, :], more=True)
            pe.wait_ge(*at("G3", "supT0", 1))
            pe.wait_ge(*at("G3", "supT1", 1))
            project(supT, w3T[:, 4:8, :], first=False)

            transposes("F3")
            xnT_ready("F3")
            pe.wait_ge(sig("ld_gate3"), 48)
            logits("F3", xnT, wr3, DC)
            pe.wait_ge(sig("ld_w31"), 16 * DC)
            pe.wait_ge(sig("ld_w32"), 16)
            small_experts("F3", w31, w32, b2_sb)


_INS = ['x', 'src', 'dst', 'edge_weight', 'L0_gnn_W', 'L0_gnn_b', 'L0_gnn_diffusion_weights', 'L0_ffn_gw1',
        'L0_ffn_gb1', 'L0_ffn_gw2', 'L0_ffn_gb2', 'L0_ffn_we1', 'L0_ffn_be1', 'L0_ffn_we2', 'L0_ffn_be2',
        'L1_gnn_weight', 'L1_gnn_bias', 'L1_ffn_Wr', 'L1_ffn_W1', 'L1_ffn_W2', 'L2_gnn_alpha', 'L2_gnn_beta',
        'L2_gnn_sigma', 'L2_ffn_Wg', 'L2_ffn_bg', 'L2_ffn_We', 'L2_ffn_be', 'L3_gnn_W', 'L3_gnn_b', 'L3_ffn_Wr',
        'L3_ffn_br', 'L3_ffn_W1', 'L3_ffn_b1', 'L3_ffn_W2', 'L3_ffn_b2']


def kernel(**inputs):
    import numpy as _np
    import concourse.bacc as _bacc
    from concourse import mybir as _mybir
    from concourse.bass_utils import run_bass_kernel_spmd as _run

    nc = _bacc.Bacc("TRN2", target_bir_lowering=False, num_devices=1)
    arrays, args = {}, []
    for name in _INS:
        a = _np.ascontiguousarray(inputs[name])
        arrays[f"in_{name}_dram"] = a
        args.append(nc.dram_tensor(f"in_{name}_dram", a.shape, _mybir.dt.from_np(a.dtype), kind="ExternalInput").ap())
    args.append(nc.dram_tensor("out_dram", (N, D), F32, kind="ExternalOutput").ap())
    build(nc, *args)
    r = _run(nc, [arrays], core_ids=[0])
    return r.results[0]["out_dram"]
```

```python
from contextlib import ExitStack

import concourse.bass as bass
from concourse import mybir

ALU = mybir.AluOpType
ACT = mybir.ActivationFunctionType
F32 = mybir.dt.float32
F32R = mybir.dt.float32r
BF16 = mybir.dt.bfloat16
I32 = mybir.dt.int32
U32 = mybir.dt.uint32
AX_X = mybir.AxisListType.X

P = 128
N = 256
NT = N // P
D = 512
DC = D // P
EDGES = 4096
EC = EDGES // P
EU = 4
HU = 8
EXPERTS = 8
H0 = 1024
HC = H0 // P
LN_EPS = 1e-5
NORM_FLOOR = 1e-12
DIFFUSION_STEPS = 3
SMOOTH_STEPS = 10
GATES2 = 16


def build(nc, x, src, dst, edge_weight, L0_gnn_W, L0_gnn_b, L0_gnn_diffusion_weights, L0_ffn_gw1, L0_ffn_gb1,
          L0_ffn_gw2, L0_ffn_gb2, L0_ffn_we1, L0_ffn_be1, L0_ffn_we2, L0_ffn_be2, L1_gnn_weight, L1_gnn_bias,
          L1_ffn_Wr, L1_ffn_W1, L1_ffn_W2, L2_gnn_alpha, L2_gnn_beta, L2_gnn_sigma, L2_ffn_Wg, L2_ffn_bg,
          L2_ffn_We, L2_ffn_be, L3_gnn_W, L3_gnn_b, L3_ffn_Wr, L3_ffn_br, L3_ffn_W1, L3_ffn_b1, L3_ffn_W2,
          L3_ffn_b2, out):
    with ExitStack() as ctx:
        def sb(name, shape, dt=F32):
            return ctx.enter_context(nc.sbuf_tensor(name, shape, dt))

        sems = {}

        def sig(name):
            if name not in sems:
                sems[name] = ctx.enter_context(nc.semaphore(name))
            return sems[name]

        every = ("G0", "F0", "G1", "F1", "G2", "F2", "G3", "F3")
        turned = tuple(s for s in every if s != "G1")
        routed = ("F0", "F1", "F3")
        GIVEN = {
            "var": dict.fromkeys(every, NT), "rstd": dict.fromkeys(every, NT), "xn": dict.fromkeys(every, NT),
            "xT": dict.fromkeys(turned, NT), "xnT": dict.fromkeys(turned, NT),
            "logits": {"F0": NT, "F1": NT, "F2": 1, "F3": NT}, "neg_m": {"F0": NT, "F1": NT, "F2": 1, "F3": NT},
            "exp": {"F0": NT, "F1": NT, "F2": 1, "F3": NT}, "cw": dict.fromkeys(routed, NT),
            "cwT_ps": dict.fromkeys(routed, NT), "cwT": dict.fromkeys(routed, NT),
            "out": dict.fromkeys(("F0", "G1", "F1", "F2", "G3", "F3"), NT),
            "hidden": {"F1": NT, "F3": NT}, "act": {"F1": NT, "F3": NT}, "hid": {"F1": NT, "F3": NT},
            "spread": {"F1": NT, "F3": NT}, "supT_ps": {"G1": 2, "G3": 2}, "supT0": {"G1": 1, "G3": 1},
            "supT1": {"G1": 1, "G3": 1},
        }

        def at(stage, name, n):
            given = GIVEN[name]
            return sig(name), n + sum(k for s, k in given.items() if every.index(s) < every.index(stage))

        X = sb("X", [P, NT, D])
        xn = sb("xn", [P, NT, D])
        xnT = sb("xnT", [P, DC, N])
        wide = sb("wide", [P, HC, N])
        halves = wide[:].rearrange("p k n -> p (k n)").rearrange("p (h t d) -> p h t d", h=2, t=NT)
        hid0 = wide[:, 0:HC // 2, :].rearrange("p k (h n) -> p (k h) n", n=P)
        spare = halves[:, 0]
        other = halves[:, 1]
        cur = sb("cur", [P, NT, D])
        acc = sb("acc", [P, NT, D])
        supT = sb("supT", [P, DC, N])
        gathT, gathT2 = (other[:, b, :].rearrange("p (c n) -> p c n", c=DC) for b in range(2))
        pickT = acc[:, 0, 0:N].rearrange("p (t n) -> p t n", t=NT)
        pickT2 = acc[:, 1, 0:N].rearrange("p (t n) -> p t n", t=NT)
        put2 = acc[:, 0, N:2 * N]
        y2 = cur[:, 0, :]
        touched = acc[:, 1, N:N + 8]
        put = sb("put", [P, 2, N], F32R)
        be1_now = sb("be1_now", [P, HC])
        y_hi = sb("y_hi", [P, D], F32R)
        y_lo = sb("y_lo", [P, D], F32R)
        bn = sb("bn", [P, NT, 6])
        mv = sb("mv", [P, NT, 2])
        rstd = sb("rstd", [P, NT])
        neg_half = sb("neg_half", [P, NT])

        ident = sb("ident", [P, P])
        ones = sb("ones", [P, P])
        iota = sb("iota", [P, N], BF16)
        upto = sb("upto", [P, P], BF16)
        ones_b = sb("ones_b", [P, P], BF16)
        iota8 = sb("iota8", [P, EXPERTS])
        spread = sb("spread", [EXPERTS, D])

        edge_i = sb("edge_i", [P, 2, EC], I32)
        edge_f = sb("edge_f", [P, 2, EC])
        ew = sb("ew", [P, EC])
        ew_hi = sb("ew_hi", [P, EC], F32R)
        ew_lo = sb("ew_lo", [P, EC])
        hot_sr = sb("hot_sr", [P, EU, N], F32R)
        hot_dw = sb("hot_dw", [P, EU, 2 * N], F32R)
        cnt = sb("cnt", [P, NT, N])
        adj = sb("adj", [P, NT, N])
        adj_sum = sb("adj_sum", [P, NT])
        adj_inv = sb("adj_inv", [P, NT])
        wgt = sb("wgt", [P, NT, N])
        wgtT = sb("wgtT", [P, NT, N])
        mean_w = sb("mean_w", [P, NT, N])
        deg_inv = sb("deg_inv", [P, N])

        diff_w = sb("diff_w", [P, DIFFUSION_STEPS + 1])
        bias_rows = sb("bias_rows", [70, P])
        bias_cols = sb("bias_cols", [P, 70])
        gb2_b = sb("gb2_b", [P, EXPERTS])
        br_b = sb("br_b", [P, EXPERTS])
        bg_b = sb("bg_b", [P, GATES2])
        be2_sb = sb("be2_sb", [EXPERTS, D])
        b2_sb = sb("b2_sb", [EXPERTS, D])
        b0_b = sb("b0_b", [P, D])
        b1_b = sb("b1_b", [P, D])
        b3_b = sb("b3_b", [P, D])
        be_sel = sb("be_sel", [P, D])
        wr_rows = sb("wr_rows", [EXPERTS, D])
        wr1T = sb("wr1T", [P, DC, EXPERTS])
        wr3 = sb("wr3", [P, DC, EXPERTS])
        gw2 = sb("gw2", [P, NT, EXPERTS])
        wg2 = sb("wg2", [P, DC, GATES2])
        abs_b = sb("abs_b", [P, 3])

        lg = sb("lg", [P, NT, GATES2])
        mx = sb("mx", [P, NT, 8])
        neg_m = sb("neg_m", [P, NT])
        ex = sb("ex", [P, NT, GATES2])
        sm = sb("sm", [P, NT])
        rs = sb("rs", [P, NT])
        sw = sb("sw", [P, NT, EXPERTS])
        m2 = sb("m2", [P, NT, 8])
        ix = sb("ix", [P, NT, 8], U32)
        ixf = sb("ixf", [P, NT, 2])
        pw = sb("pw", [P, NT, 2])
        gap = sb("gap", [P, NT])
        cwa = sb("cwa", [P, NT, EXPERTS])
        cwb = sb("cwb", [P, NT, EXPERTS])
        cw = sb("cw", [P, NT, EXPERTS])
        cwT = sb("cwT", [EXPERTS, N])
        chosen = sb("chosen", [P, NT, EXPERTS], BF16)
        slot = sb("slot", [P, NT, EXPERTS])
        before = sb("before", [P, 4, 4 + EXPERTS])
        plan = sb("plan", [P, 2, EXPERTS], I32)

        off_diag = sb("off_diag", [P, NT, N])
        norm_diag = sb("norm_diag", [P, NT, P])
        cross = supT[:, 0:2, :]
        sim = supT[:, 2:4, :]
        sup = sb("sup", [P, NT, N])
        loopT = sb("loopT", [P, NT, N])
        loop = sb("loop", [P, NT, N])
        loopTs = sb("loopTs", [P, NT, N])
        twoT = sb("twoT", [P, NT, N])
        scaled, scaled2, poly = loop, loopT, twoT
        sc = sb("sc", [P, 16])
        norm = sb("norm", [P, NT])
        r2 = sb("r2", [P, NT])
        rb = sb("rb", [P, NT])
        meanT = sb("meanT", [P, DC])
        pick = sb("pick", [P, 8], U32)

        w0 = sb("w0", [P, DC, D])
        gw1 = sb("gw1", [P, DC, N])
        w1g = sb("w1g", [P, DC, D])
        w1T = sb("w1T", [P, DC, D])
        w2T = sb("w2T", [P, DC, D])
        ring = sb("ring", [P, 2, 2, 4096])

        we1_ring = [ring[:, u, 0, :].rearrange("p (c n) -> p c n", c=DC) for u in range(2)]
        we2_ring = [ring[:, u, 1, :].rearrange("p (k n) -> p k n", k=HC) for u in range(2)]

        w1_raw = sb("w1_raw", [P, DC, D])
        w2_raw = w0
        hots = ring[:, 1, :, :].bitcast(BF16).rearrange("p m (j n) -> p m j n", n=N)
        hot_s, hot_d = hots[:, 0], hots[:, 1]
        w3_raw = ring[:, 0, 0, :].rearrange("p (c n) -> p c n", c=DC)
        w3T = ring[:, 0, 1, :].rearrange("p (k n) -> p k n", k=8)
        we_sel = ring[:, 1, 0, 0:2048].rearrange("p (c n) -> p c n", c=DC)
        w31 = ring[:, 1, 0, 2048:4096].rearrange("p (c n) -> p c n", c=DC)
        w32 = ring[:, 1, 1, 0:2048].rearrange("p (c n) -> p c n", c=DC)

        PS = ctx.enter_context(nc.psum_tensor("PS", [P, 8, 512], F32))
        WARM = (8, 8, 4)
        TR, OUT, SMALL, HID0, HID = 0, 2, 4, 4, 6
        YB, GB = 6, 7

        block = ctx.enter_context(nc.Block())

        @block.sync
        def _(sp):
            def load(to, of, name):
                sp.dma_start(to, of).then_inc(sig(name), 16)

            def load_expert(e, u):
                load(we1_ring[u], L0_ffn_we1[bass.ds(e, 1)].rearrange("a (c p) n -> p (a c) n", p=P), f"ld_we1_slot{u}")
                load(we2_ring[u], L0_ffn_we2[bass.ds(e, 1)].rearrange("a (k p) n -> p (a k) n", p=P), f"ld_we2_slot{u}")

            load(edge_i[:, 0, :], src.rearrange("(p j) -> p j", p=P), "ld_edges")
            load(edge_i[:, 1, :], dst.rearrange("(p j) -> p j", p=P), "ld_edges")
            load(X[:], x.rearrange("(t p) d -> p t d", p=P), "ld_x")
            load(w0[:], L0_gnn_W.rearrange("(c p) n -> p c n", p=P), "ld_w0")
            load(b0_b[:], L0_gnn_b.partition_broadcast(P), "ld_b0")
            load(diff_w[:], L0_gnn_diffusion_weights.partition_broadcast(P), "ld_b0")
            load(bias_rows[0:64, :], L0_ffn_be1.rearrange("e (k p) -> (e k) p", p=P), "ld_bias_rows")
            load(bias_rows[64:66, :], L0_ffn_gb1.rearrange("(k p) -> k p", p=P), "ld_bias_rows")
            load(bias_rows[66:70, :], L3_ffn_b1.rearrange("(a e) f -> a (e f)", a=4), "ld_bias_rows")
            load(gw1[:], L0_ffn_gw1.rearrange("(c p) n -> p c n", p=P), "ld_gate0")
            load(gw2[:], L0_ffn_gw2.rearrange("(c p) n -> p c n", p=P), "ld_gate0")
            load(gb2_b[:], L0_ffn_gb2.partition_broadcast(P), "ld_gate0")
            load(be2_sb[:], L0_ffn_be2, "ld_be2")
            load(ew[:], edge_weight.rearrange("(p j) -> p j", p=P), "ld_ew")
            load_expert(0, 0)
            load(w1_raw[:], L1_ffn_W1.rearrange("e f d -> (e f) d").rearrange("(c p) d -> p c d", p=P), "ld_w1_raw")
            load(w1g[:], L1_gnn_weight.rearrange("(c p) n -> p c n", p=P), "ld_w1g")
            load(b1_b[:], L1_gnn_bias.partition_broadcast(P), "ld_w1g")
            load(wr_rows[:], L1_ffn_Wr, "ld_wr1")
            load(wg2[:], L2_ffn_Wg.rearrange("(c p) n -> p c n", p=P), "ld_l2")
            load(bg_b[:], L2_ffn_bg.partition_broadcast(P), "ld_l2")
            load(abs_b[:, 0:1], L2_gnn_alpha.partition_broadcast(P), "ld_abs")
            load(abs_b[:, 1:2], L2_gnn_beta.partition_broadcast(P), "ld_abs")
            load(abs_b[:, 2:3], L2_gnn_sigma.partition_broadcast(P), "ld_abs")
            load(b3_b[:], L3_gnn_b.partition_broadcast(P), "ld_b3")
            load(wr3[:], L3_ffn_Wr.rearrange("(c p) n -> p c n", p=P), "ld_gate3")
            load(br_b[:], L3_ffn_br.partition_broadcast(P), "ld_gate3")
            load(b2_sb[:], L3_ffn_b2, "ld_gate3")
            sp.wait_ge(sig("G0_h"), NT)
            for c in range(DC):
                load(w2_raw[:, c, :].rearrange("p (e f) -> p e f", e=EXPERTS),
                     L1_ffn_W2[:, c * P:(c + 1) * P, :].rearrange("e p f -> p e f"), "ld_w2_raw")
            sp.wait_ge(sig("counted"), 1)
            load_expert(1, 1)
            with sp.Fori(1, EXPERTS // 2) as g:
                for u in range(2):
                    sp.wait_ge(sig("hotw_used"), g * 2 * EU + (u - 1) * EU)
                    load(we1_ring[u], L0_ffn_we1.rearrange("(g u) (c p) n -> g u p c n", u=2, p=P)
                         [bass.ds(g, 1), u].rearrange("g p c n -> p (g c) n"), f"ld_we1_slot{u}")
                    load(we2_ring[u], L0_ffn_we2.rearrange("(g u) (k p) n -> g u p k n", u=2, p=P)
                         [bass.ds(g, 1), u].rearrange("g p k n -> p (g k) n"), f"ld_we2_slot{u}")
            sp.wait_ge(sig("hotw_used"), (EXPERTS - 1) * EU)
            load(w3_raw, L3_gnn_W.rearrange("(c p) n -> p c n", p=P), "ld_w3_raw")
            sp.wait_ge(sig("hotw_used"), EXPERTS * EU)
            for c in range(DC):
                load(w31[:, c, :].rearrange("p (e f) -> p e f", e=EXPERTS),
                     L3_ffn_W1[:, c * P:(c + 1) * P, :].rearrange("e p f -> p e f"), "ld_w31")
            load(w32, L3_ffn_W2.rearrange("e f d -> (e f) d").rearrange("(c p) d -> p c d", p=P), "ld_w32")
            sp.wait_ge(sig("F2_pick"), 1)
            e = sp.value_load(pick[0:1, 0:1], min_val=0, max_val=GATES2 - 1)
            for c in range(DC):
                load(we_sel[:, c, :], L2_ffn_We[bass.ds(e, 1), c * P:(c + 1) * P, :].rearrange("a p n -> (a p) n"),
                     f"ld_we_sel{c}")
            load(be_sel[:], L2_ffn_be[bass.ds(e, 1)].rearrange("a n -> (a n)").partition_broadcast(P), "ld_be_sel")
            for t in range(NT):
                sp.wait_ge(sig("X_final"), t + 1)
                sp.dma_start(out[t * P:(t + 1) * P, :], X[:, t, :]).then_inc(sig("stored"), 16)
            sp.wait_ge(sig("stored"), 16 * NT)

        @block.gpsimd
        def _(pool):
            g = nc.gpsimd
            g.iota(iota[:], [[1, N]], base=0, channel_multiplier=0,
                   allow_small_or_imprecise_dtypes=True).then_inc(sig("const_iota"), 1)
            g.memset(ident[:], 0.0).then_inc(sig("pool_fill"), 1)
            g.memset(ones[:], 1.0).then_inc(sig("pool_fill"), 1)
            g.memset(neg_half[:], -0.5).then_inc(sig("pool_fill"), 1)
            pool.wait_ge(sig("pool_fill"), 3)
            g.affine_select(out=ident[:], in_=ident[:], compare_op=ALU.not_equal, fill=1.0, base=0,
                            pattern=[[-1, P]], channel_multiplier=1).then_inc(sig("const_ident"), 1)

            def inverse_std(s):
                for t in range(NT):
                    pool.wait_ge(*at(s, "var", t + 1))
                    g.tensor_scalar(rstd[:, t:t + 1], mv[:, t, 1:2], LN_EPS, None, ALU.add).then_inc(sig("var_eps"), 1)
                    pool.wait_ge(sig("var_eps"), NT * every.index(s) + t + 1)
                    g.tensor_tensor(rstd[:, t:t + 1], rstd[:, t:t + 1], neg_half[:, t:t + 1],
                                    ALU.pow).then_inc(sig("rstd"), 1)

            inverse_std("G0")
            g.iota(iota8[:], [[1, EXPERTS]], base=0, channel_multiplier=0,
                   allow_small_or_imprecise_dtypes=True).then_inc(sig("const_iota"), 1)
            g.memset(ones_b[:], 1.0).then_inc(sig("const_upto"), 1)
            g.memset(before[:], 0.0).then_inc(sig("const_upto"), 1)
            pool.wait_ge(sig("const_upto"), 1)
            g.affine_select(out=upto[:], in_=ones_b[:], compare_op=ALU.is_ge, fill=0.0, base=0,
                            pattern=[[1, P]], channel_multiplier=-1).then_inc(sig("const_upto"), 1)
            g.memset(spread[:], 1.0).then_inc(sig("const_spread"), 1)
            g.memset(off_diag[:], 1.0).then_inc(sig("const_mask"), 1)
            pool.wait_ge(sig("const_spread"), 1)
            g.affine_select(out=spread[:], in_=spread[:], compare_op=ALU.is_ge, fill=0.0, base=0,
                            pattern=[[1, D]], channel_multiplier=-64).then_inc(sig("const_spread"), 1)
            pool.wait_ge(sig("const_spread"), 2)
            g.affine_select(out=spread[:], in_=spread[:], compare_op=ALU.is_ge, fill=0.0, base=63,
                            pattern=[[-1, D]], channel_multiplier=64).then_inc(sig("const_spread"), 1)
            pool.wait_ge(sig("const_mask"), 1)
            for t in range(NT):
                g.affine_select(out=off_diag[:, t, :], in_=off_diag[:, t, :], compare_op=ALU.not_equal, fill=0.0,
                                base=t * P, pattern=[[-1, N]], channel_multiplier=1).then_inc(sig("const_mask"), 1)

            for s in ("F0", "G1", "F1", "G2"):
                inverse_std(s)
            pool.wait_ge(sig("G2_sumsq"), NT)
            g.tensor_scalar(rs[:], sm[:], NORM_FLOOR, None, ALU.max).then_inc(sig("G2_floored"), 1)
            pool.wait_ge(sig("G2_floored"), 1)
            g.tensor_tensor(rs[:], rs[:], neg_half[:], ALU.pow).then_inc(sig("G2_rnorm"), 1)
            for s in ("F2", "G3", "F3"):
                inverse_std(s)

        @block.vector
        def _(dve):
            v = nc.vector
            own = [0]

            def done(ins):
                own[0] += 1
                ins.then_inc(sig("dve_own"), 1)
                dve.wait_ge(sig("dve_own"), own[0])

            def row_stats(t):
                done(v.bn_stats(bn[:, t, :], X[:, t, :]))
                v.bn_aggr(mv[:, t, :], bn[:, t, :]).then_inc(sig("var"), 1)

            def normalise(s, t):
                dve.wait_ge(*at(s, "rstd", t + 1))
                v.tensor_scalar(xn[:, t, :], X[:, t, :], mv[:, t, 0:1], rstd[:, t:t + 1],
                                ALU.subtract, ALU.mult).then_inc(sig("xn"), 1)

            def norm_tile(s, t):
                row_stats(t)
                normalise(s, t)

            def top2(s, t, bias, softmax_of_two):
                dve.wait_ge(*at(s, "logits", t + 1))
                of = PS[:, SMALL + t, 0:EXPERTS]
                if bias is None:
                    done(v.tensor_copy(lg[:, t, 0:EXPERTS], of))
                else:
                    done(v.tensor_tensor(lg[:, t, 0:EXPERTS], of, bias[:], ALU.add))
                done(v.max(mx[:, t, :], lg[:, t, 0:EXPERTS]))
                v.tensor_scalar(neg_m[:, t:t + 1], mx[:, t, 0:1], -1.0, None, ALU.mult).then_inc(sig("neg_m"), 1)
                dve.wait_ge(*at(s, "exp", t + 1))
                done(v.reciprocal(rs[:, t:t + 1], sm[:, t:t + 1]))
                done(v.tensor_scalar(sw[:, t, :], ex[:, t, 0:EXPERTS], rs[:, t:t + 1], None, ALU.mult))
                done(v.max(m2[:, t, :], sw[:, t, :]))
                if softmax_of_two:
                    v.tensor_tensor(gap[:, t:t + 1], m2[:, t, 1:2], m2[:, t, 0:1],
                                    ALU.subtract).then_inc(sig("F0_gap"), 1)
                done(v.max_index(ix[:, t, :], m2[:, t, :], sw[:, t, :]))
                done(v.tensor_copy(ixf[:, t, :], ix[:, t, 0:2]))
                if softmax_of_two:
                    done(v.tensor_scalar(chosen[:, t, :], iota8[:], ixf[:, t, 0:1], None, ALU.is_equal))
                    v.scalar_tensor_tensor(chosen[:, t, :], in0=iota8[:], scalar=ixf[:, t, 1:2], in1=chosen[:, t, :],
                                           op0=ALU.is_equal, op1=ALU.add).then_inc(sig("F0_chosen"), 1)
                    dve.wait_ge(sig("F0_gap_exp"), t + 1)
                    done(v.tensor_scalar(pw[:, t, 0:1], gap[:, t:t + 1], 1.0, None, ALU.add))
                    done(v.reciprocal(pw[:, t, 0:1], pw[:, t, 0:1]))
                    done(v.tensor_tensor(pw[:, t, 1:2], pw[:, t, 0:1], gap[:, t:t + 1], ALU.mult))
                    weight = pw
                else:
                    weight = m2
                v.tensor_scalar(cwa[:, t, :], iota8[:], ixf[:, t, 0:1], weight[:, t, 0:1], ALU.is_equal, ALU.mult)
                done(v.tensor_scalar(cwb[:, t, :], iota8[:], ixf[:, t, 1:2], weight[:, t, 1:2],
                                     ALU.is_equal, ALU.mult))
                v.tensor_tensor(cw[:, t, :], cwa[:, t, :], cwb[:, t, :], ALU.add).then_inc(sig("cw"), 1)

            def take_cwT(s, t):
                dve.wait_ge(*at(s, "cwT_ps", t + 1))
                v.tensor_copy(cwT[:, t * P:(t + 1) * P], PS[0:EXPERTS, SMALL + t, 0:P]).then_inc(sig("cwT"), 1)

            def take_support(s):
                dve.wait_ge(*at(s, "supT_ps", 1))
                v.tensor_copy(supT[:, 0:2, :], PS[:, TR, :]).then_inc(sig("supT0"), 1)

            dve.wait_ge(sig("ld_edges"), 32)
            dve.wait_ge(sig("const_iota"), 1)
            done(v.tensor_copy(edge_f[:], edge_i[:]))
            ends8 = edge_f[:].rearrange("p s (g u) -> p s g u", u=HU)
            hot_s8 = hot_s.rearrange("p (g u) n -> p g u n", u=HU)
            hot_d8 = hot_d.rearrange("p (g u) n -> p g u n", u=HU)

            def one_hots(i):
                for u in range(HU):
                    v.tensor_scalar(hot_s8[:, bass.ds(i, 1), u], iota[:], ends8[:, 0, bass.ds(i, 1), u], None,
                                    ALU.is_equal)
                    v.tensor_scalar(hot_d8[:, bass.ds(i, 1), u], iota[:], ends8[:, 1, bass.ds(i, 1), u], None,
                                    ALU.is_equal).then_inc(sig("hot"), 1)

            one_hots(0)
            dve.wait_ge(sig("ld_x"), 16)
            for t in range(NT):
                row_stats(t)
            for t in range(NT):
                normalise("G0", t)
            with dve.Fori(1, EC // HU) as i:
                one_hots(i)
            dve.wait_ge(sig("ld_b0"), 32)

            def take_h(t):
                dve.wait_ge(sig("G0_h"), t + 1)
                v.tensor_tensor(cur[:, t, :], PS[:, OUT + t, :], b0_b[:], ALU.add).then_inc(sig("G0_cur"), 1)

            take_h(0)
            dve.wait_ge(sig("counted"), 1)
            for t in range(NT):
                v.tensor_copy(cnt[:, t, :], PS[:, 4 + t, 0:N]).then_inc(sig("cnt"), 1)
            dve.wait_ge(sig("cntT"), 1)
            for t in range(NT):
                ins = v.tensor_tensor(adj[:, t, :], cnt[:, t, :], PS[:, 6 + t, 0:N], ALU.add)
            done(ins)
            for t in range(NT):
                ins = v.tensor_scalar(adj[:, t, :], adj[:, t, :], 1.0, 0.0, ALU.min, ALU.add,
                                      accum_out=adj_sum[:, t:t + 1])
            done(ins)
            for t in range(NT):
                v.tensor_tensor(adj[:, t, t * P:(t + 1) * P], adj[:, t, t * P:(t + 1) * P], ident[:],
                                ALU.add).then_inc(sig("adj"), 1)
            done(v.tensor_scalar(adj_inv[:], adj_sum[:], 1.0, 1.0, ALU.add, ALU.max))
            done(v.reciprocal(adj_inv[:], adj_inv[:]))
            for t in range(NT):
                v.tensor_scalar(scaled[:, t, :], adj[:, t, :], adj_inv[:, t:t + 1], None, ALU.mult).then_inc(sig("G0_scaled"), 1)
            take_h(1)
            dve.wait_ge(sig("G0_cur"), NT)
            for t in range(NT):
                v.tensor_scalar(acc[:, t, :], cur[:, t, :], diff_w[:, 0:1], None, ALU.mult)
                ins = v.tensor_scalar(poly[:, t, :], adj[:, t, :], diff_w[:, 1:2], None, ALU.mult)
            done(ins)
            for k in range(2, DIFFUSION_STEPS + 1):
                for t in range(NT):
                    dve.wait_ge(sig("G0_power"), NT * (k - 2) + t + 1)
                    power = PS[:, (TR, HID)[k % 2] + t, 0:N]
                    if k < DIFFUSION_STEPS:
                        v.tensor_scalar((scaled, scaled2)[(k - 1) % 2][:, t, :], power, adj_inv[:, t:t + 1], None,
                                        ALU.mult).then_inc(sig("G0_scaled"), 1)
                for t in range(NT):
                    ins = v.scalar_tensor_tensor(poly[:, t, :], in0=PS[:, (TR, HID)[k % 2] + t, 0:N],
                                                 scalar=diff_w[:, k:k + 1], in1=poly[:, t, :], op0=ALU.mult, op1=ALU.add)
                    if k == DIFFUSION_STEPS:
                        ins.then_inc(sig("G0_poly"), 1)
                if k < DIFFUSION_STEPS:
                    done(ins)
            dve.wait_ge(sig("bias_ps"), 1)
            v.tensor_copy(bias_cols[:], PS[:, 4, 0:70]).then_inc(sig("bias_cols"), 1)
            for t in range(NT):
                dve.wait_ge(sig("G0_step"), t + 1)
                done(v.scalar_tensor_tensor(acc[:, t, :], in0=PS[:, OUT + t, :], scalar=adj_inv[:, t:t + 1],
                                            in1=acc[:, t, :], op0=ALU.mult, op1=ALU.add))
                if t:
                    normalise("F0", t - 1)
                done(v.scalar_tensor_tensor(X[:, t, :], in0=acc[:, t, :], scalar=0.0, in1=X[:, t, :],
                                            op0=ALU.max, op1=ALU.add))
                row_stats(t)
            normalise("F0", NT - 1)

            dve.wait_ge(sig("ld_gate0"), 48)
            dve.wait_ge(sig("const_iota"), 2)
            for t in range(NT):
                top2("F0", t, gb2_b, True)
            dve.wait_ge(sig("F0_place"), 1)
            place = PS[:, GB, 0:NT * EXPERTS].rearrange("p (t e) -> p t e", t=NT)
            done(v.tensor_tensor(slot[:], place, chosen[:], ALU.mult))
            v.tensor_scalar(before[:, 0, 4:4 + EXPERTS], PS[:, GB, 2 * EXPERTS:3 * EXPERTS], float(P), None, ALU.is_gt)
            done(v.tensor_scalar(slot[:], slot[:], -1.0, None, ALU.add))

            def pick_tokens(e):
                for t in range(NT):
                    ins = v.tensor_scalar(pickT[:, t, :], iota[:, 0:P], slot[:, t, bass.ds(e, 1)], None, ALU.is_equal)
                ins.then_inc(sig("F0_pickT"), 1)

            pick_tokens(0)
            for t in range(NT):
                take_cwT("F0", t)
            v.tensor_copy(plan[:, 0, :], before[:, 0, 4:4 + EXPERTS])
            done(v.tensor_tensor(before[:, 1, 4:4 + EXPERTS], before[:, 0, 3:3 + EXPERTS],
                                 before[:, 0, 2:2 + EXPERTS], ALU.add))
            for k in range(1, 3):
                done(v.tensor_tensor(before[:, k + 1, 4:4 + EXPERTS], before[:, k, 4:4 + EXPERTS],
                                     before[:, k, 4 - 2 ** k:4 - 2 ** k + EXPERTS], ALU.add))
            v.tensor_copy(plan[:, 1, :], before[:, 3, 4:4 + EXPERTS]).then_inc(sig("F0_plan"), 1)
            dve.wait_ge(sig("ld_ew"), 16)
            done(v.tensor_copy(ew_hi[:], ew[:]))
            done(v.tensor_tensor(ew_lo[:], ew[:], ew_hi[:].bitcast(F32), ALU.subtract))
            ends = edge_f[:].rearrange("p s (g u) -> p s g u", u=EU)
            hi = ew_hi[:].bitcast(F32).rearrange("p (g u) -> p g u", u=EU)
            lo = ew_lo[:].rearrange("p (g u) -> p g u", u=EU)

            def weighted(g):
                for u in range(EU):
                    v.tensor_scalar(hot_sr[:, u, :], iota[:], ends[:, 0, bass.ds(g, 1), u], None, ALU.is_equal)
                    v.tensor_scalar(hot_dw[:, u, 0:N], iota[:], ends[:, 1, bass.ds(g, 1), u],
                                    hi[:, bass.ds(g, 1), u], ALU.is_equal, ALU.mult)
                    v.tensor_scalar(hot_dw[:, u, N:2 * N], iota[:], ends[:, 1, bass.ds(g, 1), u],
                                    lo[:, bass.ds(g, 1), u], ALU.is_equal, ALU.mult).then_inc(sig("hotw"), 1)

            weighted(0)

            dve.wait_ge(sig("F0_plan"), 1)

            def add_block(e):
                for t in range(NT):
                    ins = v.scalar_tensor_tensor(X[:, t, :], in0=PS[:, OUT + t, :], scalar=cw[:, t, bass.ds(e, 1)],
                                                 in1=X[:, t, :], op0=ALU.mult, op1=ALU.add)
                return ins

            def add_expert(e):
                dve.wait_ge(sig("F0_scattered"), e + 1)
                dve.wait_ge(sig("F0_added"), e + 1)
                add_block(e).then_inc(sig("F0_added"), 1)

            def expert(e, first=False, last=False):
                second = dve.value_load(plan[0:1, 0, bass.ds(e, 1)], min_val=0, max_val=1)
                s = dve.value_load(plan[0:1, 1, bass.ds(e, 1)], min_val=0, max_val=EXPERTS)
                if not last:
                    dve.wait_ge(sig("F0_gath_ps"), e * 2 + 2)
                    pick_tokens(e + 1)
                if not first:
                    add_expert(e - 1)
                else:
                    for t in range(NT):
                        dve.wait_ge(*at("F0", "out", t + 1))
                        ins = v.tensor_tensor(X[:, t, :], PS[:, OUT + t, :], X[:, t, :], ALU.add)
                    ins.then_inc(sig("F0_added"), 1)
                dve.wait_ge(sig("F0_y"), e + 1)
                dve.wait_ge(sig("F0_y_hi"), e + 1)
                v.tensor_tensor(y_lo[:], PS[:, YB, :], y_hi[:].bitcast(F32), ALU.subtract).then_inc(sig("F0_y_lo"), 1)
                with dve.If(second > 0):
                    for t in range(NT):
                        ins = v.tensor_scalar(pickT2[:, t, :], iota[:, P:2 * P], slot[:, t, bass.ds(e, 1)], None,
                                              ALU.is_equal)
                    ins.then_inc(sig("second_dve"), 1)
                    dve.wait_ge(sig("second_pe"), s * 5 + 5)
                    dve.wait_ge(sig("F0_added"), e + 1)
                    add_block(e).then_inc(sig("second_dve"), 1)
                    dve.wait_ge(sig("second_dve"), s * 2 + 2)
                    v.memset(touched, 0.0)
                if not last:
                    dve.wait_ge(sig("hotw_used"), e * EU + EU)
                    weighted(e + 1)

            expert(0, first=True)
            with dve.Fori(1, EXPERTS - 1) as i:
                expert(i)
            expert(EXPERTS - 1, last=True)
            dve.wait_ge(sig("hotw_used"), EC)
            for t in range(NT):
                ins = v.tensor_copy(wgt[:, t, :], PS[:, TR + t, 0:N])
            done(ins)
            for t in range(NT):
                v.tensor_tensor(wgt[:, t, :], PS[:, TR + t, N:2 * N], wgt[:, t, :], ALU.add).then_inc(sig("wgt"), 1)
            add_expert(EXPERTS - 1)
            dve.wait_ge(sig("F0_added"), EXPERTS + 1)
            for t in range(NT):
                norm_tile("G1", t)

            dve.wait_ge(sig("ld_w1g"), 32)
            for t in range(NT):
                ins = v.tensor_tensor(X[:, t, :], X[:, t, :], b1_b[:], ALU.add)
            done(ins)
            take_support("G1")
            dve.wait_ge(sig("deg"), 1)
            done(v.tensor_scalar(deg_inv[:], PS[:, 6, 0:N], 1.0, None, ALU.max))
            done(v.reciprocal(deg_inv[:], deg_inv[:]))
            for t in range(NT):
                v.tensor_tensor(mean_w[:, t, :], cnt[:, t, :], deg_inv[:], ALU.mult).then_inc(sig("mean_w"), 1)
            dve.wait_ge(sig("wgtT_ps"), 1)
            for t in range(NT):
                v.tensor_copy(wgtT[:, t, :], PS[:, 7, t * N:(t + 1) * N]).then_inc(sig("wgtT"), 1)
            v.tensor_copy(wr1T[:], PS[:, 6, N:N + DC * EXPERTS]).then_inc(sig("wr1T"), 1)
            for t in range(NT):
                dve.wait_ge(*at("G1", "out", t + 1))
                done(v.tensor_tensor(X[:, t, :], PS[:, OUT + t, :], X[:, t, :], ALU.add))
                norm_tile("F1", t)

            def small_experts(s, bias):
                top2(s, 0, bias, False)
                take_cwT(s, 0)
                top2(s, 1, bias, False)
                for t in range(NT):
                    if t:
                        take_cwT(s, t)
                    dve.wait_ge(*at(s, "spread", t + 1))
                    dve.wait_ge(*at(s, "act", t + 1))
                    hidden = wide[:, t * DC:(t + 1) * DC, 0:P]
                    v.tensor_tensor(hidden, hidden, PS[:, TR + t, :].rearrange("p (k n) -> p k n", k=DC),
                                    ALU.mult).then_inc(sig("hid"), 1)

            small_experts("F1", None)
            dve.wait_ge(sig("G2_exps"), 2)
            done(v.tensor_scalar(sc[:, 3:4], sc[:, 2:3], 0.25, None, ALU.mult))
            for t in range(NT):
                dve.wait_ge(*at("F1", "out", t + 1))
                done(v.tensor_tensor(X[:, t, :], PS[:, OUT + t, :], X[:, t, :], ALU.add))
                norm_tile("G2", t)

            dve.wait_ge(*at("G2", "xn", NT))
            for t in range(NT):
                v.tensor_tensor_reduce(out=cur[:, t, :], in0=xn[:, t, :], in1=xn[:, t, :], scale=1.0, scalar=0.0,
                                       op0=ALU.mult, op1=ALU.add, accum_out=sm[:, t:t + 1]).then_inc(sig("G2_sumsq"), 1)
            dve.wait_ge(sig("G2_rnorm"), 1)
            for t in range(NT):
                v.tensor_scalar(norm_diag[:, t, :], ident[:], rs[:, t:t + 1], None, ALU.mult).then_inc(sig("G2_norm_diag"), 1)
            dve.wait_ge(sig("G2_cross_ps"), 1)
            dve.wait_ge(sig("const_mask"), 1 + NT)
            for t in range(NT):
                ins = v.tensor_tensor(cross[:, t, :], PS[:, 5, 0:N], off_diag[:, t, :], ALU.mult)
            done(ins)
            for t in range(NT):
                dve.wait_ge(sig("G2_sim"), t + 1)
                v.scalar_tensor_tensor(sim[:, t, :], in0=PS[:, OUT + t, 0:N], scalar=rs[:, t:t + 1], in1=cross[:, t, :],
                                       op0=ALU.mult, op1=ALU.mult).then_inc(sig("G2_masked"), 1)
            for t in range(NT):
                dve.wait_ge(sig("G2_simexp"), t + 1)
                v.tensor_tensor_reduce(out=loop[:, t, :], in0=wgt[:, t, :], in1=sup[:, t, :], scale=1.0,
                                       scalar=0.0, op0=ALU.mult, op1=ALU.add, accum_out=norm[:, t:t + 1])
                ins = v.tensor_tensor(loopT[:, t, :], wgtT[:, t, :], sup[:, t, :], ALU.mult)
            done(ins)
            for t in range(NT):
                v.tensor_tensor(loop[:, t, t * P:(t + 1) * P], loop[:, t, t * P:(t + 1) * P], ident[:],
                                ALU.add).then_inc(sig("G2_loop"), 1)
                ins = v.tensor_tensor(loopT[:, t, t * P:(t + 1) * P], loopT[:, t, t * P:(t + 1) * P], ident[:], ALU.add)
                ins.then_inc(sig("G2_loopT"), 1)
            done(v.tensor_scalar(norm[:], norm[:], sc[:, 0:1], sc[:, 0:1], ALU.mult, ALU.add))
            done(v.tensor_scalar(norm[:], norm[:], sc[:, 1:2], None, ALU.add))
            done(v.reciprocal(norm[:], norm[:]))
            v.tensor_scalar(r2[:], norm[:], sc[:, 0:1], None, ALU.mult)
            done(v.tensor_scalar(rb[:], norm[:], sc[:, 1:2], None, ALU.mult))
            for t in range(NT):
                v.tensor_scalar(acc[:, t, :], xn[:, t, :], rb[:, t:t + 1], None, ALU.mult).then_inc(sig("G2_const"), 1)
            dve.wait_ge(sig("G2_loopT"), NT)
            for t in range(NT):
                v.tensor_scalar(loopTs[:, t, :], loopT[:, t, :], r2[:, t:t + 1], None,
                                ALU.mult).then_inc(sig("G2_loopTs"), 1)
            dve.wait_ge(sig("G2_const"), NT)
            for t in range(NT):
                dve.wait_ge(sig("G2_const_ps"), t + 1)
                v.scalar_tensor_tensor(spare[:, t, :], in0=PS[:, OUT + t, :], scalar=r2[:, t:t + 1],
                                       in1=acc[:, t, :], op0=ALU.mult, op1=ALU.add).then_inc(sig("G2_const2"), 1)
            for t in range(NT):
                dve.wait_ge(sig("G2_twoT_ps"), t + 1)
                v.tensor_copy(twoT[:, t, :], PS[:, 4 + t, 0:N]).then_inc(sig("G2_twoT"), 1)
            dve.wait_ge(sig("G2_const2"), NT)
            for t in range(NT):
                ins = v.tensor_tensor(X[:, t, :], spare[:, t, :], X[:, t, :], ALU.add)
            done(ins)
            for k in range(SMOOTH_STEPS // 2):
                for t in range(NT):
                    dve.wait_ge(sig("G2_two"), NT * k + t + 1)
                    if k < SMOOTH_STEPS // 2 - 1:
                        v.scalar_tensor_tensor((cur, other)[k % 2][:, t, :], in0=PS[:, (OUT, TR)[k % 2] + t, :],
                                               scalar=r2[:, t:t + 1], in1=spare[:, t, :],
                                               op0=ALU.mult, op1=ALU.add).then_inc(sig("G2_cur"), 1)
                    else:
                        done(v.scalar_tensor_tensor(X[:, t, :], in0=PS[:, (OUT, TR)[k % 2] + t, :],
                                                    scalar=r2[:, t:t + 1], in1=X[:, t, :], op0=ALU.mult, op1=ALU.add))
                        norm_tile("F2", t)

            dve.wait_ge(sig("F2_mean_ps"), 1)
            v.tensor_scalar(meanT[:], PS[:, SMALL, 0:DC], 1.0 / N, None, ALU.mult).then_inc(sig("F2_mean"), 1)
            dve.wait_ge(sig("ld_l2"), 32)
            dve.wait_ge(*at("F2", "logits", 1))
            done(v.tensor_tensor(lg[:, 0, :], PS[:, SMALL, 16:16 + GATES2], bg_b[:], ALU.add))
            done(v.max(mx[:, 0, :], lg[:, 0, :]))
            v.tensor_scalar(neg_m[:, 0:1], mx[:, 0, 0:1], -1.0, None, ALU.mult).then_inc(sig("neg_m"), 1)
            dve.wait_ge(*at("F2", "exp", 1))
            done(v.reciprocal(rs[:, 0:1], sm[:, 0:1]))
            done(v.tensor_scalar(lg[:, 1, :], ex[:, 0, :], rs[:, 0:1], None, ALU.mult))
            done(v.max(m2[:, 0, :], lg[:, 1, :]))
            v.max_index(pick[:], m2[:, 0, :], lg[:, 1, :]).then_inc(sig("F2_pick"), 1)
            dve.wait_ge(sig("ld_be_sel"), 16)
            for t in range(NT):
                ins = v.scalar_tensor_tensor(X[:, t, :], in0=be_sel[:], scalar=m2[:, 0, 0:1], in1=X[:, t, :],
                                             op0=ALU.mult, op1=ALU.add)
            done(ins)
            for t in range(NT):
                dve.wait_ge(*at("F2", "out", t + 1))
                done(v.scalar_tensor_tensor(X[:, t, :], in0=PS[:, OUT + t, :], scalar=m2[:, 0, 0:1], in1=X[:, t, :],
                                            op0=ALU.mult, op1=ALU.add))
                norm_tile("G3", t)

            dve.wait_ge(sig("ld_b3"), 16)
            for t in range(NT):
                ins = v.tensor_tensor(X[:, t, :], X[:, t, :], b3_b[:], ALU.add)
            done(ins)
            take_support("G3")
            for t in range(NT):
                dve.wait_ge(*at("G3", "out", t + 1))
                done(v.tensor_tensor(X[:, t, :], PS[:, OUT + t, :], X[:, t, :], ALU.add))
                norm_tile("F3", t)

            dve.wait_ge(sig("ld_gate3"), 48)
            small_experts("F3", br_b)
            for t in range(NT):
                dve.wait_ge(*at("F3", "out", t + 1))
                v.tensor_tensor(X[:, t, :], PS[:, OUT + t, :], X[:, t, :], ALU.add).then_inc(sig("X_final"), 1)

        @block.scalar
        def _(act):
            a = nc.scalar

            def take_transposed(s, t):
                act.wait_ge(*at(s, "xT", t + 1))
                of = PS[:, TR:TR + 2, :].rearrange("p b (c n) -> p (b c) n", c=2)[:, :, t * P:(t + 1) * P]
                a.activation(xnT[:, :, t * P:(t + 1) * P], of, ACT.Copy).then_inc(sig("xnT"), 1)

            def router_exp(s, t, softmax_of_two=False):
                act.wait_ge(*at(s, "neg_m", t + 1))
                a.activation(ex[:, t, 0:EXPERTS], lg[:, t, 0:EXPERTS], ACT.Exp, bias=neg_m[:, t:t + 1],
                             accum_out=sm[:, t:t + 1]).then_inc(sig("exp"), 1)
                if softmax_of_two:
                    act.wait_ge(sig("F0_gap"), t + 1)
                    a.activation(gap[:, t:t + 1], gap[:, t:t + 1], ACT.Exp).then_inc(sig("F0_gap_exp"), 1)

            def take_support(s):
                act.wait_ge(*at(s, "supT_ps", 2))
                a.activation(supT[:, 2:4, :], PS[:, TR + 1, :], ACT.Copy).then_inc(sig("supT1"), 1)

            def activate(s, t, func, bias):
                act.wait_ge(*at(s, "hidden", t + 1))
                if bias:
                    for k in range(DC):
                        ins = a.activation(wide[:, t * DC + k, 0:P], PS[:, HID + t, k * P:(k + 1) * P], func,
                                           bias=bias_cols[:, 66 + k:67 + k])
                else:
                    ins = a.activation(wide[:, t * DC:(t + 1) * DC, 0:P],
                                       PS[:, HID + t, :].rearrange("p (k n) -> p k n", k=DC), func)
                ins.then_inc(sig("act"), 1)

            for t in range(NT):
                take_transposed("G0", t)
            def gate(t):
                act.wait_ge(sig("F0_gate"), t + 1)
                for j in range(NT):
                    a.activation(wide[:, j, t * P:(t + 1) * P], PS[:, 6, (t * NT + j) * P:(t * NT + j + 1) * P], ACT.Relu,
                                 bias=bias_cols[:, 64 + j:65 + j]).then_inc(sig("F0_gate_act"), 1)

            for c in range(DC):
                act.wait_ge(sig("wT_ps"), c + 1)
                a.activation(w1T[:, c, :], PS[:, 4 + c, :], ACT.Copy).then_inc(sig("w1T"), 1)
            take_transposed("F0", 0)
            act.wait_ge(sig("bias_cols"), 1)
            gate(0)
            take_transposed("F0", 1)
            router_exp("F0", 0, True)
            gate(1)
            router_exp("F0", 1, True)
            for c in range(DC):
                act.wait_ge(sig("wT_ps"), DC + c + 1)
                a.activation(w2T[:, c, :], PS[:, c, :], ACT.Copy).then_inc(sig("w2T"), 1)
            be1_cols = bias_cols[:, 0:EXPERTS * HC].rearrange("p (g u k) -> p g u k", u=2, k=HC)
            plans = plan[:].rearrange("p a (g u) -> p a g u", u=2)
            gb = PS[:, GB, :].rearrange("p (c n) -> p c n", c=DC)

            def take_gathered(e, u):
                act.wait_ge(sig("F0_gath_ps"), e * 2 + 1)
                a.activation(put[:, u, :], PS[:, YB, 0:N], ACT.Copy).then_inc(sig("F0_gath"), 1)
                act.wait_ge(sig("F0_gath_ps"), e * 2 + 2)
                a.activation(gathT, gb, ACT.Copy).then_inc(sig("F0_gath"), 1)

            def expert(g, u, last=False):
                e = g * 2 + u
                second = act.value_load(plans[0:1, 0, bass.ds(g, 1), u], min_val=0, max_val=1)
                s = act.value_load(plans[0:1, 1, bass.ds(g, 1), u], min_val=0, max_val=EXPERTS)

                def gelu(k, bias, name):
                    a.activation(hid0[:, k, :], PS[:, HID0 + k // 4, (k % 4) * P:(k % 4 + 1) * P], ACT.Gelu,
                                 bias=bias).then_inc(sig(name), 1)

                for k in range(HC):
                    if k % 4 == 0:
                        act.wait_ge(sig("F0_hidden"), e * 2 + (k // 4 + 1))
                    gelu(k, be1_cols[:, bass.ds(g, 1), u, k], "F0_act")
                if not last:
                    take_gathered(e + 1, (u + 1) % 2)
                act.wait_ge(sig("F0_y"), e + 1)
                a.activation(y_hi[:], PS[:, YB, :], ACT.Copy).then_inc(sig("F0_y_hi"), 1)
                with act.If(second > 0):
                    a.activation(be1_now[:], be1_cols[:, bass.ds(g, 1), u, :], ACT.Copy).then_inc(sig("second_act"), 1)
                    act.wait_ge(sig("second_pe"), s * 5 + 1)
                    a.activation(put2, PS[:, HID0, 0:N], ACT.Copy)
                    a.activation(gathT2, gb, ACT.Copy).then_inc(sig("second_act"), 1)
                    act.wait_ge(sig("second_act"), s * (HC + 3) + 1)
                    for k in range(HC):
                        if k % 4 == 0:
                            act.wait_ge(sig("second_pe"), s * 5 + (k // 4 + 2))
                        gelu(k, be1_now[:, k:k + 1], "second_act")
                    act.wait_ge(sig("second_pe"), s * 5 + 4)
                    a.activation(y2, PS[:, YB, :], ACT.Copy).then_inc(sig("second_act"), 1)

            take_gathered(0, 0)
            act.wait_ge(sig("F0_plan"), 1)
            with act.Fori(0, EXPERTS // 2 - 1) as i:
                for u in range(2):
                    expert(i, u)
            for u in range(2):
                expert(EXPERTS // 2 - 1, u, last=u == 1)

            take_support("G1")
            take_transposed("F1", 0)
            router_exp("F1", 0)
            take_transposed("F1", 1)
            router_exp("F1", 1)
            act.wait_ge(sig("ld_abs"), 48)
            a.activation(sc[:, 0:2], abs_b[:, 0:2], ACT.Exp).then_inc(sig("G2_exps"), 1)
            a.activation(sc[:, 2:3], abs_b[:, 2:3], ACT.Exp, scale=-2.0).then_inc(sig("G2_exps"), 1)
            for t in range(NT):
                activate("F1", t, ACT.Gelu, False)

            for t in range(NT):
                take_transposed("G2", t)
            for t in range(NT):
                act.wait_ge(sig("G2_masked"), t + 1)
                a.activation(sup[:, t, :], sim[:, t, :], ACT.Exp, scale=sc[:, 3:4]).then_inc(sig("G2_simexp"), 1)

            def take_w3T(k):
                act.wait_ge(sig("w3T_ps"), k + 1)
                a.activation(w3T[:, k, :], PS[:, 4 + k % 4, :], ACT.Copy).then_inc(sig("w3T"), 1)

            for k in range(4):
                take_w3T(k)
            for t in range(NT):
                take_transposed("F2", t)
            act.wait_ge(*at("F2", "neg_m", 1))
            a.activation(ex[:, 0, :], lg[:, 0, :], ACT.Exp, bias=neg_m[:, 0:1],
                         accum_out=sm[:, 0:1]).then_inc(sig("exp"), 1)
            for k in range(4, 8):
                take_w3T(k)

            for t in range(NT):
                take_transposed("G3", t)
            take_support("G3")

            take_transposed("F3", 0)
            router_exp("F3", 0)
            take_transposed("F3", 1)
            activate("F3", 0, ACT.Relu, True)
            router_exp("F3", 1)
            activate("F3", 1, ACT.Relu, True)

        @block.tensor
        def _(pe):
            mm = nc.tensor.matmul
            turn = nc.tensor.transpose

            def transposes(s, t):
                pe.wait_ge(*at(s, "xn", t + 1))
                if t:
                    pe.wait_ge(*at(s, "xnT", t))
                for c in range(DC):
                    ins = turn(PS[:, TR + c // 2, (c % 2) * N + t * P:(c % 2) * N + (t + 1) * P],
                               xn[:, t, c * P:(c + 1) * P], ident[:])
                ins.then_inc(sig("xT"), 1)

            def xnT_ready(s, t):
                pe.wait_ge(*at(s, "xnT", t + 1))

            def project(t, lhsT, w, name="out", more=False, first=True):
                for c in range(DC):
                    ins = mm(PS[:, OUT + t, :], lhsT(c, t), w[:, c, :], start=first and c == 0,
                             stop=not more and c == DC - 1)
                if not more:
                    ins.then_inc(sig(name), 1)

            def of_xnT(c, t):
                return xnT[:, c, t * P:(t + 1) * P]

            def of_supT(c, t):
                return supT[:, c, t * P:(t + 1) * P]

            def of_wide(c, t):
                return wide[:, t * DC + c, 0:P]

            def logits(t, lhsT, w, chunks):
                for c in range(chunks):
                    ins = mm(PS[:, SMALL + t, 0:EXPERTS], lhsT(c, t), w[:, c, :], start=c == 0, stop=c == chunks - 1)
                ins.then_inc(sig("logits"), 1)

            def transpose_cw(s, t):
                pe.wait_ge(*at(s, "cw", t + 1))
                turn(PS[0:EXPERTS, SMALL + t, 0:P], cw[:, t, :], ident[:]).then_inc(sig("cwT_ps"), 1)

            def aggregate(m):
                for c in range(DC):
                    for t in range(NT):
                        ins = mm(PS[:, TR + c // 2, (c % 2) * N:(c % 2 + 1) * N], xn[:, t, c * P:(c + 1) * P], m[:, t, :],
                                 start=t == 0, stop=t == NT - 1)
                    if c % 2 == 1:
                        ins.then_inc(sig("supT_ps"), 1)

            def graph_step(lhsT, z, bank, name, ready):
                for t in range(NT):
                    for k in range(NT):
                        if t == 0:
                            ready(k)
                        ins = mm(PS[:, bank + t, :], lhsT[:, k, t * P:(t + 1) * P], z[:, k, :],
                                 start=k == 0, stop=k == NT - 1)
                    ins.then_inc(sig(name), 1)

            def keep_warm(n, bank):
                for _ in range(n):
                    mm(PS[:, bank, 0:P], ones[:], ones[:], start=True, stop=True)

            pe.wait_ge(sig("const_ident"), 1)
            keep_warm(WARM[0], 7)
            hot_s8 = hot_s.rearrange("p (g u) n -> p g u n", u=HU)
            hot_d8 = hot_d.rearrange("p (g u) n -> p g u n", u=HU)

            def count_edges(g, first=False, last=False):
                for u in range(HU):
                    pe.wait_ge(sig("hot"), g * HU + (u + 1))
                    for t in range(NT):
                        ins = mm(PS[:, 4 + t, 0:N],
                                 hot_s8[:, bass.ds(g, 1), u, t * P:(t + 1) * P].rearrange("p a n -> p (a n)"),
                                 hot_d8[:, bass.ds(g, 1), u].rearrange("p a n -> p (a n)"),
                                 start=first and u == 0, stop=last and u == HU - 1)
                return ins

            def project_h(t):
                xnT_ready("G0", t)
                pe.wait_ge(sig("ld_w0"), 16)
                project(t, of_xnT, w0, "G0_h")

            count_edges(0, first=True)
            for t in range(NT):
                transposes("G0", t)
            project_h(0)
            with pe.Fori(1, EC // HU - 1) as i:
                count_edges(i)
            count_edges(EC // HU - 1, last=True).then_inc(sig("counted"), 1)
            pe.wait_ge(sig("cnt"), NT)
            for t in range(NT):
                for k in range(NT):
                    ins = turn(PS[:, 6 + t, k * P:(k + 1) * P], cnt[:, k, t * P:(t + 1) * P], ident[:])
            ins.then_inc(sig("cntT"), 1)
            project_h(1)
            pe.wait_ge(sig("adj"), NT)
            for k in range(2, DIFFUSION_STEPS + 1):
                of = (scaled, scaled2)[k % 2]
                for t in range(NT):
                    for j in range(NT):
                        if t == 0:
                            pe.wait_ge(sig("G0_scaled"), NT * (k - 2) + j + 1)
                        ins = mm(PS[:, (TR, HID)[k % 2] + t, 0:N], adj[:, j, t * P:(t + 1) * P], of[:, j, :],
                                 start=j == 0, stop=j == NT - 1)
                    ins.then_inc(sig("G0_power"), 1)
            pe.wait_ge(sig("G0_cur"), NT)
            pe.wait_ge(sig("G0_poly"), NT)
            pe.wait_ge(sig("ld_bias_rows"), 48)
            turn(PS[:, 4, 0:70], bias_rows[:], ident[0:70, 0:70]).then_inc(sig("bias_ps"), 1)
            graph_step(poly, cur, OUT, "G0_step", lambda j: None)

            pe.wait_ge(sig("ld_w1_raw"), 16)
            pe.wait_ge(sig("bias_cols"), 1)
            for c in range(DC):
                for k in range(DC):
                    ins = turn(PS[:, 4 + c, k * P:(k + 1) * P], w1_raw[:, k, c * P:(c + 1) * P], ident[:])
                ins.then_inc(sig("wT_ps"), 1)
            pe.wait_ge(sig("ld_gate0"), 48)
            for t in range(NT):
                transposes("F0", t)
                xnT_ready("F0", t)
                if t == 0:
                    pe.wait_ge(sig("w1T"), DC)
                for j in range(NT):
                    for c in range(DC):
                        ins = mm(PS[:, 6, (t * NT + j) * P:(t * NT + j + 1) * P], gw1[:, c, j * P:(j + 1) * P],
                                 of_xnT(c, t), start=c == 0, stop=c == DC - 1)
                ins.then_inc(sig("F0_gate"), 1)
                pe.wait_ge(sig("F0_gate_act"), NT * (t + 1))
                logits(t, lambda c, t: wide[:, c, t * P:(t + 1) * P], gw2, NT)
            pe.wait_ge(sig("ld_w2_raw"), 16 * DC)
            for c in range(DC):
                for k in range(DC):
                    ins = turn(PS[:, c, k * P:(k + 1) * P], w2_raw[:, k, c * P:(c + 1) * P], ident[:])
                ins.then_inc(sig("wT_ps"), 1)
            pe.wait_ge(sig("const_upto"), 3)
            pe.wait_ge(sig("F0_chosen"), 1)
            mm(PS[:, GB, 0:EXPERTS], upto[:], chosen[:, 0, :], start=True, stop=True)
            pe.wait_ge(sig("F0_chosen"), 2)
            for k in range(2):
                cols = PS[:, GB, (k + 1) * EXPERTS:(k + 2) * EXPERTS]
                mm(cols, ones_b[:], chosen[:, 0, :], start=True, stop=False)
                ins = mm(cols, (upto, ones_b)[k][:], chosen[:, 1, :], start=False, stop=True)
            ins.then_inc(sig("F0_place"), 1)
            for t in range(NT):
                transpose_cw("F0", t)

            plans = plan[:].rearrange("p a (g u) -> p a g u", u=2)

            def gather(picks):
                for c in range(DC):
                    for t in range(NT):
                        ins = mm(PS[:, GB, c * P:(c + 1) * P], xn[:, t, c * P:(c + 1) * P], picks[:, t, :],
                                 start=t == 0, stop=t == NT - 1)
                return ins

            def turn_picks(bank, picks):
                for t in range(NT):
                    ins = turn(PS[:, bank, t * P:(t + 1) * P], picks[:, t, :], ident[:])
                return ins

            def gather_expert(e):
                pe.wait_ge(sig("F0_pickT"), e + 1)
                turn_picks(YB, pickT).then_inc(sig("F0_gath_ps"), 1)
                gather(pickT).then_inc(sig("F0_gath_ps"), 1)

            def hidden_units(u, tokens, name):
                for k in range(HC):
                    for c in range(DC):
                        ins = mm(PS[:, HID0 + k // 4, (k % 4) * P:(k % 4 + 1) * P],
                                 we1_ring[u][:, c, k * P:(k + 1) * P], tokens[:, c, :], start=c == 0, stop=c == DC - 1)
                    if k % 4 == 3:
                        ins.then_inc(sig(name), 1)

            def scatter(e, u):
                pe.wait_ge(sig("F0_y_hi"), e + 1)
                pe.wait_ge(sig("F0_y_lo"), e + 1)
                pe.wait_ge(sig("F0_added"), e + 1)
                for t in range(NT):
                    for part, of in enumerate((y_hi, y_lo)):
                        ins = mm(PS[:, OUT + t, :], put[:, u, t * P:(t + 1) * P], of[:], start=part == 0, stop=part == 1)
                ins.then_inc(sig("F0_scattered"), 1)

            def expert(g, u, first=False, last=False):
                e = g * 2 + u
                second = pe.value_load(plans[0:1, 0, bass.ds(g, 1), u], min_val=0, max_val=1)
                s = pe.value_load(plans[0:1, 1, bass.ds(g, 1), u], min_val=0, max_val=EXPERTS)
                pe.wait_ge(sig(f"ld_we1_slot{u}"), g * 16 + 16)
                pe.wait_ge(sig("F0_gath"), e * 2 + 2)
                if first:
                    pe.wait_ge(*at("F0", "cwT", NT))
                    pe.wait_ge(sig("w2T"), DC)
                hidden_units(u, gathT, "F0_hidden")
                if not first:
                    pe.wait_ge(sig("hotw"), e * EU + 1)
                    scatter(e - 1, (u + 1) % 2)
                else:
                    pe.wait_ge(sig("ld_be2"), 16)
                    for t in range(NT):
                        mm(PS[:, OUT + t, :], cwT[:, t * P:(t + 1) * P], be2_sb[:], start=True,
                           stop=True).then_inc(sig("out"), 1)
                if not last:
                    gather_expert(e + 1)
                    pe.wait_ge(sig("F0_gath"), e * 2 + 3)
                pe.wait_ge(sig(f"ld_we2_slot{u}"), g * 16 + 16)
                for k in range(HC):
                    pe.wait_ge(sig("F0_act"), e * HC + (k + 1))
                    ins = mm(PS[:, YB, :], hid0[:, k, :], we2_ring[u][:, k, :], start=k == 0, stop=k == HC - 1)
                ins.then_inc(sig("F0_y"), 1)
                with pe.If(second > 0):
                    pe.wait_ge(sig("second_dve"), s * 2 + 1)
                    if not last:
                        pe.wait_ge(sig("F0_gath"), e * 2 + 4)
                    turn_picks(HID0, pickT2)
                    gather(pickT2).then_inc(sig("second_pe"), 1)
                    pe.wait_ge(sig("second_act"), s * (HC + 3) + 2)
                    hidden_units(u, gathT2, "second_pe")
                    pe.wait_ge(sig("F0_y_hi"), e + 1)
                    pe.wait_ge(sig("F0_y_lo"), e + 1)
                    for k in range(HC):
                        pe.wait_ge(sig("second_act"), s * (HC + 3) + (k + 3))
                        ins = mm(PS[:, YB, :], hid0[:, k, :], we2_ring[u][:, k, :], start=k == 0, stop=k == HC - 1)
                    ins.then_inc(sig("second_pe"), 1)
                    pe.wait_ge(sig("second_act"), s * (HC + 3) + (HC + 3))
                    pe.wait_ge(sig("F0_added"), e + 1)
                    for t in range(NT):
                        ins = mm(PS[:, OUT + t, :], put2[:, t * P:(t + 1) * P], y2, start=True, stop=True)
                    ins.then_inc(sig("second_pe"), 1)
                for j in range(EU):
                    pe.wait_ge(sig("hotw"), e * EU + (j + 1))
                    for t in range(NT):
                        ins = mm(PS[:, TR + t, :], hot_sr[:, j, t * P:(t + 1) * P], hot_dw[:, j, :],
                                 start=first and j == 0, stop=last and j == EU - 1)
                    ins.then_inc(sig("hotw_used"), 1)

            gather_expert(0)
            pe.wait_ge(sig("F0_plan"), 1)
            expert(0, 0, first=True)
            expert(0, 1)
            with pe.Fori(1, EXPERTS // 2 - 1) as i:
                for u in range(2):
                    expert(i, u)
            for u in range(2):
                expert(EXPERTS // 2 - 1, u, last=u == 1)

            pe.wait_ge(sig("ld_wr1"), 16)
            pe.wait_ge(sig("F0_y_hi"), EXPERTS)
            pe.wait_ge(sig("F0_y_lo"), EXPERTS)
            for c in range(DC):
                turn(PS[:, 6, N + c * EXPERTS:N + (c + 1) * EXPERTS], wr_rows[:, c * P:(c + 1) * P],
                     ident[0:EXPERTS, 0:EXPERTS])
            for t in range(NT):
                ins = mm(PS[:, 6, 0:N], ones[:], cnt[:, t, :], start=t == 0, stop=t == NT - 1)
            ins.then_inc(sig("deg"), 1)
            pe.wait_ge(sig("wgt"), NT)
            scatter(EXPERTS - 1, 1)
            keep_warm(WARM[1], 4)
            for t in range(NT):
                for k in range(NT):
                    ins = turn(PS[:, 7, t * N + k * P:t * N + (k + 1) * P], wgt[:, k, t * P:(t + 1) * P], ident[:])
            ins.then_inc(sig("wgtT_ps"), 1)
            pe.wait_ge(*at("G1", "xn", 1))
            keep_warm(WARM[2], 4)
            pe.wait_ge(*at("G1", "xn", NT))
            aggregate(wgt)
            pe.wait_ge(*at("G1", "supT0", 1))
            pe.wait_ge(*at("G1", "supT1", 1))
            pe.wait_ge(sig("ld_w1g"), 32)
            for t in range(NT):
                project(t, of_supT, w1g)

            def small_experts(s, wr, w1, w2, b2):
                def hidden(t):
                    for k in range(DC):
                        for c in range(DC):
                            ins = mm(PS[:, HID + t, k * P:(k + 1) * P], w1[:, c, k * P:(k + 1) * P], of_xnT(c, t),
                                     start=c == 0, stop=c == DC - 1)
                    ins.then_inc(sig("hidden"), 1)

                def spread_weights(t):
                    pe.wait_ge(*at(s, "cwT", t + 1))
                    for k in range(DC):
                        ins = mm(PS[:, TR + t, k * P:(k + 1) * P], spread[:, k * P:(k + 1) * P],
                                 cwT[:, t * P:(t + 1) * P], start=True, stop=True)
                    ins.then_inc(sig("spread"), 1)

                for t in range(NT):
                    transposes(s, t)
                    xnT_ready(s, t)
                    logits(t, of_xnT, wr, DC)
                    if t == 1:
                        transpose_cw(s, 0)
                    hidden(t)
                spread_weights(0)
                transpose_cw(s, 1)
                spread_weights(1)
                for t in range(NT):
                    if b2 is not None:
                        mm(PS[:, OUT + t, :], cwT[:, t * P:(t + 1) * P], b2[:], start=True, stop=False)
                    pe.wait_ge(*at(s, "hid", t + 1))
                    project(t, of_wide, w2, first=b2 is None)

            pe.wait_ge(sig("wr1T"), 1)
            pe.wait_ge(sig("const_spread"), 3)
            small_experts("F1", wr1T, w1T, w2T, None)

            for t in range(NT):
                transposes("G2", t)
            for t in range(NT):
                xnT_ready("G2", t)
            for t in range(NT):
                for c in range(DC):
                    ins = mm(PS[:, OUT + t, 0:N], of_xnT(c, t), xnT[:, c, :], start=c == 0, stop=c == DC - 1)
                ins.then_inc(sig("G2_sim"), 1)
                if t == 0:
                    pe.wait_ge(sig("G2_norm_diag"), NT)
                    for k in range(NT):
                        ins = mm(PS[:, 5, k * P:(k + 1) * P], ones[:], norm_diag[:, k, :], start=True, stop=True)
                    ins.then_inc(sig("G2_cross_ps"), 1)

            def transpose_w3(k):
                for c in range(DC):
                    ins = turn(PS[:, 4 + k % 4, c * P:(c + 1) * P], w3_raw[:, c, k * P:(k + 1) * P], ident[:])
                ins.then_inc(sig("w3T_ps"), 1)

            pe.wait_ge(sig("ld_w3_raw"), 16)
            pe.wait_ge(sig("G2_masked"), 1)
            for k in range(4):
                transpose_w3(k)
            pe.wait_ge(sig("G2_loopT"), NT)
            graph_step(loopT, acc, OUT, "G2_const_ps", lambda k: pe.wait_ge(sig("G2_const"), k + 1))
            pe.wait_ge(sig("G2_loop"), NT)
            pe.wait_ge(sig("G2_loopTs"), NT)
            pe.wait_ge(sig("w3T"), 4)
            for t in range(NT):
                for k in range(NT):
                    ins = mm(PS[:, 4 + t, 0:N], loop[:, k, t * P:(t + 1) * P], loopTs[:, k, :], start=k == 0, stop=k == NT - 1)
                ins.then_inc(sig("G2_twoT_ps"), 1)
            pe.wait_ge(sig("G2_const2"), NT)
            pe.wait_ge(sig("G2_twoT"), NT)
            for k in range(SMOOTH_STEPS // 2):
                graph_step(twoT, (other, cur)[k % 2] if k else xn, (OUT, TR)[k % 2], "G2_two",
                           lambda j: pe.wait_ge(sig("G2_cur"), NT * (k - 1) + j + 1) if k else None)

            transposes("F2", 0)
            pe.wait_ge(*at("F2", "xn", NT))
            for c in range(DC):
                for t in range(NT):
                    ins = mm(PS[:, SMALL, c:c + 1], xn[:, t, c * P:(c + 1) * P], ones[:, 0:1], start=t == 0, stop=t == NT - 1)
            ins.then_inc(sig("F2_mean_ps"), 1)
            transposes("F2", 1)
            pe.wait_ge(sig("F2_mean"), 1)
            pe.wait_ge(sig("ld_l2"), 32)
            for c in range(DC):
                ins = mm(PS[:, SMALL, 16:16 + GATES2], meanT[:, c:c + 1].broadcast_to([P, P]), wg2[:, c, :],
                         start=c == 0, stop=c == DC - 1)
            ins.then_inc(sig("logits"), 1)
            for k in range(4, 8):
                if k == 4:
                    pe.wait_ge(*at("F2", "neg_m", 1))
                transpose_w3(k)
            for t in range(NT):
                xnT_ready("F2", t)
            for c in range(DC):
                pe.wait_ge(sig(f"ld_we_sel{c}"), 16)
                for t in range(NT):
                    ins = mm(PS[:, OUT + t, :], of_xnT(c, t), we_sel[:, c, :], start=c == 0, stop=c == DC - 1)
                    if c == DC - 1:
                        ins.then_inc(sig("out"), 1)

            pe.wait_ge(sig("w3T"), 8)
            for t in range(NT):
                transposes("G3", t)
                xnT_ready("G3", t)
                project(t, of_xnT, w3T[:, 0:4, :], more=True)
                if t == 0:
                    continue
                pe.wait_ge(sig("mean_w"), NT)
                aggregate(mean_w)
            pe.wait_ge(*at("G3", "supT0", 1))
            pe.wait_ge(*at("G3", "supT1", 1))
            for t in range(NT):
                project(t, of_supT, w3T[:, 4:8, :], first=False)

            pe.wait_ge(sig("ld_gate3"), 48)
            pe.wait_ge(sig("ld_w31"), 16 * DC)
            pe.wait_ge(sig("ld_w32"), 16)
            small_experts("F3", wr3, w31, w32, b2_sb)


_INS = ['x', 'src', 'dst', 'edge_weight', 'L0_gnn_W', 'L0_gnn_b', 'L0_gnn_diffusion_weights', 'L0_ffn_gw1',
        'L0_ffn_gb1', 'L0_ffn_gw2', 'L0_ffn_gb2', 'L0_ffn_we1', 'L0_ffn_be1', 'L0_ffn_we2', 'L0_ffn_be2',
        'L1_gnn_weight', 'L1_gnn_bias', 'L1_ffn_Wr', 'L1_ffn_W1', 'L1_ffn_W2', 'L2_gnn_alpha', 'L2_gnn_beta',
        'L2_gnn_sigma', 'L2_ffn_Wg', 'L2_ffn_bg', 'L2_ffn_We', 'L2_ffn_be', 'L3_gnn_W', 'L3_gnn_b', 'L3_ffn_Wr',
        'L3_ffn_br', 'L3_ffn_W1', 'L3_ffn_b1', 'L3_ffn_W2', 'L3_ffn_b2']


def kernel(**inputs):
    import numpy as _np
    import concourse.bacc as _bacc
    from concourse import mybir as _mybir
    from concourse.bass_utils import run_bass_kernel_spmd as _run

    nc = _bacc.Bacc("TRN2", target_bir_lowering=False, num_devices=1)
    arrays, args = {}, []
    for name in _INS:
        a = _np.ascontiguousarray(inputs[name])
        arrays[f"in_{name}_dram"] = a
        args.append(nc.dram_tensor(f"in_{name}_dram", a.shape, _mybir.dt.from_np(a.dtype), kind="ExternalInput").ap())
    args.append(nc.dram_tensor("out_dram", (N, D), F32, kind="ExternalOutput").ap())
    build(nc, *args)
    r = _run(nc, [arrays], core_ids=[0])
    return r.results[0]["out_dram"]
```

```python
from contextlib import ExitStack

import concourse.bass as bass
from concourse import mybir

ALU = mybir.AluOpType
ACT = mybir.ActivationFunctionType
F32 = mybir.dt.float32
F32R = mybir.dt.float32r
BF16 = mybir.dt.bfloat16
I32 = mybir.dt.int32
U32 = mybir.dt.uint32
AX_X = mybir.AxisListType.X

P = 128
N = 256
NT = N // P
D = 512
DC = D // P
EDGES = 4096
EC = EDGES // P
EU = 4
HU = 8
EXPERTS = 8
H0 = 1024
HC = H0 // P
PIECES = HC // 2
LN_EPS = 1e-5
NORM_FLOOR = 1e-12
DIFFUSION_STEPS = 3
SMOOTH_STEPS = 10
GATES2 = 16


def build(nc, x, src, dst, edge_weight, L0_gnn_W, L0_gnn_b, L0_gnn_diffusion_weights, L0_ffn_gw1, L0_ffn_gb1,
          L0_ffn_gw2, L0_ffn_gb2, L0_ffn_we1, L0_ffn_be1, L0_ffn_we2, L0_ffn_be2, L1_gnn_weight, L1_gnn_bias,
          L1_ffn_Wr, L1_ffn_W1, L1_ffn_W2, L2_gnn_alpha, L2_gnn_beta, L2_gnn_sigma, L2_ffn_Wg, L2_ffn_bg,
          L2_ffn_We, L2_ffn_be, L3_gnn_W, L3_gnn_b, L3_ffn_Wr, L3_ffn_br, L3_ffn_W1, L3_ffn_b1, L3_ffn_W2,
          L3_ffn_b2, out):
    with ExitStack() as ctx:
        def sb(name, shape, dt=F32):
            return ctx.enter_context(nc.sbuf_tensor(name, shape, dt))

        sems = {}

        def sig(name):
            if name not in sems:
                sems[name] = ctx.enter_context(nc.semaphore(name))
            return sems[name]

        every = ("G0", "F0", "G1", "F1", "G2", "F2", "G3", "F3")
        turned = tuple(s for s in every if s != "G1")
        routed = ("F0", "F1", "F3")
        GIVEN = {
            "var": dict.fromkeys(every, NT), "rstd": dict.fromkeys(every, NT), "xn": dict.fromkeys(every, NT),
            "xT": dict.fromkeys(turned, NT), "xnT": dict.fromkeys(turned, NT),
            "logits": {"F0": NT, "F1": NT, "F2": 1, "F3": NT}, "neg_m": {"F0": NT, "F1": NT, "F2": 1, "F3": NT},
            "exp": {"F0": NT, "F1": NT, "F2": 1, "F3": NT}, "cw": dict.fromkeys(routed, NT),
            "cwT_ps": dict.fromkeys(routed, NT), "cwT": dict.fromkeys(routed, NT),
            "out": dict.fromkeys(("F0", "G1", "F1", "F2", "G3", "F3"), NT),
            "hidden": {"F1": NT, "F3": NT}, "act": {"F1": NT, "F3": NT}, "hid": {"F1": NT, "F3": NT},
            "spread": {"F1": NT, "F3": NT}, "supT_ps": {"G1": 2, "G3": 2}, "supT0": {"G1": 1, "G3": 1},
            "supT1": {"G1": 1, "G3": 1},
        }

        def at(stage, name, n):
            given = GIVEN[name]
            return sig(name), n + sum(k for s, k in given.items() if every.index(s) < every.index(stage))

        with ExitStack() as outside_experts:
            def early(name, shape):
                return outside_experts.enter_context(nc.sbuf_tensor(name, shape, F32))

            w0 = early("w0", [P, DC, D])
            w1_raw = early("w1_raw", [P, DC, D])
            loopT = early("loopT", [P, NT, N])
            loop = early("loop", [P, NT, N])
            loopTs = early("loopTs", [P, NT, N])
            twoT = early("twoT", [P, NT, N])
            supT = early("supT", [P, DC, N])
            wgtT = early("wgtT", [P, NT, N])
            sup = early("sup", [P, NT, N])
        w2_hi = sb("w2_hi", [P, PIECES, D], F32R)
        w2_lo = sb("w2_lo", [P, PIECES, D], F32R)
        hid_hi = sb("hid_hi", [P, HC, P], F32R)
        hid_lo = sb("hid_lo", [P, HC, P], F32R)
        xn_hi = sb("xn_hi", [P, NT, D], F32R)
        xn_lo = sb("xn_lo", [P, NT, D], F32R)

        X = sb("X", [P, NT, D])
        xn = sb("xn", [P, NT, D])
        xnT = sb("xnT", [P, DC, N])
        wide = sb("wide", [P, HC, N])
        halves = wide[:].rearrange("p k n -> p (k n)").rearrange("p (h t d) -> p h t d", h=2, t=NT)
        hid0 = wide[:, 0:HC // 2, :].rearrange("p k (h n) -> p (k h) n", n=P)
        spare = halves[:, 0]
        other = halves[:, 1]
        cur = sb("cur", [P, NT, D])
        acc = sb("acc", [P, NT, D])
        gathT = other.rearrange("p t (c u n) -> p (t c) u n", c=2, u=2)
        gathT2 = cur[:, 1, :].rearrange("p (c n) -> p c n", c=DC)
        pickT = sb("pickT", [P, NT, 2, P], F32R)
        pickT2 = acc[:, 1, 0:N].rearrange("p (t n) -> p t n", t=NT)
        put2 = acc[:, 0, N:2 * N]
        y2 = cur[:, 0, :]
        touched, touched2 = acc[:, 1, N:N + 8], acc[:, 1, N + 8:N + 16]
        put = sb("put", [P, 2, N], F32R)
        be1_now = sb("be1_now", [P, HC])
        y_hi = sb("y_hi", [P, D], F32R)
        y_lo = sb("y_lo", [P, D], F32R)
        bn = sb("bn", [P, NT, 6])
        mv = sb("mv", [P, NT, 2])
        rstd = sb("rstd", [P, NT])
        neg_half = sb("neg_half", [P, NT])

        ident = sb("ident", [P, P])
        ones = sb("ones", [P, P])
        iota = sb("iota", [P, N], BF16)
        upto = sb("upto", [P, P], BF16)
        ones_b = sb("ones_b", [P, P], BF16)
        iota8 = sb("iota8", [P, EXPERTS])
        spread = sb("spread", [EXPERTS, D])

        edge_i = sb("edge_i", [P, 2, EC], I32)
        edge_f = sb("edge_f", [P, 2, EC])
        ew = sb("ew", [P, EC])
        ew_hi = sb("ew_hi", [P, EC], F32R)
        ew_lo = sb("ew_lo", [P, EC])
        hot_sr = sb("hot_sr", [P, EU, N], F32R)
        hot_dw = sb("hot_dw", [P, EU, 2 * N], F32R)
        cnt = sb("cnt", [P, NT, N])
        adj = sb("adj", [P, NT, N])
        adj_sum = sb("adj_sum", [P, NT])
        adj_inv = sb("adj_inv", [P, NT])
        wgt = sb("wgt", [P, NT, N])
        mean_w = sb("mean_w", [P, NT, N])
        deg_inv = sb("deg_inv", [P, N])

        diff_w = sb("diff_w", [P, DIFFUSION_STEPS + 1])
        bias_rows = sb("bias_rows", [70, P])
        bias_cols = sb("bias_cols", [P, 70])
        gb2_b = sb("gb2_b", [P, EXPERTS])
        br_b = sb("br_b", [P, EXPERTS])
        bg_b = sb("bg_b", [P, GATES2])
        be2_sb = sb("be2_sb", [EXPERTS, D])
        b2_sb = sb("b2_sb", [EXPERTS, D])
        b0_b = sb("b0_b", [P, D])
        b1_b = sb("b1_b", [P, D])
        b3_b = sb("b3_b", [P, D])
        be_sel = sb("be_sel", [P, D])
        wr_rows = sb("wr_rows", [EXPERTS, D])
        wr1T = sb("wr1T", [P, DC, EXPERTS])
        wr3 = sb("wr3", [P, DC, EXPERTS])
        gw2 = sb("gw2", [P, NT, EXPERTS])
        wg2 = sb("wg2", [P, DC, GATES2])
        abs_b = sb("abs_b", [P, 3])

        lg = sb("lg", [P, NT, GATES2])
        mx = sb("mx", [P, NT, 8])
        neg_m = sb("neg_m", [P, NT])
        ex = sb("ex", [P, NT, GATES2])
        sm = sb("sm", [P, NT])
        rs = sb("rs", [P, NT])
        sw = sb("sw", [P, NT, EXPERTS])
        m2 = sb("m2", [P, NT, 8])
        ix = sb("ix", [P, NT, 8], U32)
        ixf = sb("ixf", [P, NT, 2])
        pw = sb("pw", [P, NT, 2])
        gap = sb("gap", [P, NT])
        cwa = sb("cwa", [P, NT, EXPERTS])
        cwb = sb("cwb", [P, NT, EXPERTS])
        cw = sb("cw", [P, NT, EXPERTS])
        cwT = sb("cwT", [EXPERTS, N])
        chosen = sb("chosen", [P, NT, EXPERTS], BF16)
        slot = sb("slot", [P, NT, EXPERTS])
        before = sb("before", [P, 4, 4 + EXPERTS])
        plan = sb("plan", [P, 2, EXPERTS], I32)

        off_diag = sb("off_diag", [P, NT, N])
        norm_diag = sb("norm_diag", [P, NT, P])
        cross = supT[:, 0:2, :]
        sim = supT[:, 2:4, :]
        scaled, scaled2, poly = loop, loopT, twoT
        sc = sb("sc", [P, 16])
        norm = sb("norm", [P, NT])
        r2 = sb("r2", [P, NT])
        rb = sb("rb", [P, NT])
        meanT = sb("meanT", [P, DC])
        pick = sb("pick", [P, 8], U32)

        gw1 = sb("gw1", [P, DC, N])
        w1g = sb("w1g", [P, DC, D])
        w1T = sb("w1T", [P, DC, D])
        w2T = sb("w2T", [P, DC, D])
        ring = sb("ring", [P, 2, 2, 4096])

        we1_ring = [ring[:, u, 0, :].rearrange("p (c n) -> p c n", c=DC) for u in range(2)]
        we2_ring = [ring[:, u, 1, :].rearrange("p (k n) -> p k n", k=HC) for u in range(2)]

        w2_raw = w0
        hots = ring[:, 1, :, :].bitcast(BF16).rearrange("p m (j n) -> p m j n", n=N)
        hot_s, hot_d = hots[:, 0], hots[:, 1]
        w3_raw = ring[:, 0, 0, :].rearrange("p (c n) -> p c n", c=DC)
        w3T = ring[:, 0, 1, :].rearrange("p (k n) -> p k n", k=8)
        we_sel = ring[:, 1, 0, 0:2048].rearrange("p (c n) -> p c n", c=DC)
        w31 = ring[:, 1, 0, 2048:4096].rearrange("p (c n) -> p c n", c=DC)
        w32 = ring[:, 1, 1, 0:2048].rearrange("p (c n) -> p c n", c=DC)

        PS = ctx.enter_context(nc.psum_tensor("PS", [P, 8, 512], F32))
        WARM = {'F2d': 11, 'F0c': 8, 'F0a': 2, 'F0b': 4, 'G0': 8, 'G1a': 13, 'cwT': 5, 'G2a': 12, 'G2b': 8, 'F2a': 6, 'F2b': 7, 'G3': 2}
        TR, OUT, SMALL, HID0, HID = 0, 2, 4, 4, 6
        YB, GB = 6, 7

        block = ctx.enter_context(nc.Block())

        @block.sync
        def _(sp):
            def load(to, of, name):
                sp.dma_start(to, of).then_inc(sig(name), 16)

            def load_expert(e, u):
                load(we1_ring[u], L0_ffn_we1[bass.ds(e, 1)].rearrange("a (c p) n -> p (a c) n", p=P), f"ld_we1_slot{u}")
                load(we2_ring[u], L0_ffn_we2[bass.ds(e, 1)].rearrange("a (k p) n -> p (a k) n", p=P), f"ld_we2_slot{u}")

            load(edge_i[:, 0, :], src.rearrange("(p j) -> p j", p=P), "ld_edges")
            load(edge_i[:, 1, :], dst.rearrange("(p j) -> p j", p=P), "ld_edges")
            load(X[:], x.rearrange("(t p) d -> p t d", p=P), "ld_x")
            load(w0[:], L0_gnn_W.rearrange("(c p) n -> p c n", p=P), "ld_w0")
            load(b0_b[:], L0_gnn_b.partition_broadcast(P), "ld_b0")
            load(diff_w[:], L0_gnn_diffusion_weights.partition_broadcast(P), "ld_b0")
            load(bias_rows[0:64, :], L0_ffn_be1.rearrange("e (k p) -> (e k) p", p=P), "ld_bias_rows")
            load(bias_rows[64:66, :], L0_ffn_gb1.rearrange("(k p) -> k p", p=P), "ld_bias_rows")
            load(bias_rows[66:70, :], L3_ffn_b1.rearrange("(a e) f -> a (e f)", a=4), "ld_bias_rows")
            load(gw1[:], L0_ffn_gw1.rearrange("(c p) n -> p c n", p=P), "ld_gate0")
            load(gw2[:], L0_ffn_gw2.rearrange("(c p) n -> p c n", p=P), "ld_gate0")
            load(gb2_b[:], L0_ffn_gb2.partition_broadcast(P), "ld_gate0")
            load(be2_sb[:], L0_ffn_be2, "ld_be2")
            load(ew[:], edge_weight.rearrange("(p j) -> p j", p=P), "ld_ew")
            load_expert(0, 0)
            load(w1_raw[:], L1_ffn_W1.rearrange("e f d -> (e f) d").rearrange("(c p) d -> p c d", p=P), "ld_w1_raw")
            load(w1g[:], L1_gnn_weight.rearrange("(c p) n -> p c n", p=P), "ld_w1g")
            load(b1_b[:], L1_gnn_bias.partition_broadcast(P), "ld_w1g")
            load(wr_rows[:], L1_ffn_Wr, "ld_wr1")
            load(wg2[:], L2_ffn_Wg.rearrange("(c p) n -> p c n", p=P), "ld_l2")
            load(bg_b[:], L2_ffn_bg.partition_broadcast(P), "ld_l2")
            load(abs_b[:, 0:1], L2_gnn_alpha.partition_broadcast(P), "ld_abs")
            load(abs_b[:, 1:2], L2_gnn_beta.partition_broadcast(P), "ld_abs")
            load(abs_b[:, 2:3], L2_gnn_sigma.partition_broadcast(P), "ld_abs")
            load(b3_b[:], L3_gnn_b.partition_broadcast(P), "ld_b3")
            load(wr3[:], L3_ffn_Wr.rearrange("(c p) n -> p c n", p=P), "ld_gate3")
            load(br_b[:], L3_ffn_br.partition_broadcast(P), "ld_gate3")
            load(b2_sb[:], L3_ffn_b2, "ld_gate3")
            sp.wait_ge(sig("G0_h"), NT)
            for c in range(DC):
                load(w2_raw[:, c, :].rearrange("p (e f) -> p e f", e=EXPERTS),
                     L1_ffn_W2[:, c * P:(c + 1) * P, :].rearrange("e p f -> p e f"), "ld_w2_raw")
            sp.wait_ge(sig("counted"), 1)
            load_expert(1, 1)
            with sp.Fori(1, EXPERTS // 2) as g:
                for u in range(2):
                    sp.wait_ge(sig("hotw_used"), g * 2 * EU + (u - 1) * EU)
                    load(we1_ring[u], L0_ffn_we1.rearrange("(g u) (c p) n -> g u p c n", u=2, p=P)
                         [bass.ds(g, 1), u].rearrange("g p c n -> p (g c) n"), f"ld_we1_slot{u}")
                    load(we2_ring[u], L0_ffn_we2.rearrange("(g u) (k p) n -> g u p k n", u=2, p=P)
                         [bass.ds(g, 1), u].rearrange("g p k n -> p (g k) n"), f"ld_we2_slot{u}")
            sp.wait_ge(sig("hotw_used"), (EXPERTS - 1) * EU)
            load(w3_raw, L3_gnn_W.rearrange("(c p) n -> p c n", p=P), "ld_w3_raw")
            sp.wait_ge(sig("hotw_used"), EXPERTS * EU)
            for c in range(DC):
                load(w31[:, c, :].rearrange("p (e f) -> p e f", e=EXPERTS),
                     L3_ffn_W1[:, c * P:(c + 1) * P, :].rearrange("e p f -> p e f"), "ld_w31")
            load(w32, L3_ffn_W2.rearrange("e f d -> (e f) d").rearrange("(c p) d -> p c d", p=P), "ld_w32")
            sp.wait_ge(sig("F2_pick"), 1)
            e = sp.value_load(pick[0:1, 0:1], min_val=0, max_val=GATES2 - 1)
            for c in range(DC):
                load(we_sel[:, c, :], L2_ffn_We[bass.ds(e, 1), c * P:(c + 1) * P, :].rearrange("a p n -> (a p) n"),
                     f"ld_we_sel{c}")
            load(be_sel[:], L2_ffn_be[bass.ds(e, 1)].rearrange("a n -> (a n)").partition_broadcast(P), "ld_be_sel")
            for t in range(NT):
                sp.wait_ge(sig("X_final"), t + 1)
                sp.dma_start(out[t * P:(t + 1) * P, :], X[:, t, :]).then_inc(sig("stored"), 16)
            sp.wait_ge(sig("stored"), 16 * NT)

        @block.gpsimd
        def _(pool):
            g = nc.gpsimd
            g.iota(iota[:], [[1, N]], base=0, channel_multiplier=0,
                   allow_small_or_imprecise_dtypes=True).then_inc(sig("const_iota"), 1)
            g.memset(ident[:], 0.0).then_inc(sig("pool_fill"), 1)
            g.memset(ones[:], 1.0).then_inc(sig("pool_fill"), 1)
            g.memset(neg_half[:], -0.5).then_inc(sig("pool_fill"), 1)
            pool.wait_ge(sig("pool_fill"), 3)
            g.affine_select(out=ident[:], in_=ident[:], compare_op=ALU.not_equal, fill=1.0, base=0,
                            pattern=[[-1, P]], channel_multiplier=1).then_inc(sig("const_ident"), 1)

            def inverse_std(s):
                for t in range(NT):
                    pool.wait_ge(*at(s, "var", t + 1))
                    g.tensor_scalar(rstd[:, t:t + 1], mv[:, t, 1:2], LN_EPS, None, ALU.add).then_inc(sig("var_eps"), 1)
                    pool.wait_ge(sig("var_eps"), NT * every.index(s) + t + 1)
                    g.tensor_tensor(rstd[:, t:t + 1], rstd[:, t:t + 1], neg_half[:, t:t + 1],
                                    ALU.pow).then_inc(sig("rstd"), 1)

            inverse_std("G0")
            g.iota(iota8[:], [[1, EXPERTS]], base=0, channel_multiplier=0,
                   allow_small_or_imprecise_dtypes=True).then_inc(sig("const_iota"), 1)
            g.memset(ones_b[:], 1.0).then_inc(sig("const_upto"), 1)
            g.memset(before[:], 0.0).then_inc(sig("const_upto"), 1)
            pool.wait_ge(sig("const_upto"), 1)
            g.affine_select(out=upto[:], in_=ones_b[:], compare_op=ALU.is_ge, fill=0.0, base=0,
                            pattern=[[1, P]], channel_multiplier=-1).then_inc(sig("const_upto"), 1)
            g.memset(spread[:], 1.0).then_inc(sig("const_spread"), 1)
            g.memset(off_diag[:], 1.0).then_inc(sig("const_mask"), 1)
            pool.wait_ge(sig("const_spread"), 1)
            g.affine_select(out=spread[:], in_=spread[:], compare_op=ALU.is_ge, fill=0.0, base=0,
                            pattern=[[1, D]], channel_multiplier=-64).then_inc(sig("const_spread"), 1)
            pool.wait_ge(sig("const_spread"), 2)
            g.affine_select(out=spread[:], in_=spread[:], compare_op=ALU.is_ge, fill=0.0, base=63,
                            pattern=[[-1, D]], channel_multiplier=64).then_inc(sig("const_spread"), 1)
            pool.wait_ge(sig("const_mask"), 1)
            for t in range(NT):
                g.affine_select(out=off_diag[:, t, :], in_=off_diag[:, t, :], compare_op=ALU.not_equal, fill=0.0,
                                base=t * P, pattern=[[-1, N]], channel_multiplier=1).then_inc(sig("const_mask"), 1)

            inverse_std("F0")
            for t in range(NT):
                pool.wait_ge(sig("F0_parts"), 1 + 2 * t)
                g.tensor_tensor(xn_lo[:, t, :], xn[:, t, :], xn_hi[:, t, :].bitcast(F32),
                                ALU.subtract).then_inc(sig("F0_parts"), 1)
            for s in ("G1", "F1", "G2"):
                inverse_std(s)
            pool.wait_ge(sig("G2_sumsq"), NT)
            g.tensor_scalar(rs[:], sm[:], NORM_FLOOR, None, ALU.max).then_inc(sig("G2_floored"), 1)
            pool.wait_ge(sig("G2_floored"), 1)
            g.tensor_tensor(rs[:], rs[:], neg_half[:], ALU.pow).then_inc(sig("G2_rnorm"), 1)
            for s in ("F2", "G3", "F3"):
                inverse_std(s)

        @block.vector
        def _(dve):
            v = nc.vector
            own = [0]

            def done(ins):
                own[0] += 1
                ins.then_inc(sig("dve_own"), 1)
                dve.wait_ge(sig("dve_own"), own[0])

            def row_stats(t):
                done(v.bn_stats(bn[:, t, :], X[:, t, :]))
                v.bn_aggr(mv[:, t, :], bn[:, t, :]).then_inc(sig("var"), 1)

            def normalise(s, t):
                dve.wait_ge(*at(s, "rstd", t + 1))
                v.tensor_scalar(xn[:, t, :], X[:, t, :], mv[:, t, 0:1], rstd[:, t:t + 1],
                                ALU.subtract, ALU.mult).then_inc(sig("xn"), 1)

            def norm_tile(s, t):
                row_stats(t)
                normalise(s, t)

            def choose(s, t, bias, softmax_of_two):
                dve.wait_ge(*at(s, "logits", t + 1))
                of = PS[:, SMALL + t, 0:EXPERTS]
                if bias is None:
                    done(v.tensor_copy(lg[:, t, 0:EXPERTS], of))
                else:
                    done(v.tensor_tensor(lg[:, t, 0:EXPERTS], of, bias[:], ALU.add))
                done(v.max(mx[:, t, :], lg[:, t, 0:EXPERTS]))
                v.tensor_scalar(neg_m[:, t:t + 1], mx[:, t, 0:1], -1.0, None, ALU.mult).then_inc(sig("neg_m"), 1)
                dve.wait_ge(*at(s, "exp", t + 1))
                done(v.reciprocal(rs[:, t:t + 1], sm[:, t:t + 1]))
                done(v.tensor_scalar(sw[:, t, :], ex[:, t, 0:EXPERTS], rs[:, t:t + 1], None, ALU.mult))
                done(v.max(m2[:, t, :], sw[:, t, :]))
                if softmax_of_two:
                    v.tensor_tensor(gap[:, t:t + 1], m2[:, t, 1:2], m2[:, t, 0:1],
                                    ALU.subtract).then_inc(sig("F0_gap"), 1)
                done(v.max_index(ix[:, t, :], m2[:, t, :], sw[:, t, :]))
                done(v.tensor_copy(ixf[:, t, :], ix[:, t, 0:2]))
                if softmax_of_two:
                    done(v.tensor_scalar(chosen[:, t, :], iota8[:], ixf[:, t, 0:1], None, ALU.is_equal))
                    v.scalar_tensor_tensor(chosen[:, t, :], in0=iota8[:], scalar=ixf[:, t, 1:2], in1=chosen[:, t, :],
                                           op0=ALU.is_equal, op1=ALU.add).then_inc(sig("F0_chosen"), 1)

            def weigh(t, softmax_of_two):
                if softmax_of_two:
                    dve.wait_ge(sig("F0_gap_exp"), t + 1)
                    done(v.tensor_scalar(pw[:, t, 0:1], gap[:, t:t + 1], 1.0, None, ALU.add))
                    done(v.reciprocal(pw[:, t, 0:1], pw[:, t, 0:1]))
                    done(v.tensor_tensor(pw[:, t, 1:2], pw[:, t, 0:1], gap[:, t:t + 1], ALU.mult))
                    weight = pw
                else:
                    weight = m2
                v.tensor_scalar(cwa[:, t, :], iota8[:], ixf[:, t, 0:1], weight[:, t, 0:1], ALU.is_equal, ALU.mult)
                done(v.tensor_scalar(cwb[:, t, :], iota8[:], ixf[:, t, 1:2], weight[:, t, 1:2],
                                     ALU.is_equal, ALU.mult))
                v.tensor_tensor(cw[:, t, :], cwa[:, t, :], cwb[:, t, :], ALU.add).then_inc(sig("cw"), 1)

            def top2(s, t, bias):
                choose(s, t, bias, False)
                weigh(t, False)

            def take_cwT(s, t, bank=SMALL):
                dve.wait_ge(*at(s, "cwT_ps", t + 1))
                v.tensor_copy(cwT[:, t * P:(t + 1) * P], PS[0:EXPERTS, bank + t, 0:P]).then_inc(sig("cwT"), 1)

            def take_support(s, bank=TR):
                dve.wait_ge(*at(s, "supT_ps", 1))
                v.tensor_copy(supT[:, 0:2, :], PS[:, bank, :]).then_inc(sig("supT0"), 1)

            dve.wait_ge(sig("ld_edges"), 32)
            dve.wait_ge(sig("const_iota"), 1)
            done(v.tensor_copy(edge_f[:], edge_i[:]))
            ends8 = edge_f[:].rearrange("p s (g u) -> p s g u", u=HU)
            hot_s8 = hot_s.rearrange("p (g u) n -> p g u n", u=HU)
            hot_d8 = hot_d.rearrange("p (g u) n -> p g u n", u=HU)

            def one_hots(i):
                for u in range(HU):
                    v.tensor_scalar(hot_s8[:, bass.ds(i, 1), u], iota[:], ends8[:, 0, bass.ds(i, 1), u], None,
                                    ALU.is_equal)
                    v.tensor_scalar(hot_d8[:, bass.ds(i, 1), u], iota[:], ends8[:, 1, bass.ds(i, 1), u], None,
                                    ALU.is_equal).then_inc(sig("hot"), 1)

            one_hots(0)
            dve.wait_ge(sig("ld_x"), 16)
            for t in range(NT):
                row_stats(t)
            for t in range(NT):
                normalise("G0", t)
            with dve.Fori(1, EC // HU) as i:
                one_hots(i)
            dve.wait_ge(sig("ld_b0"), 32)

            def take_h(t):
                dve.wait_ge(sig("G0_h"), t + 1)
                v.tensor_tensor(cur[:, t, :], PS[:, OUT + t, :], b0_b[:], ALU.add).then_inc(sig("G0_cur"), 1)

            take_h(0)
            dve.wait_ge(sig("counted"), 1)
            for t in range(NT):
                v.tensor_copy(cnt[:, t, :], PS[:, 4 + t, 0:N]).then_inc(sig("cnt"), 1)
            dve.wait_ge(sig("cntT"), 1)
            for t in range(NT):
                ins = v.tensor_tensor(adj[:, t, :], cnt[:, t, :], PS[:, 6 + t, 0:N], ALU.add)
            done(ins)
            for t in range(NT):
                ins = v.tensor_scalar(adj[:, t, :], adj[:, t, :], 1.0, 0.0, ALU.min, ALU.add,
                                      accum_out=adj_sum[:, t:t + 1])
            done(ins)
            for t in range(NT):
                v.tensor_tensor(adj[:, t, t * P:(t + 1) * P], adj[:, t, t * P:(t + 1) * P], ident[:],
                                ALU.add).then_inc(sig("adj"), 1)
            done(v.tensor_scalar(adj_inv[:], adj_sum[:], 1.0, 1.0, ALU.add, ALU.max))
            done(v.reciprocal(adj_inv[:], adj_inv[:]))
            for t in range(NT):
                v.tensor_scalar(scaled[:, t, :], adj[:, t, :], adj_inv[:, t:t + 1], None, ALU.mult).then_inc(sig("G0_scaled"), 1)
            take_h(1)
            dve.wait_ge(sig("G0_cur"), NT)
            for t in range(NT):
                v.tensor_scalar(acc[:, t, :], cur[:, t, :], diff_w[:, 0:1], None, ALU.mult)
                ins = v.tensor_scalar(poly[:, t, :], adj[:, t, :], diff_w[:, 1:2], None, ALU.mult)
            done(ins)
            for k in range(2, DIFFUSION_STEPS + 1):
                for t in range(NT):
                    dve.wait_ge(sig("G0_power"), NT * (k - 2) + t + 1)
                    power = PS[:, (TR, HID)[k % 2] + t, 0:N]
                    if k < DIFFUSION_STEPS:
                        v.tensor_scalar((scaled, scaled2)[(k - 1) % 2][:, t, :], power, adj_inv[:, t:t + 1], None,
                                        ALU.mult).then_inc(sig("G0_scaled"), 1)
                for t in range(NT):
                    ins = v.scalar_tensor_tensor(poly[:, t, :], in0=PS[:, (TR, HID)[k % 2] + t, 0:N],
                                                 scalar=diff_w[:, k:k + 1], in1=poly[:, t, :], op0=ALU.mult, op1=ALU.add)
                    if k == DIFFUSION_STEPS:
                        ins.then_inc(sig("G0_poly"), 1)
                if k < DIFFUSION_STEPS:
                    done(ins)
            dve.wait_ge(sig("bias_ps"), 1)
            v.tensor_copy(bias_cols[:], PS[:, 4, 0:70]).then_inc(sig("bias_cols"), 1)
            for t in range(NT):
                dve.wait_ge(sig("G0_step"), t + 1)
                done(v.scalar_tensor_tensor(acc[:, t, :], in0=PS[:, OUT + t, :], scalar=adj_inv[:, t:t + 1],
                                            in1=acc[:, t, :], op0=ALU.mult, op1=ALU.add))
                if t:
                    normalise("F0", t - 1)
                done(v.scalar_tensor_tensor(X[:, t, :], in0=acc[:, t, :], scalar=0.0, in1=X[:, t, :],
                                            op0=ALU.max, op1=ALU.add))
                row_stats(t)
            normalise("F0", NT - 1)

            dve.wait_ge(sig("ld_gate0"), 48)
            dve.wait_ge(sig("const_iota"), 2)
            for t in range(NT):
                choose("F0", t, gb2_b, True)
            dve.wait_ge(sig("F0_place"), 1)
            place = PS[:, GB, 0:NT * EXPERTS].rearrange("p (t e) -> p t e", t=NT)
            done(v.tensor_tensor(slot[:], place, chosen[:], ALU.mult))
            v.tensor_scalar(before[:, 0, 4:4 + EXPERTS], PS[:, GB, 2 * EXPERTS:3 * EXPERTS], float(P), None, ALU.is_gt)
            done(v.tensor_scalar(slot[:], slot[:], -1.0, None, ALU.add))

            slots = slot[:].rearrange("p t (g u) -> p t g u", u=2)

            def pick_tokens(g):
                for t in range(NT):
                    for u in range(2):
                        ins = v.tensor_scalar(pickT[:, t, u, :], iota[:, 0:P], slots[:, t, bass.ds(g, 1), u], None,
                                              ALU.is_equal)
                ins.then_inc(sig("F0_pickT"), 1)

            pick_tokens(0)
            v.tensor_copy(plan[:, 0, :], before[:, 0, 4:4 + EXPERTS])
            done(v.tensor_tensor(before[:, 1, 4:4 + EXPERTS], before[:, 0, 3:3 + EXPERTS],
                                 before[:, 0, 2:2 + EXPERTS], ALU.add))
            for k in range(1, 3):
                done(v.tensor_tensor(before[:, k + 1, 4:4 + EXPERTS], before[:, k, 4:4 + EXPERTS],
                                     before[:, k, 4 - 2 ** k:4 - 2 ** k + EXPERTS], ALU.add))
            v.tensor_copy(plan[:, 1, :], before[:, 3, 4:4 + EXPERTS]).then_inc(sig("F0_plan"), 1)
            for t in range(NT):
                weigh(t, True)
            dve.wait_ge(sig("ld_ew"), 16)
            done(v.tensor_copy(ew_hi[:], ew[:]))
            done(v.tensor_tensor(ew_lo[:], ew[:], ew_hi[:].bitcast(F32), ALU.subtract))
            ends = edge_f[:].rearrange("p s (g u) -> p s g u", u=EU)
            hi = ew_hi[:].bitcast(F32).rearrange("p (g u) -> p g u", u=EU)
            lo = ew_lo[:].rearrange("p (g u) -> p g u", u=EU)

            def weighted(g):
                for u in range(EU):
                    v.tensor_scalar(hot_sr[:, u, :], iota[:], ends[:, 0, bass.ds(g, 1), u], None, ALU.is_equal)
                    v.tensor_scalar(hot_dw[:, u, 0:N], iota[:], ends[:, 1, bass.ds(g, 1), u],
                                    hi[:, bass.ds(g, 1), u], ALU.is_equal, ALU.mult)
                    v.tensor_scalar(hot_dw[:, u, N:2 * N], iota[:], ends[:, 1, bass.ds(g, 1), u],
                                    lo[:, bass.ds(g, 1), u], ALU.is_equal, ALU.mult).then_inc(sig("hotw"), 1)

            weighted(0)

            dve.wait_ge(sig("F0_plan"), 1)

            def add_block(e):
                for t in range(NT):
                    ins = v.scalar_tensor_tensor(X[:, t, :], in0=PS[:, OUT + t, :], scalar=cw[:, t, bass.ds(e, 1)],
                                                 in1=X[:, t, :], op0=ALU.mult, op1=ALU.add)
                return ins

            def add_expert(e):
                dve.wait_ge(sig("F0_scattered"), e + 1)
                dve.wait_ge(sig("F0_added"), e + 1)
                add_block(e).then_inc(sig("F0_added"), 1)

            def weights_lo(u, k, e):
                dve.wait_ge(sig("F0_w2_hi"), e * HC + (k + 1))
                v.tensor_tensor(w2_lo[:, k % PIECES, :], we2_ring[u][:, k, :], w2_hi[:, k % PIECES, :].bitcast(F32),
                                ALU.subtract).then_inc(sig("F0_w2_lo"), 1)

            def hidden_lo(h, e):
                dve.wait_ge(sig("F0_hid_hi"), e * 2 + (h + 1))
                half = slice(h * HC // 2, (h + 1) * HC // 2)
                v.tensor_tensor(hid_lo[:, half, :], hid0[:, half, :], hid_hi[:, half, :].bitcast(F32),
                                ALU.subtract).then_inc(sig("F0_hid_lo"), 1)

            def expert(g, u, first=False, last=False):
                e = g * 2 + u
                second = dve.value_load(plan[0:1, 0, bass.ds(e, 1)], min_val=0, max_val=1)
                s = dve.value_load(plan[0:1, 1, bass.ds(e, 1)], min_val=0, max_val=EXPERTS)
                if u == 1 and not last:
                    dve.wait_ge(sig("F0_turned"), e + 1)
                    pick_tokens(g + 1)
                for k in range(PIECES):
                    weights_lo(u, k, e)
                hidden_lo(0, e)
                if not first:
                    add_expert(e - 1)
                else:
                    for t in range(NT):
                        take_cwT("F0", t, OUT)
                    hidden_lo(1, e)
                    for t in range(NT):
                        dve.wait_ge(*at("F0", "out", t + 1))
                        ins = v.tensor_tensor(X[:, t, :], PS[:, OUT + t, :], X[:, t, :], ALU.add)
                    ins.then_inc(sig("F0_added"), 1)
                if not first:
                    hidden_lo(1, e)
                for k in range(PIECES, HC):
                    weights_lo(u, k, e)
                dve.wait_ge(sig("F0_w2_used"), e * HC + HC)
                dve.wait_ge(sig("F0_y_hi"), e + 1)
                v.tensor_tensor(y_lo[:], PS[:, YB, :], y_hi[:].bitcast(F32), ALU.subtract).then_inc(sig("F0_y_lo"), 1)
                with dve.If(second > 0):
                    for t in range(NT):
                        ins = v.tensor_scalar(pickT2[:, t, :], iota[:, P:2 * P], slot[:, t, bass.ds(e, 1)], None,
                                              ALU.is_equal)
                    ins.then_inc(sig("second_dve"), 1)
                    dve.wait_ge(sig("second_pe"), s * 5 + 5)
                    dve.wait_ge(sig("F0_added"), e + 1)
                    add_block(e).then_inc(sig("second_dve"), 1)
                    dve.wait_ge(sig("second_dve"), s * 2 + 2)
                    v.memset(touched, 0.0)
                if not last:
                    dve.wait_ge(sig("hotw_used"), e * EU + EU)
                    weighted(e + 1)

            expert(0, 0, first=True)
            expert(0, 1)
            with dve.Fori(1, EXPERTS // 2 - 1) as i:
                for u in range(2):
                    expert(i, u)
            for u in range(2):
                expert(EXPERTS // 2 - 1, u, last=u == 1)
            v.memset(touched2, 0.0).then_inc(sig("F0_over"), 1)
            add_expert(EXPERTS - 1)
            dve.wait_ge(sig("F0_added"), EXPERTS + 1)
            for t in range(NT):
                row_stats(t)
            dve.wait_ge(sig("hotw_used"), EC)
            for t in range(NT):
                ins = v.tensor_copy(wgt[:, t, :], PS[:, TR + t, 0:N])
            done(ins)
            normalise("G1", 0)
            for t in range(NT):
                v.tensor_tensor(wgt[:, t, :], PS[:, TR + t, N:2 * N], wgt[:, t, :], ALU.add).then_inc(sig("wgt"), 1)
            normalise("G1", 1)

            dve.wait_ge(sig("ld_w1g"), 32)
            for t in range(NT):
                ins = v.tensor_tensor(X[:, t, :], X[:, t, :], b1_b[:], ALU.add)
            done(ins)
            take_support("G1")
            dve.wait_ge(sig("deg"), 1)
            done(v.tensor_scalar(deg_inv[:], PS[:, 6, 0:N], 1.0, None, ALU.max))
            done(v.reciprocal(deg_inv[:], deg_inv[:]))
            for t in range(NT):
                v.tensor_tensor(mean_w[:, t, :], cnt[:, t, :], deg_inv[:], ALU.mult).then_inc(sig("mean_w"), 1)
            dve.wait_ge(sig("wgtT_ps"), 1)
            for t in range(NT):
                v.tensor_copy(wgtT[:, t, :], PS[:, 7, t * N:(t + 1) * N]).then_inc(sig("wgtT"), 1)
            v.tensor_copy(wr1T[:], PS[:, 6, N:N + DC * EXPERTS]).then_inc(sig("wr1T"), 1)
            for t in range(NT):
                dve.wait_ge(*at("G1", "out", t + 1))
                done(v.tensor_tensor(X[:, t, :], PS[:, OUT + t, :], X[:, t, :], ALU.add))
                norm_tile("F1", t)

            def small_experts(s, bias):
                top2(s, 0, bias)
                take_cwT(s, 0)
                top2(s, 1, bias)
                for t in range(NT):
                    if t:
                        take_cwT(s, t)
                    dve.wait_ge(*at(s, "spread", t + 1))
                    dve.wait_ge(*at(s, "act", t + 1))
                    hidden = wide[:, t * DC:(t + 1) * DC, 0:P]
                    v.tensor_tensor(hidden, hidden, PS[:, TR + t, :].rearrange("p (k n) -> p k n", k=DC),
                                    ALU.mult).then_inc(sig("hid"), 1)

            small_experts("F1", None)
            dve.wait_ge(sig("G2_exps"), 2)
            done(v.tensor_scalar(sc[:, 3:4], sc[:, 2:3], 0.25, None, ALU.mult))
            for t in range(NT):
                dve.wait_ge(*at("F1", "out", t + 1))
                done(v.tensor_tensor(X[:, t, :], PS[:, OUT + t, :], X[:, t, :], ALU.add))
                norm_tile("G2", t)

            dve.wait_ge(*at("G2", "xn", NT))
            for t in range(NT):
                v.tensor_tensor_reduce(out=cur[:, t, :], in0=xn[:, t, :], in1=xn[:, t, :], scale=1.0, scalar=0.0,
                                       op0=ALU.mult, op1=ALU.add, accum_out=sm[:, t:t + 1]).then_inc(sig("G2_sumsq"), 1)
            dve.wait_ge(sig("G2_rnorm"), 1)
            for t in range(NT):
                v.tensor_scalar(norm_diag[:, t, :], ident[:], rs[:, t:t + 1], None, ALU.mult).then_inc(sig("G2_norm_diag"), 1)
            dve.wait_ge(sig("G2_cross_ps"), 1)
            dve.wait_ge(sig("const_mask"), 1 + NT)
            for t in range(NT):
                ins = v.tensor_tensor(cross[:, t, :], PS[:, 5, 0:N], off_diag[:, t, :], ALU.mult)
            done(ins)
            for t in range(NT):
                dve.wait_ge(sig("G2_sim"), t + 1)
                v.scalar_tensor_tensor(sim[:, t, :], in0=PS[:, OUT + t, 0:N], scalar=rs[:, t:t + 1], in1=cross[:, t, :],
                                       op0=ALU.mult, op1=ALU.mult).then_inc(sig("G2_masked"), 1)
            for t in range(NT):
                dve.wait_ge(sig("G2_simexp"), t + 1)
                v.tensor_tensor_reduce(out=loop[:, t, :], in0=wgt[:, t, :], in1=sup[:, t, :], scale=1.0,
                                       scalar=0.0, op0=ALU.mult, op1=ALU.add, accum_out=norm[:, t:t + 1])
                ins = v.tensor_tensor(loopT[:, t, :], wgtT[:, t, :], sup[:, t, :], ALU.mult)
            done(ins)
            for t in range(NT):
                v.tensor_tensor(loop[:, t, t * P:(t + 1) * P], loop[:, t, t * P:(t + 1) * P], ident[:],
                                ALU.add).then_inc(sig("G2_loop"), 1)
                ins = v.tensor_tensor(loopT[:, t, t * P:(t + 1) * P], loopT[:, t, t * P:(t + 1) * P], ident[:], ALU.add)
                ins.then_inc(sig("G2_loopT"), 1)
            done(v.tensor_scalar(norm[:], norm[:], sc[:, 0:1], sc[:, 0:1], ALU.mult, ALU.add))
            done(v.tensor_scalar(norm[:], norm[:], sc[:, 1:2], None, ALU.add))
            done(v.reciprocal(norm[:], norm[:]))
            v.tensor_scalar(r2[:], norm[:], sc[:, 0:1], None, ALU.mult)
            done(v.tensor_scalar(rb[:], norm[:], sc[:, 1:2], None, ALU.mult))
            for t in range(NT):
                v.tensor_scalar(acc[:, t, :], xn[:, t, :], rb[:, t:t + 1], None, ALU.mult).then_inc(sig("G2_const"), 1)
            dve.wait_ge(sig("G2_loopT"), NT)
            for t in range(NT):
                v.tensor_scalar(loopTs[:, t, :], loopT[:, t, :], r2[:, t:t + 1], None,
                                ALU.mult).then_inc(sig("G2_loopTs"), 1)
            dve.wait_ge(sig("G2_const"), NT)
            for t in range(NT):
                dve.wait_ge(sig("G2_const_ps"), t + 1)
                v.scalar_tensor_tensor(spare[:, t, :], in0=PS[:, OUT + t, :], scalar=r2[:, t:t + 1],
                                       in1=acc[:, t, :], op0=ALU.mult, op1=ALU.add).then_inc(sig("G2_const2"), 1)
            for t in range(NT):
                dve.wait_ge(sig("G2_twoT_ps"), t + 1)
                v.tensor_copy(twoT[:, t, :], PS[:, 4 + t, 0:N]).then_inc(sig("G2_twoT"), 1)
            dve.wait_ge(sig("G2_const2"), NT)
            for t in range(NT):
                ins = v.tensor_tensor(X[:, t, :], spare[:, t, :], X[:, t, :], ALU.add)
            done(ins)
            for k in range(SMOOTH_STEPS // 2):
                for t in range(NT):
                    dve.wait_ge(sig("G2_two"), NT * k + t + 1)
                    if k < SMOOTH_STEPS // 2 - 1:
                        v.scalar_tensor_tensor((cur, other)[k % 2][:, t, :], in0=PS[:, (OUT, TR)[k % 2] + t, :],
                                               scalar=r2[:, t:t + 1], in1=spare[:, t, :],
                                               op0=ALU.mult, op1=ALU.add).then_inc(sig("G2_cur"), 1)
                    else:
                        done(v.scalar_tensor_tensor(X[:, t, :], in0=PS[:, (OUT, TR)[k % 2] + t, :],
                                                    scalar=r2[:, t:t + 1], in1=X[:, t, :], op0=ALU.mult, op1=ALU.add))
                        norm_tile("F2", t)

            dve.wait_ge(sig("F2_mean_ps"), 1)
            done(v.tensor_scalar(meanT[:], PS[:, SMALL, 0:DC], 1.0 / N, None, ALU.mult))
            dve.wait_ge(sig("F2_mean_ps"), 2)
            v.scalar_tensor_tensor(meanT[:], in0=PS[:, SMALL + 1, 0:DC], scalar=1.0 / N, in1=meanT[:],
                                   op0=ALU.mult, op1=ALU.add).then_inc(sig("F2_mean"), 1)
            dve.wait_ge(sig("ld_l2"), 32)
            dve.wait_ge(*at("F2", "logits", 1))
            done(v.tensor_tensor(lg[:, 0, :], PS[:, SMALL, 16:16 + GATES2], bg_b[:], ALU.add))
            done(v.max(mx[:, 0, :], lg[:, 0, :]))
            v.tensor_scalar(neg_m[:, 0:1], mx[:, 0, 0:1], -1.0, None, ALU.mult).then_inc(sig("neg_m"), 1)
            dve.wait_ge(*at("F2", "exp", 1))
            done(v.reciprocal(rs[:, 0:1], sm[:, 0:1]))
            done(v.tensor_scalar(lg[:, 1, :], ex[:, 0, :], rs[:, 0:1], None, ALU.mult))
            done(v.max(m2[:, 0, :], lg[:, 1, :]))
            v.max_index(pick[:], m2[:, 0, :], lg[:, 1, :]).then_inc(sig("F2_pick"), 1)
            dve.wait_ge(sig("ld_be_sel"), 16)
            for t in range(NT):
                ins = v.scalar_tensor_tensor(X[:, t, :], in0=be_sel[:], scalar=m2[:, 0, 0:1], in1=X[:, t, :],
                                             op0=ALU.mult, op1=ALU.add)
            done(ins)
            for t in range(NT):
                dve.wait_ge(*at("F2", "out", t + 1))
                done(v.scalar_tensor_tensor(X[:, t, :], in0=PS[:, OUT + t, :], scalar=m2[:, 0, 0:1], in1=X[:, t, :],
                                            op0=ALU.mult, op1=ALU.add))
                norm_tile("G3", t)

            dve.wait_ge(sig("ld_b3"), 16)
            for t in range(NT):
                ins = v.tensor_tensor(X[:, t, :], X[:, t, :], b3_b[:], ALU.add)
            done(ins)
            take_support("G3", SMALL)
            for t in range(NT):
                dve.wait_ge(*at("G3", "out", t + 1))
                done(v.tensor_tensor(X[:, t, :], PS[:, OUT + t, :], X[:, t, :], ALU.add))
                norm_tile("F3", t)

            dve.wait_ge(sig("ld_gate3"), 48)
            small_experts("F3", br_b)
            for t in range(NT):
                dve.wait_ge(*at("F3", "out", t + 1))
                v.tensor_tensor(X[:, t, :], PS[:, OUT + t, :], X[:, t, :], ALU.add).then_inc(sig("X_final"), 1)

        @block.scalar
        def _(act):
            a = nc.scalar

            def take_transposed(s, t):
                act.wait_ge(*at(s, "xT", t + 1))
                of = PS[:, TR:TR + 2, :].rearrange("p b (c n) -> p (b c) n", c=2)[:, :, t * P:(t + 1) * P]
                a.activation(xnT[:, :, t * P:(t + 1) * P], of, ACT.Copy).then_inc(sig("xnT"), 1)

            def router_exp(s, t, softmax_of_two=False):
                act.wait_ge(*at(s, "neg_m", t + 1))
                a.activation(ex[:, t, 0:EXPERTS], lg[:, t, 0:EXPERTS], ACT.Exp, bias=neg_m[:, t:t + 1],
                             accum_out=sm[:, t:t + 1]).then_inc(sig("exp"), 1)
                if softmax_of_two:
                    act.wait_ge(sig("F0_gap"), t + 1)
                    a.activation(gap[:, t:t + 1], gap[:, t:t + 1], ACT.Exp).then_inc(sig("F0_gap_exp"), 1)

            def take_support(s, bank=TR):
                act.wait_ge(*at(s, "supT_ps", 2))
                a.activation(supT[:, 2:4, :], PS[:, bank + 1, :], ACT.Copy).then_inc(sig("supT1"), 1)

            def activate(s, t, func, bias):
                act.wait_ge(*at(s, "hidden", t + 1))
                if bias:
                    for k in range(DC):
                        ins = a.activation(wide[:, t * DC + k, 0:P], PS[:, HID + t, k * P:(k + 1) * P], func,
                                           bias=bias_cols[:, 66 + k:67 + k])
                else:
                    ins = a.activation(wide[:, t * DC:(t + 1) * DC, 0:P],
                                       PS[:, HID + t, :].rearrange("p (k n) -> p k n", k=DC), func)
                ins.then_inc(sig("act"), 1)

            for t in range(NT):
                take_transposed("G0", t)
            def split_xn(t):
                act.wait_ge(*at("F0", "xn", t + 1))
                a.activation(xn_hi[:, t, :], xn[:, t, :], ACT.Copy).then_inc(sig("F0_parts"), 1)

            def gate(t):
                act.wait_ge(sig("F0_gate"), t + 1)
                for j in range(NT):
                    a.activation(wide[:, j, t * P:(t + 1) * P], PS[:, 6, (t * NT + j) * P:(t * NT + j + 1) * P], ACT.Relu,
                                 bias=bias_cols[:, 64 + j:65 + j]).then_inc(sig("F0_gate_act"), 1)

            for c in range(DC):
                act.wait_ge(sig("wT_ps"), c + 1)
                a.activation(w1T[:, c, :], PS[:, 4 + c, :], ACT.Copy).then_inc(sig("w1T"), 1)
            take_transposed("F0", 0)
            act.wait_ge(sig("bias_cols"), 1)
            gate(0)
            take_transposed("F0", 1)
            router_exp("F0", 0, True)
            gate(1)
            split_xn(0)
            split_xn(1)
            router_exp("F0", 1, True)
            for c in range(DC):
                act.wait_ge(sig("wT_ps"), DC + c + 1)
                a.activation(w2T[:, c, :], PS[:, c, :], ACT.Copy).then_inc(sig("w2T"), 1)
            be1_cols = bias_cols[:, 0:EXPERTS * HC].rearrange("p (g u k) -> p g u k", u=2, k=HC)
            plans = plan[:].rearrange("p a (g u) -> p a g u", u=2)
            def take_gathered(g):
                for h in range(2):
                    act.wait_ge(sig("F0_gath_ps"), g * 2 + (h + 1))
                    a.activation(gathT[:, 2 * h:2 * h + 2], PS[:, (GB, HID0)[h], :].rearrange("p (c u n) -> p c u n", c=2, u=2),
                                 ACT.Copy).then_inc(sig("F0_gath"), 1)

            def take_put(e, u):
                act.wait_ge(sig("F0_turned"), e + 1)
                a.activation(put[:, u, :], PS[:, YB, 0:N], ACT.Copy).then_inc(sig("F0_put"), 1)

            def weights_hi(g, u, k, first=False):
                if not first:
                    act.wait_ge(sig("F0_w2_used"), (g * 2 + u) * HC + (k - PIECES + 1))
                a.activation(w2_hi[:, k % PIECES, :], we2_ring[u][:, k, :], ACT.Copy).then_inc(sig("F0_w2_hi"), 1)

            def expert(g, u, first=False, last=False):
                e = g * 2 + u
                second = act.value_load(plans[0:1, 0, bass.ds(g, 1), u], min_val=0, max_val=1)
                s = act.value_load(plans[0:1, 1, bass.ds(g, 1), u], min_val=0, max_val=EXPERTS)

                def gelu(k, bias, name):
                    a.activation(hid0[:, k, :], PS[:, HID0 + k // 4, (k % 4) * P:(k % 4 + 1) * P], ACT.Gelu,
                                 bias=bias).then_inc(sig(name), 1)

                act.wait_ge(sig(f"ld_we2_slot{u}"), g * 16 + 16)
                for k in range(PIECES):
                    weights_hi(g, u, k, first)
                for k in range(HC):
                    if k % 4 == 0:
                        act.wait_ge(sig("F0_hidden"), e * 2 + (k // 4 + 1))
                    gelu(k, be1_cols[:, bass.ds(g, 1), u, k], "F0_act")
                    if k == HC - 1 and not last:
                        take_put(e + 1, (u + 1) % 2)
                    if k % 4 == 3:
                        act.wait_ge(sig("F0_act"), e * HC + (k + 1))
                        half = slice(k - 3, k + 1)
                        a.activation(hid_hi[:, half, :], hid0[:, half, :], ACT.Copy).then_inc(sig("F0_hid_hi"), 1)
                if u == 1 and not last:
                    take_gathered(g + 1)
                for k in range(PIECES, HC):
                    weights_hi(g, u, k)
                act.wait_ge(sig("F0_w2_used"), e * HC + HC)
                a.activation(y_hi[:], PS[:, YB, :], ACT.Copy).then_inc(sig("F0_y_hi"), 1)
                with act.If(second > 0):
                    a.activation(be1_now[:], be1_cols[:, bass.ds(g, 1), u, :], ACT.Copy).then_inc(sig("second_act"), 1)
                    act.wait_ge(sig("second_pe"), s * 5 + 1)
                    a.activation(put2, PS[:, HID0, 0:N], ACT.Copy)
                    a.activation(gathT2, PS[:, GB, :].rearrange("p (c n) -> p c n", c=DC), ACT.Copy).then_inc(sig("second_act"), 1)
                    act.wait_ge(sig("second_act"), s * (HC + 3) + 1)
                    for k in range(HC):
                        if k % 4 == 0:
                            act.wait_ge(sig("second_pe"), s * 5 + (k // 4 + 2))
                        gelu(k, be1_now[:, k:k + 1], "second_act")
                    act.wait_ge(sig("second_pe"), s * 5 + 4)
                    a.activation(y2, PS[:, YB, :], ACT.Copy).then_inc(sig("second_act"), 1)

            take_gathered(0)
            take_put(0, 0)
            act.wait_ge(sig("F0_plan"), 1)
            expert(0, 0, first=True)
            expert(0, 1)
            with act.Fori(1, EXPERTS // 2 - 1) as i:
                for u in range(2):
                    expert(i, u)
            for u in range(2):
                expert(EXPERTS // 2 - 1, u, last=u == 1)

            take_support("G1")
            take_transposed("F1", 0)
            router_exp("F1", 0)
            take_transposed("F1", 1)
            router_exp("F1", 1)
            act.wait_ge(sig("ld_abs"), 48)
            a.activation(sc[:, 0:2], abs_b[:, 0:2], ACT.Exp).then_inc(sig("G2_exps"), 1)
            a.activation(sc[:, 2:3], abs_b[:, 2:3], ACT.Exp, scale=-2.0).then_inc(sig("G2_exps"), 1)
            for t in range(NT):
                activate("F1", t, ACT.Gelu, False)

            for t in range(NT):
                take_transposed("G2", t)
            for t in range(NT):
                act.wait_ge(sig("G2_masked"), t + 1)
                a.activation(sup[:, t, :], sim[:, t, :], ACT.Exp, scale=sc[:, 3:4]).then_inc(sig("G2_simexp"), 1)

            def take_w3T(k):
                act.wait_ge(sig("w3T_ps"), k + 1)
                a.activation(w3T[:, k, :], PS[:, 4 + k % 4, :], ACT.Copy).then_inc(sig("w3T"), 1)

            for k in range(4):
                take_w3T(k)
            for t in range(NT):
                take_transposed("F2", t)
            act.wait_ge(*at("F2", "neg_m", 1))
            a.activation(ex[:, 0, :], lg[:, 0, :], ACT.Exp, bias=neg_m[:, 0:1],
                         accum_out=sm[:, 0:1]).then_inc(sig("exp"), 1)
            for k in range(4, 8):
                take_w3T(k)

            for t in range(NT):
                take_transposed("G3", t)
            take_support("G3", SMALL)

            take_transposed("F3", 0)
            router_exp("F3", 0)
            take_transposed("F3", 1)
            activate("F3", 0, ACT.Relu, True)
            router_exp("F3", 1)
            activate("F3", 1, ACT.Relu, True)

        @block.tensor
        def _(pe):
            mm = nc.tensor.matmul
            turn = nc.tensor.transpose

            def transposes(s, t):
                pe.wait_ge(*at(s, "xn", t + 1))
                if t:
                    pe.wait_ge(*at(s, "xnT", t))
                for c in range(DC):
                    ins = turn(PS[:, TR + c // 2, (c % 2) * N + t * P:(c % 2) * N + (t + 1) * P],
                               xn[:, t, c * P:(c + 1) * P], ident[:])
                ins.then_inc(sig("xT"), 1)

            def xnT_ready(s, t):
                pe.wait_ge(*at(s, "xnT", t + 1))

            def project(t, lhsT, w, name="out", more=False, first=True):
                for c in range(DC):
                    ins = mm(PS[:, OUT + t, :], lhsT(c, t), w[:, c, :], start=first and c == 0,
                             stop=not more and c == DC - 1)
                if not more:
                    ins.then_inc(sig(name), 1)

            def of_xnT(c, t):
                return xnT[:, c, t * P:(t + 1) * P]

            def of_supT(c, t):
                return supT[:, c, t * P:(t + 1) * P]

            def of_wide(c, t):
                return wide[:, t * DC + c, 0:P]

            def logits(t, lhsT, w, chunks):
                for c in range(chunks):
                    ins = mm(PS[:, SMALL + t, 0:EXPERTS], lhsT(c, t), w[:, c, :], start=c == 0, stop=c == chunks - 1)
                ins.then_inc(sig("logits"), 1)

            def transpose_cw(s, t, bank=SMALL):
                pe.wait_ge(*at(s, "cw", t + 1))
                turn(PS[0:EXPERTS, bank + t, 0:P], cw[:, t, :], ident[:]).then_inc(sig("cwT_ps"), 1)

            def aggregate(m, bank=TR):
                for c in range(DC):
                    for t in range(NT):
                        ins = mm(PS[:, bank + c // 2, (c % 2) * N:(c % 2 + 1) * N], xn[:, t, c * P:(c + 1) * P], m[:, t, :],
                                 start=t == 0, stop=t == NT - 1)
                    if c % 2 == 1:
                        ins.then_inc(sig("supT_ps"), 1)

            def graph_step(lhsT, z, bank, name, ready):
                for t in range(NT):
                    for k in range(NT):
                        if t == 0:
                            ready(k)
                        ins = mm(PS[:, bank + t, :], lhsT[:, k, t * P:(t + 1) * P], z[:, k, :],
                                 start=k == 0, stop=k == NT - 1)
                    ins.then_inc(sig(name), 1)

            def keep_warm(n, bank):
                for _ in range(n):
                    mm(PS[:, bank, 0:P], ones[:], ones[:], start=True, stop=True)

            pe.wait_ge(sig("const_ident"), 1)
            keep_warm(WARM['G0'], 7)
            hot_s8 = hot_s.rearrange("p (g u) n -> p g u n", u=HU)
            hot_d8 = hot_d.rearrange("p (g u) n -> p g u n", u=HU)

            def count_edges(g, first=False, last=False):
                for u in range(HU):
                    pe.wait_ge(sig("hot"), g * HU + (u + 1))
                    for t in range(NT):
                        ins = mm(PS[:, 4 + t, 0:N],
                                 hot_s8[:, bass.ds(g, 1), u, t * P:(t + 1) * P].rearrange("p a n -> p (a n)"),
                                 hot_d8[:, bass.ds(g, 1), u].rearrange("p a n -> p (a n)"),
                                 start=first and u == 0, stop=last and u == HU - 1)
                return ins

            def project_h(t):
                xnT_ready("G0", t)
                pe.wait_ge(sig("ld_w0"), 16)
                project(t, of_xnT, w0, "G0_h")

            count_edges(0, first=True)
            for t in range(NT):
                transposes("G0", t)
            project_h(0)
            with pe.Fori(1, EC // HU - 1) as i:
                count_edges(i)
            count_edges(EC // HU - 1, last=True).then_inc(sig("counted"), 1)
            pe.wait_ge(sig("cnt"), NT)
            for t in range(NT):
                for k in range(NT):
                    ins = turn(PS[:, 6 + t, k * P:(k + 1) * P], cnt[:, k, t * P:(t + 1) * P], ident[:])
            ins.then_inc(sig("cntT"), 1)
            project_h(1)
            pe.wait_ge(sig("adj"), NT)
            for k in range(2, DIFFUSION_STEPS + 1):
                of = (scaled, scaled2)[k % 2]
                for t in range(NT):
                    for j in range(NT):
                        if t == 0:
                            pe.wait_ge(sig("G0_scaled"), NT * (k - 2) + j + 1)
                        ins = mm(PS[:, (TR, HID)[k % 2] + t, 0:N], adj[:, j, t * P:(t + 1) * P], of[:, j, :],
                                 start=j == 0, stop=j == NT - 1)
                    ins.then_inc(sig("G0_power"), 1)
            pe.wait_ge(sig("G0_cur"), NT)
            pe.wait_ge(sig("G0_poly"), NT)
            pe.wait_ge(sig("ld_bias_rows"), 48)
            turn(PS[:, 4, 0:70], bias_rows[:], ident[0:70, 0:70]).then_inc(sig("bias_ps"), 1)
            graph_step(poly, cur, OUT, "G0_step", lambda j: None)

            pe.wait_ge(sig("ld_w1_raw"), 16)
            pe.wait_ge(sig("bias_cols"), 1)
            for c in range(DC):
                for k in range(DC):
                    ins = turn(PS[:, 4 + c, k * P:(k + 1) * P], w1_raw[:, k, c * P:(c + 1) * P], ident[:])
                ins.then_inc(sig("wT_ps"), 1)
            pe.wait_ge(sig("ld_gate0"), 48)

            def gate(t):
                xnT_ready("F0", t)
                for j in range(NT):
                    for c in range(DC):
                        ins = mm(PS[:, 6, (t * NT + j) * P:(t * NT + j + 1) * P], gw1[:, c, j * P:(j + 1) * P],
                                 of_xnT(c, t), start=c == 0, stop=c == DC - 1)
                ins.then_inc(sig("F0_gate"), 1)

            def gate_logits(t):
                pe.wait_ge(sig("F0_gate_act"), NT * (t + 1))
                logits(t, lambda c, t: wide[:, c, t * P:(t + 1) * P], gw2, NT)

            transposes("F0", 0)
            pe.wait_ge(sig("w1T"), DC)
            gate(0)
            transposes("F0", 1)
            gate_logits(0)
            gate(1)
            gate_logits(1)
            pe.wait_ge(sig("ld_w2_raw"), 16 * DC)
            for c in range(DC):
                for k in range(DC):
                    ins = turn(PS[:, c, k * P:(k + 1) * P], w2_raw[:, k, c * P:(c + 1) * P], ident[:])
                ins.then_inc(sig("wT_ps"), 1)
            pe.wait_ge(sig("const_upto"), 3)
            pe.wait_ge(sig("F0_chosen"), 1)
            mm(PS[:, GB, 0:EXPERTS], upto[:], chosen[:, 0, :], start=True, stop=True)
            pe.wait_ge(sig("F0_chosen"), 2)
            for k in range(2):
                cols = PS[:, GB, (k + 1) * EXPERTS:(k + 2) * EXPERTS]
                mm(cols, ones_b[:], chosen[:, 0, :], start=True, stop=False)
                ins = mm(cols, (upto, ones_b)[k][:], chosen[:, 1, :], start=False, stop=True)
            ins.then_inc(sig("F0_place"), 1)
            keep_warm(WARM['F0a'], 6)
            plans = plan[:].rearrange("p a (g u) -> p a g u", u=2)

            def gather_pair(g):
                pe.wait_ge(sig("F0_pickT"), g + 1)
                for c in range(DC):
                    for k, (part, t) in enumerate((part, t) for part in (xn_hi, xn_lo) for t in range(NT)):
                        ins = mm(PS[:, (GB, HID0)[c // 2], (c % 2) * 2 * P:(c % 2 + 1) * 2 * P],
                                 part[:, t, c * P:(c + 1) * P], pickT[:, t, :, :], start=k == 0, stop=k == 2 * NT - 1)
                    if c % 2 == 1:
                        ins.then_inc(sig("F0_gath_ps"), 1)

            def turn_picks(bank, u):
                for t in range(NT):
                    ins = turn(PS[:, bank, t * P:(t + 1) * P], pickT[:, t, u, :].bitcast(F32), ident[:])
                return ins

            def hidden_units(u, tokens, name):
                for k in range(HC):
                    for c in range(DC):
                        ins = mm(PS[:, HID0 + k // 4, (k % 4) * P:(k % 4 + 1) * P],
                                 we1_ring[u][:, c, k * P:(k + 1) * P], tokens[:, c, :], start=c == 0, stop=c == DC - 1)
                    if k % 4 == 3:
                        ins.then_inc(sig(name), 1)

            def scatter(e, u):
                pe.wait_ge(sig("F0_put"), e + 1)
                pe.wait_ge(sig("F0_y_hi"), e + 1)
                pe.wait_ge(sig("F0_y_lo"), e + 1)
                pe.wait_ge(sig("F0_added"), e + 1)
                for t in range(NT):
                    for part, of in enumerate((y_hi, y_lo)):
                        ins = mm(PS[:, OUT + t, :], put[:, u, t * P:(t + 1) * P], of[:], start=part == 0, stop=part == 1)
                ins.then_inc(sig("F0_scattered"), 1)

            def expert(g, u, first=False, last=False):
                e = g * 2 + u

                def edges(j0, j1):
                    for j in range(j0, j1):
                        pe.wait_ge(sig("hotw"), e * EU + (j + 1))
                        for t in range(NT):
                            ins = mm(PS[:, TR + t, :], hot_sr[:, j, t * P:(t + 1) * P], hot_dw[:, j, :],
                                     start=first and j == 0, stop=last and j == EU - 1)
                        ins.then_inc(sig("hotw_used"), 1)

                pe.wait_ge(sig(f"ld_we1_slot{u}"), g * 16 + 16)
                if u == 0:
                    pe.wait_ge(sig("F0_gath"), g * 2 + 2)
                if first:
                    pe.wait_ge(sig("w2T"), DC)
                    pe.wait_ge(sig("F0_put"), 1)
                hidden_units(u, gathT[:, :, u, :], "F0_hidden")
                if first:
                    pe.wait_ge(sig("F0_plan"), 1)
                second = pe.value_load(plans[0:1, 0, bass.ds(g, 1), u], min_val=0, max_val=1)
                s = pe.value_load(plans[0:1, 1, bass.ds(g, 1), u], min_val=0, max_val=EXPERTS)
                if not first:
                    pe.wait_ge(sig("hotw"), e * EU + 1)
                    scatter(e - 1, (u + 1) % 2)
                else:
                    for t in range(NT):
                        transpose_cw("F0", t, OUT)
                front = EU // 2 if u == 0 or last else 0
                if u == 0:
                    turn_picks(YB, 1).then_inc(sig("F0_turned"), 1)
                elif not last:
                    pe.wait_ge(sig("F0_act"), e * HC + HC // 2)
                    pe.wait_ge(sig("F0_pickT"), g + 2)
                    turn_picks(YB, 0).then_inc(sig("F0_turned"), 1)
                    gather_pair(g + 1)
                edges(0, front)
                if first:
                    pe.wait_ge(sig("ld_be2"), 16)
                    pe.wait_ge(*at("F0", "cwT", NT))
                    for t in range(NT):
                        mm(PS[:, OUT + t, :], cwT[:, t * P:(t + 1) * P], be2_sb[:], start=True,
                           stop=True).then_inc(sig("out"), 1)
                if not last:
                    pe.wait_ge(sig("F0_put"), e + 2)
                for k in range(HC):
                    if k % 4 == 0:
                        pe.wait_ge(sig("F0_hid_hi"), e * 2 + (k // 4 + 1))
                    pe.wait_ge(sig("F0_w2_hi"), e * HC + (k + 1))
                    mm(PS[:, YB, :], hid_hi[:, k, :], w2_hi[:, k % PIECES, :], start=k == 0, stop=False)
                    pe.wait_ge(sig("F0_w2_lo"), e * HC + (k + 1))
                    mm(PS[:, YB, :], hid_hi[:, k, :], w2_lo[:, k % PIECES, :], start=False, stop=False)
                    if k % 4 == 0:
                        pe.wait_ge(sig("F0_hid_lo"), e * 2 + (k // 4 + 1))
                    mm(PS[:, YB, :], hid_lo[:, k, :], w2_hi[:, k % PIECES, :], start=False,
                       stop=k == HC - 1).then_inc(sig("F0_w2_used"), 1)
                with pe.If(second > 0):
                    pe.wait_ge(sig("F0_gath"), g * 2 + (4 if u == 1 and not last else 2))
                    keep_warm(WARM['F0c'], GB)
                    pe.wait_ge(sig("second_dve"), s * 2 + 1)
                    for t in range(NT):
                        turn(PS[:, HID0, t * P:(t + 1) * P], pickT2[:, t, :], ident[:])
                    for c in range(DC):
                        for t in range(NT):
                            ins = mm(PS[:, GB, c * P:(c + 1) * P], xn[:, t, c * P:(c + 1) * P], pickT2[:, t, :],
                                     start=t == 0, stop=t == NT - 1)
                    ins.then_inc(sig("second_pe"), 1)
                    pe.wait_ge(sig("second_act"), s * (HC + 3) + 2)
                    hidden_units(u, gathT2, "second_pe")
                    pe.wait_ge(sig("F0_y_hi"), e + 1)
                    pe.wait_ge(sig("F0_y_lo"), e + 1)
                    for k in range(HC):
                        pe.wait_ge(sig("second_act"), s * (HC + 3) + (k + 3))
                        ins = mm(PS[:, YB, :], hid0[:, k, :], we2_ring[u][:, k, :], start=k == 0, stop=k == HC - 1)
                    ins.then_inc(sig("second_pe"), 1)
                    pe.wait_ge(sig("second_act"), s * (HC + 3) + (HC + 3))
                    pe.wait_ge(sig("F0_added"), e + 1)
                    for t in range(NT):
                        ins = mm(PS[:, OUT + t, :], put2[:, t * P:(t + 1) * P], y2, start=True, stop=True)
                    ins.then_inc(sig("second_pe"), 1)
                edges(front, EU)

            keep_warm(WARM['F0b'], 6)
            pe.wait_ge(sig("F0_parts"), 2 * NT)
            gather_pair(0)
            turn_picks(YB, 0).then_inc(sig("F0_turned"), 1)
            expert(0, 0, first=True)
            expert(0, 1)
            with pe.Fori(1, EXPERTS // 2 - 1) as i:
                for u in range(2):
                    expert(i, u)
            for u in range(2):
                expert(EXPERTS // 2 - 1, u, last=u == 1)

            pe.wait_ge(sig("F0_over"), 1)
            scatter(EXPERTS - 1, 1)
            pe.wait_ge(sig("ld_wr1"), 16)
            for c in range(DC):
                turn(PS[:, 6, N + c * EXPERTS:N + (c + 1) * EXPERTS], wr_rows[:, c * P:(c + 1) * P],
                     ident[0:EXPERTS, 0:EXPERTS])
            for t in range(NT):
                ins = mm(PS[:, 6, 0:N], ones[:], cnt[:, t, :], start=t == 0, stop=t == NT - 1)
            ins.then_inc(sig("deg"), 1)
            keep_warm(WARM['G1a'], 4)
            pe.wait_ge(sig("wgt"), NT)
            pe.wait_ge(*at("G1", "xn", 1))
            pe.wait_ge(*at("G1", "xn", NT))
            aggregate(wgt)
            for t in range(NT):
                for k in range(NT):
                    ins = turn(PS[:, 7, t * N + k * P:t * N + (k + 1) * P], wgt[:, k, t * P:(t + 1) * P], ident[:])
            ins.then_inc(sig("wgtT_ps"), 1)
            pe.wait_ge(*at("G1", "supT0", 1))
            pe.wait_ge(*at("G1", "supT1", 1))
            pe.wait_ge(sig("ld_w1g"), 32)
            for t in range(NT):
                project(t, of_supT, w1g)

            def small_experts(s, wr, w1, w2, b2):
                def hidden(t, k0=0, k1=DC):
                    for k in range(k0, k1):
                        for c in range(DC):
                            ins = mm(PS[:, HID + t, k * P:(k + 1) * P], w1[:, c, k * P:(k + 1) * P], of_xnT(c, t),
                                     start=c == 0, stop=c == DC - 1)
                    if k1 == DC:
                        ins.then_inc(sig("hidden"), 1)

                def spread_weights(t):
                    pe.wait_ge(*at(s, "cwT", t + 1))
                    for k in range(DC):
                        ins = mm(PS[:, TR + t, k * P:(k + 1) * P], spread[:, k * P:(k + 1) * P],
                                 cwT[:, t * P:(t + 1) * P], start=True, stop=True)
                    ins.then_inc(sig("spread"), 1)

                transposes(s, 0)
                xnT_ready(s, 0)
                logits(0, of_xnT, wr, DC)
                hidden(0, 0, DC // 2)
                transposes(s, 1)
                hidden(0, DC // 2)
                xnT_ready(s, 1)
                logits(1, of_xnT, wr, DC)
                transpose_cw(s, 0)
                hidden(1)
                spread_weights(0)
                transpose_cw(s, 1)
                keep_warm(WARM['cwT'], OUT)
                spread_weights(1)
                for t in range(NT):
                    if b2 is not None:
                        mm(PS[:, OUT + t, :], cwT[:, t * P:(t + 1) * P], b2[:], start=True, stop=False)
                    pe.wait_ge(*at(s, "hid", t + 1))
                    project(t, of_wide, w2, first=b2 is None)

            pe.wait_ge(sig("wr1T"), 1)
            pe.wait_ge(sig("const_spread"), 3)
            small_experts("F1", wr1T, w1T, w2T, None)

            transposes("G2", 0)
            keep_warm(WARM['G2a'], SMALL)
            transposes("G2", 1)
            for t in range(NT):
                xnT_ready("G2", t)
            for t in range(NT):
                for c in range(DC):
                    ins = mm(PS[:, OUT + t, 0:N], of_xnT(c, t), xnT[:, c, :], start=c == 0, stop=c == DC - 1)
                ins.then_inc(sig("G2_sim"), 1)
                if t == 0:
                    pe.wait_ge(sig("G2_norm_diag"), NT)
                    for k in range(NT):
                        ins = mm(PS[:, 5, k * P:(k + 1) * P], ones[:], norm_diag[:, k, :], start=True, stop=True)
                    ins.then_inc(sig("G2_cross_ps"), 1)

            def transpose_w3(k):
                for c in range(DC):
                    ins = turn(PS[:, 4 + k % 4, c * P:(c + 1) * P], w3_raw[:, c, k * P:(k + 1) * P], ident[:])
                ins.then_inc(sig("w3T_ps"), 1)

            pe.wait_ge(sig("ld_w3_raw"), 16)
            pe.wait_ge(sig("G2_masked"), 1)
            for k in range(4):
                transpose_w3(k)
            keep_warm(WARM['G2b'], TR)
            pe.wait_ge(sig("G2_loopT"), NT)
            graph_step(loopT, acc, OUT, "G2_const_ps", lambda k: pe.wait_ge(sig("G2_const"), k + 1))
            pe.wait_ge(sig("G2_loop"), NT)
            pe.wait_ge(sig("G2_loopTs"), NT)
            pe.wait_ge(sig("w3T"), 4)
            for t in range(NT):
                for k in range(NT):
                    ins = mm(PS[:, 4 + t, 0:N], loop[:, k, t * P:(t + 1) * P], loopTs[:, k, :], start=k == 0, stop=k == NT - 1)
                ins.then_inc(sig("G2_twoT_ps"), 1)
            pe.wait_ge(sig("G2_const2"), NT)
            pe.wait_ge(sig("G2_twoT"), NT)
            for k in range(SMOOTH_STEPS // 2):
                graph_step(twoT, (other, cur)[k % 2] if k else xn, (OUT, TR)[k % 2], "G2_two",
                           lambda j: pe.wait_ge(sig("G2_cur"), NT * (k - 1) + j + 1) if k else None)

            keep_warm(WARM['F2a'], 7)
            for t in range(NT):
                pe.wait_ge(*at("F2", "xn", t + 1))
                for c in range(DC):
                    ins = mm(PS[:, SMALL + t, c:c + 1], xn[:, t, c * P:(c + 1) * P], ones[:, 0:1], start=True, stop=True)
                ins.then_inc(sig("F2_mean_ps"), 1)
                transposes("F2", t)
                if t == 0:
                    keep_warm(WARM['F2b'], 7)
            pe.wait_ge(sig("F2_mean"), 1)
            pe.wait_ge(sig("ld_l2"), 32)
            for c in range(DC):
                ins = mm(PS[:, SMALL, 16:16 + GATES2], meanT[:, c:c + 1].broadcast_to([P, P]), wg2[:, c, :],
                         start=c == 0, stop=c == DC - 1)
            ins.then_inc(sig("logits"), 1)
            for k in range(4, 8):
                if k == 4:
                    pe.wait_ge(*at("F2", "neg_m", 1))
                transpose_w3(k)
            for t in range(NT):
                xnT_ready("F2", t)
            keep_warm(WARM['F2d'], TR)
            for c, t in [(0, t) for t in range(NT)] + [(c, t) for t in range(NT) for c in range(1, DC)]:
                if t == 0:
                    pe.wait_ge(sig(f"ld_we_sel{c}"), 16)
                ins = mm(PS[:, OUT + t, :], of_xnT(c, t), we_sel[:, c, :], start=c == 0, stop=c == DC - 1)
                if c == DC - 1:
                    ins.then_inc(sig("out"), 1)

            pe.wait_ge(sig("w3T"), 8)
            keep_warm(WARM['G3'], 4)
            transposes("G3", 0)
            xnT_ready("G3", 0)
            project(0, of_xnT, w3T[:, 0:4, :], more=True)
            transposes("G3", 1)
            pe.wait_ge(sig("mean_w"), NT)
            aggregate(mean_w, SMALL)
            xnT_ready("G3", 1)
            project(1, of_xnT, w3T[:, 0:4, :], more=True)
            pe.wait_ge(*at("G3", "supT0", 1))
            pe.wait_ge(*at("G3", "supT1", 1))
            for t in range(NT):
                project(t, of_supT, w3T[:, 4:8, :], first=False)

            pe.wait_ge(sig("ld_gate3"), 48)
            pe.wait_ge(sig("ld_w31"), 16 * DC)
            pe.wait_ge(sig("ld_w32"), 16)
            small_experts("F3", wr3, w31, w32, b2_sb)


_INS = ['x', 'src', 'dst', 'edge_weight', 'L0_gnn_W', 'L0_gnn_b', 'L0_gnn_diffusion_weights', 'L0_ffn_gw1',
        'L0_ffn_gb1', 'L0_ffn_gw2', 'L0_ffn_gb2', 'L0_ffn_we1', 'L0_ffn_be1', 'L0_ffn_we2', 'L0_ffn_be2',
        'L1_gnn_weight', 'L1_gnn_bias', 'L1_ffn_Wr', 'L1_ffn_W1', 'L1_ffn_W2', 'L2_gnn_alpha', 'L2_gnn_beta',
        'L2_gnn_sigma', 'L2_ffn_Wg', 'L2_ffn_bg', 'L2_ffn_We', 'L2_ffn_be', 'L3_gnn_W', 'L3_gnn_b', 'L3_ffn_Wr',
        'L3_ffn_br', 'L3_ffn_W1', 'L3_ffn_b1', 'L3_ffn_W2', 'L3_ffn_b2']


def kernel(**inputs):
    import numpy as _np
    import concourse.bacc as _bacc
    from concourse import mybir as _mybir
    from concourse.bass_utils import run_bass_kernel_spmd as _run

    nc = _bacc.Bacc("TRN2", target_bir_lowering=False, num_devices=1)
    arrays, args = {}, []
    for name in _INS:
        a = _np.ascontiguousarray(inputs[name])
        arrays[f"in_{name}_dram"] = a
        args.append(nc.dram_tensor(f"in_{name}_dram", a.shape, _mybir.dt.from_np(a.dtype), kind="ExternalInput").ap())
    args.append(nc.dram_tensor("out_dram", (N, D), F32, kind="ExternalOutput").ap())
    build(nc, *args)
    r = _run(nc, [arrays], core_ids=[0])
    return r.results[0]["out_dram"]
```
